# Optimizing a Trainium2 kernel written in Bass

```python
import numpy as np
import jax
import jax.numpy as jnp

def _softmax(x, axis=-1):
    return jax.nn.softmax(x, axis=axis)

def _gelu(x):
    return jax.nn.gelu(x, approximate=True)

def _silu(x):
    return jax.nn.silu(x)

def _sigmoid(x):
    return jax.nn.sigmoid(x)

def _layernorm(x, axis=-1, eps=1e-05):
    m = jnp.mean(x, axis=axis, keepdims=True)
    v = jnp.var(x, axis=axis, keepdims=True)
    return (x - m) / jnp.sqrt(v + eps)

def _scatter_add(tgt, idx, src, axis=0):
    return tgt.at[idx].add(src)

def _segment_sum(src, seg, n):
    return jax.ops.segment_sum(src, seg, n)
kernel_name = 'mk_gnn_ffn_d1_gnn_r8_355786'

def setup_inputs(seed: int=0):
    np.random.seed(seed)
    _w = jnp.asarray

    def _rec_inputs():
        import jax
        import jax.numpy as jnp
        _gk = jax.random.key(seed)
        x = -6.415e-05 + 1 * jax.random.normal(jax.random.fold_in(_gk, 1), (1250, 1024), jnp.float32)
        _s = jax.random.randint(jax.random.fold_in(_gk, 2), (10000,), 0, 1250, jnp.int32)
        _d = jax.random.randint(jax.random.fold_in(_gk, 3), (10000,), 0, 1250, jnp.int32)
        _loop = jnp.arange(1250, dtype=jnp.int32)
        src = jnp.concatenate([_s, _d, _loop])
        dst = jnp.concatenate([_d, _s, _loop])
        _o = jnp.argsort(dst, stable=True)
        src = src[_o]
        dst = dst[_o]
        edge_type_8 = jax.random.randint(jax.random.fold_in(_gk, 12), (21250,), 0, 8, jnp.int32)
        return (x, src, dst, edge_type_8)
    x, src, dst, edge_type_8 = _rec_inputs()

    def _L0_gnn_setup():
        import jax, jax.numpy as jnp
        import numpy as np
        N, D, R, E = (1250, 1024, 8, 10000)

        def _rgcn(x, edge_index, edge_type, weight, root, bias):
            src, dst = (edge_index[0], edge_index[1])
            msgs = x[src]
            out = x @ root + bias
            n = x.shape[0]
            for r in range(weight.shape[0]):
                mask = (edge_type == r).astype(x.dtype)
                sums = jax.ops.segment_sum(msgs * mask[:, None], dst, num_segments=n)
                cnt = jax.ops.segment_sum(mask, dst, num_segments=n)
                mean = sums / jnp.maximum(cnt, 1.0)[:, None]
                out = out + mean @ weight[r]
            return out
        key = jax.random.key(seed)
        ks = jax.random.split(key, 8)
        s = 1.0 / np.sqrt(D)
        x = jax.random.normal(ks[0], (N, D), dtype=jnp.float32)
        edge_index = jax.random.randint(ks[1], (2, E), 0, N, dtype=jnp.int64)
        edge_type = jax.random.randint(ks[2], (E,), 0, R, dtype=jnp.int64)
        weight = jax.random.normal(ks[3], (R, D, D), dtype=jnp.float32) * s
        root = jax.random.normal(ks[4], (D, D), dtype=jnp.float32) * s
        bias = jnp.zeros((D,), dtype=jnp.float32)
        w_gate = jax.random.normal(ks[5], (2 * D, D), dtype=jnp.float32) * (1.0 / np.sqrt(2 * D))
        b_gate = jnp.zeros((D,), dtype=jnp.float32)
        return {'x': x, 'edge_index': edge_index, 'edge_type': edge_type, 'weight': weight, 'root': root, 'bias': bias, 'w_gate': w_gate, 'b_gate': b_gate}
    _L0_gnn_all = _L0_gnn_setup()
    _L0_gnn_in = {k: v for k, v in _L0_gnn_all.items() if k in ('weight', 'root', 'bias', 'w_gate', 'b_gate')}
    del _L0_gnn_all

    def _L0_ffn_setup():
        import jax, jax.numpy as jnp
        import numpy as np
        E, K, D, H = (8, 2, 1024, 256)
        B, S = (1, 1024)

        def _grouped_swiglu(x_sorted, counts, w1, w2, w3):
            if hasattr(jax.lax, 'ragged_dot'):
                gs = counts.astype(jnp.int32)
                h = jax.nn.silu(jax.lax.ragged_dot(x_sorted, w1, gs)) * jax.lax.ragged_dot(x_sorted, w3, gs)
                return jax.lax.ragged_dot(h, w2, gs)
            pos = jnp.arange(x_sorted.shape[0])
            eid = jnp.searchsorted(jnp.cumsum(counts), pos, side='right')
            out = jnp.zeros((x_sorted.shape[0], w2.shape[-1]), x_sorted.dtype)
            for e in range(w1.shape[0]):
                xm = jnp.where((eid == e)[:, None], x_sorted, 0.0)
                he = jax.nn.silu(xm @ w1[e]) * (xm @ w3[e])
                out = out + he @ w2[e]
            return out
        key = jax.random.key(seed)
        k0, k1, k2, k3, k4 = jax.random.split(key, 5)
        sD = 1.0 / np.sqrt(D)
        sH = 1.0 / np.sqrt(H)
        return {'hidden_states': jax.random.normal(k0, (B, S, D), jnp.float32), 'gate_w': jax.random.normal(k1, (E, D), jnp.float32) * sD, 'w1': jax.random.normal(k2, (E, D, H), jnp.float32) * sD, 'w2': jax.random.normal(k3, (E, H, D), jnp.float32) * sH, 'w3': jax.random.normal(k4, (E, D, H), jnp.float32) * sD}
    _L0_ffn_all = _L0_ffn_setup()
    _L0_ffn_in = {k: v for k, v in _L0_ffn_all.items() if k in ('gate_w', 'w1', 'w2', 'w3')}
    del _L0_ffn_all
    return {'x': x, 'src': src, 'dst': dst, 'edge_type_8': edge_type_8, 'L0_gnn_weight': _L0_gnn_in['weight'], 'L0_gnn_root': _L0_gnn_in['root'], 'L0_gnn_bias': _L0_gnn_in['bias'], 'L0_gnn_w_gate': _L0_gnn_in['w_gate'], 'L0_gnn_b_gate': _L0_gnn_in['b_gate'], 'L0_ffn_gate_w': _L0_ffn_in['gate_w'], 'L0_ffn_w1': _L0_ffn_in['w1'], 'L0_ffn_w2': _L0_ffn_in['w2'], 'L0_ffn_w3': _L0_ffn_in['w3']}

def reference(x, src, dst, edge_type_8, L0_gnn_weight, L0_gnn_root, L0_gnn_bias, L0_gnn_w_gate, L0_gnn_b_gate, L0_ffn_gate_w, L0_ffn_w1, L0_ffn_w2, L0_ffn_w3):
    import jax
    import jax.numpy as jnp

    def _L0_gnn_ref(x, edge_index, edge_type, weight, root, bias, w_gate, b_gate):
        import jax, jax.numpy as jnp
        import numpy as np
        N, D, R, E = (1250, 1024, 8, 10000)

        def _rgcn(x, edge_index, edge_type, weight, root, bias):
            src, dst = (edge_index[0], edge_index[1])
            msgs = x[src]
            out = x @ root + bias
            n = x.shape[0]
            for r in range(weight.shape[0]):
                mask = (edge_type == r).astype(x.dtype)
                sums = jax.ops.segment_sum(msgs * mask[:, None], dst, num_segments=n)
                cnt = jax.ops.segment_sum(mask, dst, num_segments=n)
                mean = sums / jnp.maximum(cnt, 1.0)[:, None]
                out = out + mean @ weight[r]
            return out
        u = _rgcn(x, edge_index, edge_type, weight, root, bias)
        z = jnp.concatenate([u, x], axis=1) @ w_gate + b_gate
        h = jnp.tanh(u) * z + x * (1.0 - z)
        return h

    def _L0_ffn_ref(hidden_states, gate_w, w1, w2, w3):
        import jax, jax.numpy as jnp
        import numpy as np
        E, K, D, H = (8, 2, 1024, 256)
        B, S = (1, 1024)

        def _grouped_swiglu(x_sorted, counts, w1, w2, w3):
            if hasattr(jax.lax, 'ragged_dot'):
                gs = counts.astype(jnp.int32)
                h = jax.nn.silu(jax.lax.ragged_dot(x_sorted, w1, gs)) * jax.lax.ragged_dot(x_sorted, w3, gs)
                return jax.lax.ragged_dot(h, w2, gs)
            pos = jnp.arange(x_sorted.shape[0])
            eid = jnp.searchsorted(jnp.cumsum(counts), pos, side='right')
            out = jnp.zeros((x_sorted.shape[0], w2.shape[-1]), x_sorted.dtype)
            for e in range(w1.shape[0]):
                xm = jnp.where((eid == e)[:, None], x_sorted, 0.0)
                he = jax.nn.silu(xm @ w1[e]) * (xm @ w3[e])
                out = out + he @ w2[e]
            return out
        x = hidden_states.reshape(-1, D)
        N = x.shape[0]
        scores = jax.nn.softmax(x @ gate_w.T, axis=-1)
        top_scores, sel = jax.lax.top_k(scores, K)
        sel_flat = sel.T.reshape(-1)
        scores_flat = top_scores.T.reshape(-1)
        order = jnp.argsort(sel_flat, stable=True)
        tok_sorted = order % N
        scores_sorted = scores_flat[order]
        counts = jnp.bincount(sel_flat, length=E)
        x_sorted = x[tok_sorted]
        y = _grouped_swiglu(x_sorted, counts, w1, w2, w3)
        weighted = y * scores_sorted[:, None]
        out = jnp.zeros((N, D), x.dtype).at[tok_sorted].add(weighted)
        return out.reshape(hidden_states.shape)
    edge_index = jnp.stack([src, dst])
    x = x + _L0_gnn_ref(_layernorm(x, axis=-1), edge_index, edge_type_8, L0_gnn_weight, L0_gnn_root, L0_gnn_bias, L0_gnn_w_gate, L0_gnn_b_gate)
    x = x + _L0_ffn_ref(_layernorm(x, axis=-1)[None], L0_ffn_gate_w, L0_ffn_w1, L0_ffn_w2, L0_ffn_w3)[0]
    return x

_drawn_inputs = setup_inputs


def setup_inputs(seed=0):
    import zlib

    import numpy as np

    out = dict(_drawn_inputs(seed))
    spreads = {'L0_gnn_bias': (0.0, 0.1), 'L0_gnn_b_gate': (0.0, 0.1)}
    factors = {}
    for name, (base, spread) in spreads.items():
        noise = np.random.default_rng([zlib.crc32(name.encode()), seed]).standard_normal(out[name].shape)
        drawn = base * np.exp(spread * noise) if base else spread * noise
        out[name] = jnp.asarray(drawn.astype(out[name].dtype))
    for name, factor in factors.items():
        out[name] = (out[name] * factor).astype(out[name].dtype)
    return out
```

```python
import numpy as np
import concourse.bass as bass
from concourse import mybir
from contextlib import ExitStack

F32 = mybir.dt.float32
F32R = mybir.dt.float32r
BF16 = mybir.dt.bfloat16
I32 = mybir.dt.int32
U32 = mybir.dt.uint32
ALU = mybir.AluOpType
ACT = mybir.ActivationFunctionType
AX = mybir.AxisListType

P = 128
BANK = 512
EPS = 1e-5
GROUP = 2


def shapes(x, src, weight, w1, gate_w):
    s = {}
    s["N"], s["D"] = x.shape
    s["E"] = src.shape[0]
    s["R"] = weight.shape[0]
    s["X"], _, s["H"] = w1.shape
    s["NT"] = -(-s["N"] // P)
    s["NP"] = s["NT"] * P
    s["KC"] = s["D"] // P
    s["HC"] = s["H"] // P
    s["EFULL"] = s["E"] // P
    s["EREST"] = s["E"] - s["EFULL"] * P
    s["ECOLS"] = 168
    pad = GROUP * P
    pairs = (s["E"] + s["NT"] * (pad - 1)) // pad
    s["PAIRS"] = 4 * (-(-pairs // 8) * 2)
    s["ET"] = s["PAIRS"] * GROUP
    s["MT"] = (2 * s["N"] + s["X"] * (P - 1)) // P
    s["MTE"] = s["MT"] + s["MT"] % 2
    return s


def build_program(nc, x, src, dst, edge_type, weight, root, bias, w_gate, b_gate,
                  gate_w, w1, w2, w3, out):
    s = shapes(x, src, weight, w1, gate_w)
    N, D, R, X, H, NT, NP, KC, HC = (s[k] for k in ("N", "D", "R", "X", "H", "NT", "NP", "KC", "HC"))
    E, EFULL, EREST, ECOLS, PAIRS, ET, MT, MTE = (
        s[k] for k in ("E", "EFULL", "EREST", "ECOLS", "PAIRS", "ET", "MT", "MTE"))
    LASTP = N - (NT - 1) * P
    HALF = D // 2
    assert ECOLS >= EFULL + (EREST > 0) and HALF == BANK and D == 1024 and R == 8 and X == 8
    KEYS = NP * R
    KHI = KEYS // 256

    with ExitStack() as ctx:
        psum = [ctx.enter_context(nc.psum_tensor(f"bank{i}", [P, BANK], F32)) for i in range(8)]

        def sem(name):
            return ctx.enter_context(nc.semaphore(name))

        size = {F32: 4, F32R: 4, BF16: 2, I32: 4, U32: 4}

        class Zone:
            def __init__(self, start, length):
                self.at, self.end, self.start = start, start + length, start

            def put(self, name, shape, dt):
                n = size[dt] * int(np.prod(shape[1:]))
                n = -(-n // 32) * 32
                assert self.at + n <= self.end, (name, self.at + n - self.end)
                t = nc.alloc_sbuf_tensor_at(name, shape, dt, offset=self.at)
                self.at += n
                return t

        KB = 1024
        base = -(-nc.sbuf_base // 32) * 32
        LIMIT = nc.sbuf_base + nc.sbuf_bytes_remaining
        keep = Zone(base, 13 * KB // 2)
        OFF_T = base + 13 * KB // 2
        OFF_STAGE = OFF_T + 80 * KB
        OFF_YOUT = OFF_STAGE + 8 * KB
        OFF_W0 = OFF_YOUT + 8 * KB
        OFF_W1 = OFF_W0 + 32 * KB
        OFF_END = OFF_W1 + 32 * KB

        ident = keep.put("ident", [P, P], F32)
        iota = keep.put("iota", [P, 257], F32)
        lanes = keep.put("lanes", [P, 1], F32)
        mean = keep.put("mean", [P, NT], F32)
        rstd = keep.put("rstd", [P, NT], F32)
        edge_row = keep.put("edge_row", [P, ET], I32)
        edge_dst = keep.put("edge_dst", [P, ET], F32)
        edge_key = keep.put("edge_key", [P, ET], I32)
        edge_w = keep.put("edge_w", [P, ET], F32)
        tile_block = keep.put("tile_block", [P, ET], I32)
        tri = keep.put("tri", [P, P], BF16)
        ones = keep.put("ones", [P, P], BF16)

        def dram(name, shape, dt=F32):
            return nc.dram_tensor(name, shape, dt, kind="Internal").ap()

        Y = dram("Y", (R * NP, D))
        YX = dram("YX", (2, NP, D))
        INV = dram("INV", (KEYS, 1))
        XN2 = dram("XN2", (NP, D))
        X1 = dram("X1", (NP, D))
        YS = dram("YS", (MT * P, D))

        def rows(j):
            return LASTP if j == NT - 1 else P

        def chain(eng, name):
            done, count = sem(name), [0]

            def step(ins):
                count[0] += 1
                ins.then_inc(done, 1)
                eng.wait_ge(done, count[0])
            return step

        xhi = nc.alloc_sbuf_tensor_at("xhi", [P, KC, NP], F32R, offset=OFF_T)
        xlo = nc.alloc_sbuf_tensor_at("xlo", [P, KC, NP], F32R, offset=OFF_T + 4 * KC * NP)
        z1 = Zone(OFF_W0, 64 * KB)
        x_all = z1.put("x_all", [P, NT, D], F32)
        stat = z1.put("stat", [P, NT, 2, 6], F32)
        aggr = z1.put("aggr", [P, NT, 2], F32)
        tmp10 = z1.put("tmp10", [P, 4, NT], F32)
        z2 = Zone(OFF_END, LIMIT - OFF_END)
        place_lo = z2.put("place_lo", [P, ECOLS], F32)
        place_hi = z2.put("place_hi", [P, ECOLS], F32)
        val_src = z2.put("val_src", [P, ECOLS], F32)
        val_dst = z2.put("val_dst", [P, ECOLS], F32)
        key_hi = z2.put("key_hi", [P, ECOLS], F32)
        key_lo = z2.put("key_lo", [P, ECOLS], F32)
        blk_base = z2.put("blk_base", [P, NT], F32)
        z2t = Zone(z2.at, LIMIT - z2.at)
        onehot = z2t.put("onehot", [P, NT, ECOLS], BF16)
        before = z2t.put("before", [P, NT, ECOLS], F32)
        within = z2t.put("within", [P, 3 * ECOLS], F32)
        ones_f = z2t.put("ones_f", [P, ECOLS], F32)
        edge_tmp = z2t.put("edge_tmp", [P, ECOLS], I32)
        dlo = z2t.put("dlo", [P, ECOLS], F32)
        blk = z2t.put("blk", [P, ECOLS], F32)
        typ = z2t.put("typ", [P, ECOLS], F32)
        posf = z2t.put("posf", [P, ECOLS], F32)
        src_i = z2t.put("src_i", [P, ECOLS], I32)
        dst_i = z2t.put("dst_i", [P, ECOLS], I32)
        typ_i = z2t.put("typ_i", [P, ECOLS], I32)
        cnt_f = z2t.put("cnt_f", [P, 3, NT], F32)
        cnt_i = z2t.put("cnt_i", [P, 2, NT], I32)

        xin = [sem(f"x_loaded{j}") for j in range(NT)]
        edges_set, edges_in = sem("edges_set"), sem("edges_in")
        consts = sem("consts_ready")
        onehot_ready, totals_done, totals_read, tri_done, tri_read = (
            sem("block_onehot_ready"), sem("column_totals_done"), sem("column_totals_read"),
            sem("ranks_done"), sem("ranks_read"))
        pad_set = sem("pad_rows_set")
        norm_ready, tr_done, hi_done, lo_done = (
            sem("norm_ready"), sem("transposed"), sem("xhi_written"), sem("xlo_written"))
        var_ready, sqrt_ready = sem("var_ready"), sem("sqrt_ready")

        groups = [list(range(a, min(a + 3, NT))) for a in range(0, NT, 3)]
        with nc.Block() as block:
            @block.sync
            def _(sp):
                for j in range(NT):
                    if j == NT - 1:
                        sp.wait_ge(pad_set, 1)
                    sp.dma_start(x_all[:rows(j), j, :], x[j * P:j * P + rows(j), :]).then_inc(xin[j], 16)

            @block.gpsimd
            def _(pool):
                built = sem("built")
                nc.gpsimd.memset(ident[:], 0.0).then_inc(built, 1)
                nc.gpsimd.memset(tri[:], 1.0).then_inc(built, 1)
                nc.gpsimd.memset(ones[:], 1.0).then_inc(consts, 1)
                nc.gpsimd.iota(iota[:], pattern=[[1, 257]], base=0, channel_multiplier=0,
                               allow_small_or_imprecise_dtypes=True).then_inc(consts, 1)
                nc.gpsimd.iota(lanes[:], pattern=[[1, 1]], base=0, channel_multiplier=1,
                               allow_small_or_imprecise_dtypes=True).then_inc(consts, 1)
                pool.wait_ge(built, 2)
                nc.gpsimd.affine_select(out=ident[:], in_=ident[:], compare_op=ALU.not_equal, fill=1.0,
                                        base=0, pattern=[[-1, P]], channel_multiplier=1).then_inc(consts, 1)
                nc.gpsimd.affine_select(out=tri[:], in_=tri[:], compare_op=ALU.is_gt, fill=0.0,
                                        base=0, pattern=[[1, P]], channel_multiplier=-1).then_inc(consts, 1)

            @block.scalar
            def _(act):
                act.wait_ge(edges_set, 1)
                for tile, vec in ((src_i, src), (dst_i, dst), (typ_i, edge_type)):
                    act.dma_start(tile[:, 0:EFULL], vec[0:EFULL * P].rearrange("(p c) -> p c", p=P)
                                  ).then_inc(edges_in, 16)
                    act.dma_start(tile[0:EREST, EFULL:EFULL + 1],
                                  vec[EFULL * P:E].rearrange("(p c) -> p c", c=1)).then_inc(edges_in, 16)
                act.wait_ge(var_ready, 1)
                nc.scalar.activation(tmp10[:, 1, :], tmp10[:, 0, :], ACT.Sqrt).then_inc(sqrt_ready, 1)
                for j in range(NT):
                    for g in range(2):
                        n = 2 * j + g
                        act.wait_ge(tr_done, n + 1)
                        nc.scalar.activation(xhi[:, 4 * g:4 * g + 4, j * P:(j + 1) * P],
                                             psum[n % 4][:].rearrange("p (k n) -> p k n", k=4),
                                             ACT.Copy).then_inc(hi_done, 1)

            @block.vector
            def _(dve):
                v = nc.vector
                step = chain(dve, "stage1_step")
                v.memset(x_all[96:P, NT - 1, :], 0.0).then_inc(pad_set, 1)
                step(v.memset(src_i[:], 0))
                step(v.memset(typ_i[:], 0))
                v.memset(dst_i[:], -1).then_inc(edges_set, 1)
                step(v.memset(ones_f[:], 1.0))
                for j in range(NT):
                    dve.wait_ge(xin[j], 16)
                    v.bn_stats(stat[:, j, 0, :], x_all[:, j, 0:HALF])
                    step(v.bn_stats(stat[:, j, 1, :], x_all[:, j, HALF:D]))
                    step(v.bn_aggr(aggr[:, j, :], stat[:, j, :, :].rearrange("p a b -> p (a b)")))
                step(v.tensor_copy(mean[:], aggr[:, :, 0]))
                v.tensor_scalar(tmp10[:, 0, :], aggr[:, :, 1], EPS, None, ALU.add).then_inc(var_ready, 1)
                dve.wait_ge(sqrt_ready, 1)
                dve.wait_ge(var_ready, 1)
                step(v.reciprocal(tmp10[:, 2, :], tmp10[:, 1, :]))
                step(v.tensor_tensor(tmp10[:, 3, :], tmp10[:, 2, :], tmp10[:, 2, :], ALU.mult))
                step(v.tensor_tensor(tmp10[:, 3, :], tmp10[:, 3, :], tmp10[:, 0, :], ALU.mult))
                step(v.tensor_scalar(tmp10[:, 3, :], tmp10[:, 3, :], -0.5, 1.5, ALU.mult, ALU.add))
                step(v.tensor_tensor(rstd[:], tmp10[:, 3, :], tmp10[:, 2, :], ALU.mult))
                for j in range(NT):
                    v.tensor_scalar(x_all[:, j, :], x_all[:, j, :], mean[:, j:j + 1], rstd[:, j:j + 1],
                                    ALU.subtract, ALU.mult).then_inc(norm_ready, 1)
                for n in range(2 * NT):
                    j, g = n // 2, n % 2
                    dve.wait_ge(hi_done, n + 1)
                    sl = (slice(None), slice(4 * g, 4 * g + 4), slice(j * P, (j + 1) * P))
                    v.tensor_tensor(xlo[sl], psum[n % 4][:].rearrange("p (k n) -> p k n", k=4),
                                    xhi[sl].bitcast(F32), ALU.subtract).then_inc(lo_done, 1)

            @block.tensor
            def _(pe):
                pe.wait_ge(consts, 5)
                for n in range(2 * NT):
                    j, g = n // 2, n % 2
                    pe.wait_ge(norm_ready, j + 1)
                    if n >= 4:
                        pe.wait_ge(lo_done, n - 3)
                    for k in range(4):
                        kc = 4 * g + k
                        ins = pe.transpose(psum[n % 4][:, k * P:(k + 1) * P], x_all[:, j, kc * P:(kc + 1) * P], ident[:])
                    ins.then_inc(tr_done, 1)

        stage = nc.alloc_sbuf_tensor_at("w_stage", [P, 2, 2, HALF], F32, offset=OFF_STAGE)
        yout = nc.alloc_sbuf_tensor_at("y_out", [P, 4, HALF], F32, offset=OFF_YOUT)
        whi = [nc.alloc_sbuf_tensor_at(f"whi{h}", [P, KC, HALF], F32R, offset=o)
               for h, o in enumerate((OFF_W0, OFF_W1))]
        wlo = [nc.alloc_sbuf_tensor_at(f"wlo{h}", [P, KC, HALF], F32R, offset=o + 16 * KB)
               for h, o in enumerate((OFF_W0, OFF_W1))]
        z2b = Zone(z2.at, LIMIT - z2.at)
        CPQ = 7
        SORT_R = ECOLS // (8 * CPQ)
        assert SORT_R * 8 * CPQ == ECOLS
        oh_lo = z2b.put("oh_lo", [P, CPQ, P], F32R)
        oh_val = z2b.put("oh_val", [P, CPQ, 2, ET], F32R)
        oh_khi = z2b.put("oh_khi", [P, CPQ, KHI], BF16)
        oh_klo = z2b.put("oh_klo", [P, CPQ, 256], BF16)
        placed = z2b.put("placed", [P, 2, ET], F32)
        placed_i = z2b.put("placed_i", [P, 3, ET], I32)
        tfl = z2b.put("tfl", [P, 4, ET], F32)
        inv = z2b.put("inv", [KHI, 256], F32)
        YB, PLACE_BANK, COUNT_BANK = 4, psum[6], psum[7]

        w_in = [sem(f"w_stage_loaded{i}") for i in range(2)]
        w_hi, w_lo = sem("w_hi_written"), sem("w_lo_written")
        y_ready, y_evac = sem("y_ready"), sem("y_evacuated")
        y_out = [sem(f"y_stored{i}") for i in range(YB)]
        cols_ready, cols_used = sem("onehots_ready"), sem("onehots_used")
        inv_ready, inv_out, key_ready, w_gathered = (
            sem("inv_ready"), sem("inv_stored"), sem("keys_ready"), sem("edge_w_gathered"))

        def w_rows(w, q, h):
            return w[2 * q * P:(2 * q + 2) * P, h * HALF:(h + 1) * HALF].rearrange("(k p) n -> p k n", p=P)

        with nc.Block() as block:
            @block.sync
            def _(sp):
                def load(r, h, q, first=False):
                    n = r * 8 + h * 4 + q
                    if not first:
                        sp.wait_ge(w_lo, n - 1)
                    w = weight[r] if isinstance(r, int) else weight[bass.ds(r, 1)].rearrange("a k n -> (a k) n")
                    sp.dma_start(stage[:, q % 2], w_rows(w, q, h)).then_inc(w_in[q % 2], 16)

                def store(r, h, j):
                    m = r * 2 * NT + h * NT + j
                    sp.wait_ge(y_evac, m + 1)
                    sp.dma_start(Y[bass.ds(r * NP + j * P, P), h * HALF:(h + 1) * HALF],
                                 yout[:, (h * NT + j) % YB]).then_inc(y_out[(h * NT + j) % YB], 16)

                load(0, 0, 0, True)
                load(0, 0, 1, True)
                for q in (2, 3):
                    load(0, 0, q)
                for q in (0, 1):
                    load(0, 1, q)

                def relation(r, last=False):
                    for h in range(2):
                        for j in range(NT):
                            store(r, h, j)
                            if j % 2 == 0 and j < 8:
                                q = j // 2 + 2
                                r2, h2 = (r, h + 1) if q < 4 else (r, h + 2)
                                if h2 >= 2:
                                    if last:
                                        continue
                                    r2, h2 = r2 + 1, h2 - 2
                                load(r2, h2, q % 4)
                relation(0)
                with sp.Fori(1, R - 1) as r:
                    relation(r)
                relation(R - 1, True)
                for i in range(YB):
                    sp.wait_ge(y_out[i], 16 * (R * 2 * NT // YB))

            @block.scalar
            def _(act):
                def split_hi(r, h, q, first=False):
                    n = r * 8 + h * 4 + q
                    act.wait_ge(w_in[q % 2], 16 * (r * 4 + h * 2 + q // 2 + 1))
                    if not first and q == 0:
                        act.wait_ge(y_ready, (r * 2 + h - 1) * NT)
                    nc.scalar.activation(whi[h][:, 2 * q:2 * q + 2, :], stage[:, q % 2], ACT.Copy).then_inc(w_hi, 1)

                def evacuate(r, h, j, first=False):
                    m = r * 2 * NT + h * NT + j
                    slot = (h * NT + j) % YB
                    act.wait_ge(y_ready, m + 1)
                    if not (first and h * NT + j < YB):
                        act.wait_ge(y_out[slot], 16 * (r * (2 * NT // YB) + (h * NT + j) // YB))
                    nc.scalar.activation(yout[:, slot], psum[slot][:], ACT.Copy).then_inc(y_evac, 1)

                for q in range(4):
                    split_hi(0, 0, q, True)

                def relation(r, first=False, last=False):
                    for h in range(2):
                        for j in range(NT):
                            evacuate(r, h, j, first)
                            if j % 2 == 0 and j < 8 and not (last and h == 1):
                                split_hi(*((r, 1) if h == 0 else (r + 1, 0)), j // 2, first and h == 0)
                relation(0, first=True)
                with act.Fori(1, R - 1) as r:
                    relation(r)
                relation(R - 1, last=True)

            @block.vector
            def _(dve):
                v = nc.vector

                def split_lo(r, h, q):
                    dve.wait_ge(w_hi, r * 8 + h * 4 + q + 1)
                    v.tensor_tensor(wlo[h][:, 2 * q:2 * q + 2, :], stage[:, q % 2],
                                    whi[h][:, 2 * q:2 * q + 2, :].bitcast(F32), ALU.subtract).then_inc(w_lo, 1)

                def columns(r, part, first=False):
                    if not first:
                        dve.wait_ge(cols_used, (r - 1) * 8 + part)
                    for i in range(CPQ):
                        c = (r - 1) * 8 * CPQ + part * CPQ + i
                        at = bass.ds(c, 1)
                        v.tensor_scalar(oh_lo[:, i], iota[:, 0:P], place_lo[:, at], None, ALU.is_equal)
                        v.tensor_scalar(oh_val[:, i, 0], iota[:, 0:ET], place_hi[:, at], val_src[:, at],
                                        ALU.is_equal, ALU.mult)
                        v.tensor_scalar(oh_val[:, i, 1], iota[:, 0:ET], place_hi[:, at], val_dst[:, at],
                                        ALU.is_equal, ALU.mult)
                        v.tensor_scalar(oh_khi[:, i], iota[:, 0:KHI], key_hi[:, at], None, ALU.is_equal)
                        ins = v.tensor_scalar(oh_klo[:, i], iota[:, 0:256], key_lo[:, at], None, ALU.is_equal)
                    ins.then_inc(cols_ready, 1)

                def edge_places():
                    step = chain(dve, "places_step")
                    dve.wait_ge(edges_in, 16 * 6)
                    v.tensor_copy(val_src[:], src_i[:])
                    step(v.tensor_copy(typ[:], typ_i[:]))
                    step(v.tensor_scalar(edge_tmp[:], dst_i[:], 7, None, ALU.arith_shift_right))
                    step(v.tensor_copy(blk[:], edge_tmp[:]))
                    for j in range(NT):
                        ins = v.tensor_scalar(onehot[:, j, :], blk[:], float(j), None, ALU.is_equal)
                    ins.then_inc(onehot_ready, 1)
                    step(v.tensor_scalar(edge_tmp[:], dst_i[:], P - 1, None, ALU.bitwise_and))
                    step(v.tensor_copy(dlo[:], edge_tmp[:]))
                    step(v.tensor_scalar(dlo[:], dlo[:], 1.0, float(R), ALU.add, ALU.mult))
                    step(v.tensor_tensor(val_dst[:], dlo[:], typ[:], ALU.add))
                    step(v.tensor_scalar(edge_tmp[:], dst_i[:], 5, None, ALU.arith_shift_right))
                    step(v.tensor_copy(key_hi[:], edge_tmp[:]))
                    step(v.tensor_scalar(edge_tmp[:], dst_i[:], 31, None, ALU.bitwise_and))
                    step(v.tensor_copy(dlo[:], edge_tmp[:]))
                    step(v.scalar_tensor_tensor(key_lo[:], dlo[:], float(R), typ[:], ALU.mult, ALU.add))
                    for g, js in enumerate(groups):
                        dve.wait_ge(totals_done, g + 1)
                        for n, j in enumerate(js):
                            step(v.tensor_tensor_scan(before[:, j, :], ones_f[:], psum[4 + g][:, n * ECOLS:(n + 1) * ECOLS],
                                                      0.0, ALU.mult, ALU.add))
                            step(v.tensor_copy(cnt_f[:, 0, j:j + 1], before[:, j, ECOLS - 1:ECOLS]))
                            ins = v.tensor_tensor(before[:, j, :], before[:, j, :],
                                                  psum[4 + g][:, n * ECOLS:(n + 1) * ECOLS], ALU.subtract)
                            step(ins)
                    shift = (GROUP * P).bit_length() - 1
                    step(v.tensor_scalar(cnt_i[:, 0, :], cnt_f[:, 0, :], float(GROUP * P - 1), None, ALU.add))
                    step(v.tensor_scalar(cnt_i[:, 1, :], cnt_i[:, 0, :], shift, shift,
                                         ALU.arith_shift_right, ALU.logical_shift_left))
                    step(v.tensor_copy(cnt_f[:, 1, :], cnt_i[:, 1, :]))
                    step(v.tensor_tensor_scan(cnt_f[:, 2, :], ones_f[:, 0:NT], cnt_f[:, 1, :], 0.0, ALU.mult, ALU.add))
                    step(v.tensor_tensor(blk_base[:], cnt_f[:, 2, :], cnt_f[:, 1, :], ALU.subtract))
                    v.tensor_copy(cnt_f[:, 0, :], cnt_f[:, 2, :]).then_inc(totals_read, 1)
                    step(v.tensor_scalar(posf[:], blk[:], 0.0, float(1 << 16), ALU.is_lt, ALU.mult))
                    for g, js in enumerate(groups):
                        dve.wait_ge(tri_done, g + 1)
                        w = len(js) * ECOLS
                        step(v.tensor_tensor(within[:, :w], psum[4 + g][:, :w],
                                             before[:, js[0]:js[-1] + 1, :].rearrange("p j c -> p (j c)"), ALU.add))
                        for n, j in enumerate(js):
                            cut = within[:, n * ECOLS:(n + 1) * ECOLS]
                            step(v.scalar_tensor_tensor(cut, cut, blk_base[:, j:j + 1], onehot[:, j, :],
                                                        ALU.add, ALU.mult))
                            step(v.tensor_tensor(posf[:], posf[:], cut, ALU.add))
                    v.tensor_copy(edge_tmp[:], posf[:]).then_inc(tri_read, 1)
                    dve.wait_ge(tri_read, 1)
                    step(v.tensor_scalar(dst_i[:], edge_tmp[:], P - 1, None, ALU.bitwise_and))
                    step(v.tensor_copy(place_lo[:], dst_i[:]))
                    step(v.tensor_scalar(dst_i[:], edge_tmp[:], 7, None, ALU.arith_shift_right))
                    step(v.tensor_copy(place_hi[:], dst_i[:]))

                for q in range(4):
                    split_lo(0, 0, q)
                edge_places()

                def relation(r, sorts, first=False, last=False):
                    for h in range(2):
                        for q in range(4):
                            if sorts:
                                columns(r, 4 * h + q, first and h * 4 + q == 0)
                            if not (last and h == 1):
                                split_lo(*((r, 1) if h == 0 else (r + 1, 0)), q)
                relation(0, False)
                relation(1, True, first=True)
                with dve.Fori(2, 1 + SORT_R) as r:
                    relation(r, True)
                step = chain(dve, "stage2_step")
                dve.wait_ge(cols_used, 8 * SORT_R)
                step(v.tensor_copy(placed[:], PLACE_BANK[:, 0:2 * ET].rearrange("p (a t) -> p a t", a=2)))
                step(v.tensor_scalar(inv[:], COUNT_BANK[0:KHI, 0:256], 1.0, None, ALU.max))
                v.reciprocal(inv[:], inv[:]).then_inc(inv_ready, 1)
                step(v.tensor_copy(placed_i[:, 0], placed[:, 1]))
                step(v.tensor_scalar(placed_i[:, 1], placed_i[:, 0], 3, None, ALU.arith_shift_right))
                step(v.tensor_copy(edge_dst[:], placed_i[:, 1]))
                step(v.tensor_scalar(placed_i[:, 2], placed_i[:, 0], R - 1, None, ALU.bitwise_and))
                step(v.tensor_copy(tfl[:, 0], placed_i[:, 2]))
                step(v.scalar_tensor_tensor(edge_row[:], tfl[:, 0], float(NP), placed[:, 0], ALU.mult, ALU.add))
                step(v.tensor_scalar(tfl[:, 1], iota[:, 0:ET], float(P), None, ALU.mult))
                step(v.memset(tfl[:, 2], 0.0))
                for j in range(1, NT):
                    step(v.scalar_tensor_tensor(tfl[:, 2], tfl[:, 1], blk_base[:, j:j + 1], tfl[:, 2],
                                                ALU.is_ge, ALU.add))
                step(v.tensor_copy(tile_block[:], tfl[:, 2]))
                step(v.scalar_tensor_tensor(tfl[:, 3], tfl[:, 2], float(P * R), placed[:, 1], ALU.mult, ALU.add))
                v.tensor_scalar(edge_key[:], tfl[:, 3], -float(R), 0.0, ALU.add, ALU.max).then_inc(key_ready, 1)
                with dve.Fori(1 + SORT_R, R - 1) as r:
                    relation(r, False)
                relation(R - 1, False, last=True)

            @block.gpsimd
            def _(pool):
                pool.wait_ge(inv_ready, 1)
                pool.dma_start(INV.rearrange("(a b) c -> a (b c)", b=256), inv[:]).then_inc(inv_out, 16)
                pool.wait_ge(inv_out, 16)
                pool.wait_ge(key_ready, 1)
                for t in range(ET):
                    nc.gpsimd.indirect_dma_start(
                        out=edge_w[:, t:t + 1], out_offset=None, in_=INV,
                        in_offset=bass.IndirectOffsetOnAxis(ap=edge_key[:, t:t + 1], axis=0)).then_inc(w_gathered, 16)
                pool.wait_ge(w_gathered, 16 * ET)

            @block.tensor
            def _(pe):
                def product(r, h, j, first=False):
                    m = r * 2 * NT + h * NT + j
                    slot = (h * NT + j) % YB
                    if j == 0:
                        pe.wait_ge(w_lo, r * 8 + h * 4 + 4)
                    if not (first and h * NT + j < YB):
                        pe.wait_ge(y_evac, m + 1 - YB)
                    at = slice(j * P, (j + 1) * P)
                    for k in range(KC):
                        pe.matmul(psum[slot][:], xhi[:, k, at], whi[h][:, k], start=(k == 0), stop=False)
                        pe.matmul(psum[slot][:], xhi[:, k, at], wlo[h][:, k], start=False, stop=False)
                        ins = pe.matmul(psum[slot][:], xlo[:, k, at], whi[h][:, k], start=False, stop=(k == KC - 1))
                    ins.then_inc(y_ready, 1)

                def columns(r, part, first=False, last=False):
                    pe.wait_ge(cols_ready, (r - 1) * 8 + part + 1)
                    for i in range(CPQ):
                        a, z = first and i == 0, last and i == CPQ - 1
                        pe.matmul(PLACE_BANK[:, 0:2 * ET], oh_lo[:, i],
                                  oh_val[:, i].rearrange("p a t -> p (a t)"), start=a, stop=z, skip_group_check=True)
                        ins = pe.matmul(COUNT_BANK[0:KHI, 0:256], oh_khi[:, i], oh_klo[:, i],
                                        start=a, stop=z, skip_group_check=True)
                    ins.then_inc(cols_used, 1)

                def ranks(left, done):
                    pe.wait_ge(onehot_ready, 1)
                    for g, js in enumerate(groups):
                        pe.matmul(psum[4 + g][:, :len(js) * ECOLS], left[:],
                                  onehot[:, js[0]:js[-1] + 1, :].rearrange("p j c -> p (j c)"),
                                  start=True, stop=True).then_inc(done, 1)

                def relation(r, sorts, start=False, first=False, last=False):
                    for h in range(2):
                        for j in range(NT):
                            product(r, h, j, start)
                            if start and h == 0 and j == 1:
                                ranks(ones, totals_done)
                            if start and h == 0 and j == 5:
                                pe.wait_ge(totals_read, 1)
                                ranks(tri, tri_done)
                            if sorts and j % 2 == 1 and j < 8:
                                part = 4 * h + j // 2
                                columns(r, part, first and part == 0, last and part == 7)
                relation(0, False, start=True)
                relation(1, True, first=True)
                with pe.Fori(2, SORT_R) as r:
                    relation(r, True)
                relation(SORT_R, True, last=True)
                with pe.Fori(1 + SORT_R, R) as r:
                    relation(r, False)


        z3 = Zone(OFF_W1, LIMIT - OFF_W1)
        acc = z3.put("acc", [P, NT * D], F32)
        after_acc = z3.at
        gath = z3.put("gathered", [P, 4, D], F32)
        ghi = z3.put("ghi", [P, 2, D], F32R)
        glo = z3.put("glo", [P, 2, D], F32R)
        sel = z3.put("sel", [P, 2, P], F32R)
        PH = PAIRS // 4
        TH = PH * GROUP
        EXTRA = PH - 2 * NT
        assert GROUP == 2 and EXTRA >= 1 and TH % 4 == 0
        w_in = [sem(f"w3_stage_loaded{i}") for i in range(2)]
        w_hi, w_lo = sem("w3_hi_written"), sem("w3_lo_written")
        y_ready, y_evac = sem("y3_ready"), sem("y3_evacuated")
        y_out = [sem(f"y3_stored{i}") for i in range(2)]
        g_in = [sem(f"rows_gathered{i}") for i in range(4)]
        g_hi, g_lo, g_used, acc_done = (
            sem("rows_hi"), sem("rows_lo"), sem("edge_tiles_used"), sem("pairs_accumulated"))
        acc_zero = sem("acc_zeroed")

        def changes(g):
            for q in range(4):
                yield "split", q
                if q < EXTRA:
                    yield "pair", 2 * NT + q
            for e in range(4, EXTRA):
                yield "pair", 2 * NT + e

        with nc.Block() as block:
            @block.sync
            def _(sp):
                def load(g, q):
                    n = 4 * g + q
                    if n >= 2:
                        sp.wait_ge(w_lo, n - 1)
                    w = root if g < 2 else w_gate[D:2 * D, :]
                    sp.dma_start(stage[:, q % 2], w_rows(w, q, g % 2)).then_inc(w_in[q % 2], 16)

                load(0, 0)
                load(0, 1)
                for g in range(4):
                    load(g, 2)
                    load(g, 3)
                    if g < 3:
                        load(g + 1, 0)
                        load(g + 1, 1)
                    for j in range(NT):
                        sp.wait_ge(y_evac, g * NT + j + 1)
                        sp.dma_start(YX[g // 2, j * P:(j + 1) * P, (g % 2) * HALF:(g % 2 + 1) * HALF],
                                     yout[:, j % 2]).then_inc(y_out[j % 2], 16)
                for i in range(2):
                    sp.wait_ge(y_out[i], 16 * 2 * NT)

            @block.gpsimd
            def _(pool):
                for t in range(ET):
                    if t >= 4:
                        pool.wait_ge(g_lo, t - 3)
                    nc.gpsimd.indirect_dma_start(
                        out=gath[:, t % 4], out_offset=None, in_=Y,
                        in_offset=bass.IndirectOffsetOnAxis(ap=edge_row[:, t:t + 1], axis=0)).then_inc(g_in[t % 4], 16)

            @block.scalar
            def _(act):
                def split_hi(g, q):
                    act.wait_ge(w_in[q % 2], 16 * (2 * g + q // 2 + 1))
                    nc.scalar.activation(whi[0][:, 2 * q:2 * q + 2, :], stage[:, q % 2], ACT.Copy).then_inc(w_hi, 1)

                def pair_hi(g, p, first=False):
                    for i in range(2):
                        tl = 2 * p + i
                        t = g * TH + tl
                        act.wait_ge(g_in[tl % 4], 16 * (g * (TH // 4) + tl // 4 + 1))
                        if not (first and tl < 2):
                            act.wait_ge(g_used, t - 1)
                        nc.scalar.activation(ghi[:, i], gath[:, tl % 4], ACT.Copy,
                                             scale=edge_w[:, bass.ds(t, 1)]).then_inc(g_hi, 1)

                def half(g, first=False, last=False):
                    for j in range(NT):
                        for b in range(2):
                            pair_hi(g, 2 * j + b, first)
                        act.wait_ge(y_ready, g * NT + j + 1)
                        if not (first and j < 2):
                            act.wait_ge(y_out[j % 2], 16 * (g * (NT // 2) + j // 2))
                        nc.scalar.activation(yout[:, j % 2], psum[j % 2][:], ACT.Copy).then_inc(y_evac, 1)
                    for what, n in changes(g):
                        if what == "pair":
                            pair_hi(g, n)
                        elif not last:
                            split_hi(g + 1, n)
                for q in range(4):
                    split_hi(0, q)
                half(0, first=True)
                with act.Fori(1, 3) as g:
                    half(g)
                half(3, last=True)

            @block.vector
            def _(dve):
                v = nc.vector

                def split_lo(g, q):
                    dve.wait_ge(w_hi, 4 * g + q + 1)
                    v.tensor_tensor(wlo[0][:, 2 * q:2 * q + 2, :], stage[:, q % 2],
                                    whi[0][:, 2 * q:2 * q + 2, :].bitcast(F32), ALU.subtract).then_inc(w_lo, 1)

                def pair_lo(g, p, first=False):
                    for i in range(2):
                        tl = 2 * p + i
                        t = g * TH + tl
                        if not (first and tl < 2):
                            dve.wait_ge(g_used, t - 1)
                        v.tensor_scalar(sel[:, i], iota[:, 1:P + 1], edge_dst[:, bass.ds(t, 1)], None, ALU.is_equal)
                        dve.wait_ge(g_hi, t + 1)
                        v.scalar_tensor_tensor(glo[:, i], gath[:, tl % 4], edge_w[:, bass.ds(t, 1)],
                                               ghi[:, i].bitcast(F32), ALU.mult, ALU.subtract).then_inc(g_lo, 1)

                def accumulate(g, p, first=False):
                    n = g * PH + p
                    block_of = dve.value_load(tile_block[0:1, bass.ds(n * GROUP, 1)], min_val=0, max_val=NT - 1)
                    at = bass.ds(block_of * D, D)
                    dve.wait_ge(g_used, 2 * (n + 1))
                    if not first:
                        dve.wait_ge(acc_done, n)
                    for c in range(2):
                        at = bass.ds(block_of * D + c * BANK, BANK)
                        ins = v.tensor_tensor(acc[:, at], acc[:, at], psum[4 + 2 * (p % 2) + c][:], ALU.add)
                    ins.then_inc(acc_done, 1)

                def half(g, first=False, last=False):
                    for p in range(2 * NT):
                        pair_lo(g, p, first)
                        if p:
                            accumulate(g, p - 1, first and p == 1)
                    for what, n in changes(g):
                        if what == "pair":
                            pair_lo(g, n)
                            accumulate(g, n - 1)
                        elif not last:
                            split_lo(g + 1, n)
                    accumulate(g, PH - 1)
                v.memset(acc[:], 0.0).then_inc(acc_zero, 1)
                for q in range(4):
                    split_lo(0, q)
                dve.wait_ge(acc_zero, 1)
                half(0, first=True)
                with dve.Fori(1, 3) as g:
                    half(g)
                half(3, last=True)

            @block.tensor
            def _(pe):
                def product(g, j, b, first=False):
                    if b == 0:
                        if j == 0:
                            pe.wait_ge(w_lo, 4 * (g + 1))
                        if not (first and j < 2):
                            pe.wait_ge(y_evac, g * NT + j - 1)
                    at = slice(j * P, (j + 1) * P)
                    for k in range(4 * b, 4 * b + 4):
                        pe.matmul(psum[j % 2][:], xhi[:, k, at], whi[0][:, k], start=(k == 0), stop=False)
                        pe.matmul(psum[j % 2][:], xhi[:, k, at], wlo[0][:, k], start=False, stop=False)
                        ins = pe.matmul(psum[j % 2][:], xlo[:, k, at], whi[0][:, k], start=False, stop=(k == KC - 1))
                    if b == 1:
                        ins.then_inc(y_ready, 1)

                def pair(g, p, first=False):
                    if not (first and p < 2):
                        pe.wait_ge(acc_done, g * PH + p - 1)
                    for i in range(2):
                        pe.wait_ge(g_lo, g * TH + 2 * p + i + 1)
                        for c in range(2):
                            bank = psum[4 + 2 * (p % 2) + c]
                            cols = slice(c * BANK, (c + 1) * BANK)
                            pe.matmul(bank[:], sel[:, i], ghi[:, i, cols], start=(i == 0), stop=False)
                            ins = pe.matmul(bank[:], sel[:, i], glo[:, i, cols], start=False, stop=(i == 1))
                        ins.then_inc(g_used, 1)

                def half(g, first=False):
                    for j in range(NT):
                        for b in range(2):
                            product(g, j, b, first)
                            pair(g, 2 * j + b, first)
                    for e in range(EXTRA):
                        pair(g, 2 * NT + e)
                half(0, True)
                with pe.Fori(1, 4) as g:
                    half(g)


        wghi = nc.alloc_sbuf_tensor_at("wghi", [P, KC, D], F32R, offset=OFF_T)
        wglo = nc.alloc_sbuf_tensor_at("wglo", [P, KC, D], F32R, offset=OFF_T + 32 * KB)
        za, zb, zc = (Zone(OFF_T + 64 * KB, 16 * KB), Zone(OFF_YOUT, OFF_W1 - OFF_YOUT),
                      Zone(after_acc, LIMIT - after_acc))
        uhi = za.put("uhi", [P, 2, D], F32R)
        ulo = za.put("ulo", [P, 2, D], F32R)
        u = zb.put("u", [P, 2, D], F32)
        xr = zb.put("xr", [P, 2, D], F32)
        zg = zb.put("zg", [P, 2, D], F32)
        th = zb.put("th", [P, 2, D], F32)
        xn = zb.put("xn", [P, 2, D], F32)
        x1 = zc.put("x1", [P, 2, D], F32)
        xn2 = zc.put("xn2", [P, 2, D], F32)
        xn2t = zc.put("xn2t", [P, KC, P], F32)
        bias_b = zc.put("bias_b", [P, D], F32)
        bgate_b = zc.put("bgate_b", [P, D], F32)
        gw_rows = zc.put("gw_rows", [P, D], F32)
        gw_t = zc.put("gw_t", [P, KC, X], F32)
        st2 = zc.put("st2", [P, 2, 6], F32)
        ag2 = zc.put("ag2", [P, 2], F32)
        rs = zc.put("rs", [P, 4], F32)
        rs_i = zc.put("rs_i", [P, 2], I32)
        LOGITS = psum[6]

        w_in = [sem(f"wg_stage_loaded{i}") for i in range(2)]
        w_hi, w_lo = sem("wg_hi_written"), sem("wg_lo_written")
        rows_in, small_in = sem("small_rows_loaded"), sem("gate_w_loaded")
        x_in, r_in, g_in4 = ([sem(f"{n}_loaded{i}") for i in range(2)] for n in ("xr", "u", "zg"))
        bias_done, bg_done, sum_done = sem("bias_added"), sem("bgate_added"), sem("x_plus_norm")
        u_done, xn_done, tu_done, uhi_done, ulo_done, th_done = (
            sem("u_done"), sem("xn_done"), sem("u_transposed"), sem("uhi_done"), sem("ulo_done"), sem("tanh_done"))
        z_done, zg_done, x1_done, xn2_done = sem("z_done"), sem("z_read"), sem("x1_done"), sem("xn2_done")
        tx_done, tx_evac, lg_done = sem("xn2_transposed"), sem("xn2t_written"), sem("logits_done")
        x1_out, xn2_out = ([sem(f"{n}_stored{i}") for i in range(2)] for n in ("x1", "xn2"))
        gwt_done, gwt_evac = sem("gate_w_transposed"), sem("gate_w_t_written")

        with nc.Block() as block:
            @block.sync
            def _(sp):
                def fetch_u(j):
                    if j >= 2:
                        sp.wait_ge(th_done, j - 1)
                        sp.wait_ge(tu_done, 2 * (j - 1))
                    sp.dma_start(u[:, j % 2], YX[0, j * P:(j + 1) * P, :]).then_inc(r_in[j % 2], 16)

                def fetch_x(j):
                    if j >= 2:
                        sp.wait_ge(x1_done, j - 1)
                    sp.dma_start(xr[:rows(j), j % 2], x[j * P:j * P + rows(j), :]).then_inc(x_in[j % 2], 16)
                    sp.dma_start(zg[:, j % 2], YX[1, j * P:(j + 1) * P, :]).then_inc(g_in4[j % 2], 16)

                for n in range(8):
                    h, q = n // 4, n % 4
                    if n >= 2:
                        sp.wait_ge(w_lo, n - 1)
                    sp.dma_start(stage[:, q % 2], w_rows(w_gate, q, h)).then_inc(w_in[q % 2], 16)
                    if n == 1:
                        fetch_u(0)
                        fetch_u(1)
                        sp.dma_start(bias_b[:], bias.partition_broadcast(P)).then_inc(rows_in, 16)
                        sp.dma_start(bgate_b[:], b_gate.partition_broadcast(P)).then_inc(rows_in, 16)
                        sp.dma_start(gw_rows[0:X, :], gate_w).then_inc(small_in, 16)
                        fetch_x(0)
                        fetch_x(1)
                for j in range(NT + 1):
                    if j + 2 < NT:
                        fetch_u(j + 2)
                    if j == 0:
                        continue
                    d = j - 1
                    sp.wait_ge(x1_done, d + 1)
                    sp.dma_start(X1[d * P:(d + 1) * P, :], x1[:, d % 2]).then_inc(x1_out[d % 2], 16)
                    if d + 2 < NT:
                        fetch_x(d + 2)
                    sp.wait_ge(xn2_done, d + 1)
                    sp.dma_start(XN2[d * P:(d + 1) * P, :], xn2[:, d % 2]).then_inc(xn2_out[d % 2], 16)
                for i in range(2):
                    sp.wait_ge(x1_out[i], 16 * NT // 2)
                    sp.wait_ge(xn2_out[i], 16 * NT // 2)

            @block.gpsimd
            def _(pool):
                pool.wait_ge(rows_in, 32)

                def add_biases(j):
                    pool.wait_ge(r_in[j % 2], 16 * (j // 2 + 1))
                    nc.gpsimd.tensor_tensor(u[:, j % 2], u[:, j % 2], bias_b[:], ALU.add).then_inc(bias_done, 1)
                add_biases(0)
                add_biases(1)
                for j in range(NT):
                    if j + 2 < NT:
                        add_biases(j + 2)
                    pool.wait_ge(g_in4[j % 2], 16 * (j // 2 + 1))
                    nc.gpsimd.tensor_tensor(zg[:, j % 2], zg[:, j % 2], bgate_b[:], ALU.add).then_inc(bg_done, 1)
                    pool.wait_ge(xn_done, j + 1)
                    nc.gpsimd.tensor_tensor(xr[:, j % 2], xr[:, j % 2], xn[:, j % 2], ALU.add).then_inc(sum_done, 1)

            @block.scalar
            def _(act):
                def split_hi(n):
                    h, q = n // 4, n % 4
                    act.wait_ge(w_in[q % 2], 16 * (n // 2 + 1))
                    nc.scalar.activation(wghi[:, 2 * q:2 * q + 2, h * HALF:(h + 1) * HALF], stage[:, q % 2],
                                         ACT.Copy).then_inc(w_hi, 1)

                def u_part(j):
                    for g in range(2):
                        act.wait_ge(tu_done, 2 * j + g + 1)
                        if j >= 2:
                            act.wait_ge(z_done, 2 * (j - 1))
                        nc.scalar.activation(uhi[:, j % 2, g * BANK:(g + 1) * BANK], psum[g][:],
                                             ACT.Copy).then_inc(uhi_done, 1)
                    if j >= 2:
                        act.wait_ge(x1_done, j - 1)
                    act.wait_ge(u_done, j + 1)
                    nc.scalar.activation(th[:, j % 2], u[:, j % 2], ACT.Tanh).then_inc(th_done, 1)

                def xt_part(j):
                    for g in range(2):
                        act.wait_ge(tx_done, 2 * j + g + 1)
                        if j >= 1:
                            act.wait_ge(lg_done, j)
                        nc.scalar.activation(xn2t[:, 4 * g:4 * g + 4, :],
                                             psum[g][:].rearrange("p (k n) -> p k n", k=4),
                                             ACT.Copy).then_inc(tx_evac, 1)
                split_hi(0)
                split_hi(1)
                u_part(0)
                for n in range(2, 8):
                    split_hi(n)
                act.wait_ge(gwt_done, 1)
                nc.scalar.activation(gw_t[:], psum[7][:, 0:KC * X].rearrange("p (k e) -> p k e", e=X),
                                     ACT.Copy).then_inc(gwt_evac, 1)
                for j in range(NT):
                    if j + 1 < NT:
                        u_part(j + 1)
                    if j >= 2:
                        xt_part(j - 2)
                xt_part(NT - 2)
                xt_part(NT - 1)

            @block.vector
            def _(dve):
                v = nc.vector
                step = chain(dve, "stage4_step")

                def split_lo(n):
                    h, q = n // 4, n % 4
                    dve.wait_ge(w_hi, n + 1)
                    at = (slice(None), slice(2 * q, 2 * q + 2), slice(h * HALF, (h + 1) * HALF))
                    v.tensor_tensor(wglo[at], stage[:, q % 2], wghi[at].bitcast(F32), ALU.subtract).then_inc(w_lo, 1)

                def make_u(j):
                    dve.wait_ge(bias_done, j + 1)
                    v.tensor_tensor(u[:, j % 2], u[:, j % 2], acc[:, j * D:(j + 1) * D], ALU.add).then_inc(u_done, 1)

                def u_low(j):
                    for g in range(2):
                        dve.wait_ge(uhi_done, 2 * j + g + 1)
                        at = (slice(None), j % 2, slice(g * BANK, (g + 1) * BANK))
                        v.tensor_tensor(ulo[at], psum[g][:], uhi[at].bitcast(F32), ALU.subtract).then_inc(ulo_done, 1)

                def finish(j):
                    i = j % 2
                    dve.wait_ge(x_in[i], 16 * (j // 2 + 1))
                    v.tensor_scalar(xn[:, i], xr[:, i], mean[:, j:j + 1], rstd[:, j:j + 1],
                                    ALU.subtract, ALU.mult).then_inc(xn_done, 1)
                    dve.wait_ge(th_done, j + 1)
                    dve.wait_ge(xn_done, j + 1)
                    step(v.tensor_tensor(th[:, i], th[:, i], xn[:, i], ALU.subtract))
                    dve.wait_ge(bg_done, j + 1)
                    for c in range(2):
                        dve.wait_ge(z_done, 2 * j + c + 1)
                        ins = v.tensor_tensor(zg[:, i, c * BANK:(c + 1) * BANK], psum[2 + 2 * i + c][:],
                                              zg[:, i, c * BANK:(c + 1) * BANK], ALU.add)
                    ins.then_inc(zg_done, 1)
                    dve.wait_ge(zg_done, j + 1)
                    step(v.tensor_tensor(th[:, i], th[:, i], zg[:, i], ALU.mult))
                    dve.wait_ge(sum_done, j + 1)
                    if j >= 2:
                        dve.wait_ge(x1_out[i], 16 * (j // 2))
                        dve.wait_ge(xn2_out[i], 16 * (j // 2))
                        dve.wait_ge(tx_done, 2 * (j - 1))
                    v.tensor_tensor(x1[:, i], xr[:, i], th[:, i], ALU.add).then_inc(x1_done, 1)
                    dve.wait_ge(x1_done, j + 1)
                    v.bn_stats(st2[:, 0, :], x1[:, i, 0:HALF])
                    step(v.bn_stats(st2[:, 1, :], x1[:, i, HALF:D]))
                    step(v.bn_aggr(ag2[:], st2[:].rearrange("p a b -> p (a b)")))
                    step(v.tensor_scalar(rs[:, 0:1], ag2[:, 1:2], EPS, None, ALU.add))
                    step(v.tensor_scalar(rs_i[:, 0:1], rs[:, 0:1].bitcast(I32), 1, None, ALU.arith_shift_right))
                    step(v.tensor_scalar(rs_i[:, 1:2], rs_i[:, 0:1], -1.0, float(0x5F3759DF), ALU.mult, ALU.add))
                    y = rs_i[:, 1:2].bitcast(F32)
                    for n in range(4):
                        step(v.scalar_tensor_tensor(rs[:, 1:2], y, rs[:, 0:1], y, ALU.mult, ALU.mult))
                        step(v.tensor_scalar(rs[:, 2:3], rs[:, 1:2], -0.5, 1.5, ALU.mult, ALU.add))
                        step(v.tensor_tensor(rs[:, 3:4], y, rs[:, 2:3], ALU.mult))
                        y = rs[:, 3:4]
                    v.tensor_scalar(xn2[:, i], x1[:, i], ag2[:, 0:1], rs[:, 3:4],
                                    ALU.subtract, ALU.mult).then_inc(xn2_done, 1)
                    dve.wait_ge(xn2_done, j + 1)

                split_lo(0)
                split_lo(1)
                make_u(0)
                make_u(1)
                u_low(0)
                for n in range(2, 8):
                    split_lo(n)
                for j in range(NT):
                    if j + 1 < NT:
                        u_low(j + 1)
                    if j >= 1:
                        finish(j - 1)
                    if j + 2 < NT:
                        dve.wait_ge(r_in[j % 2], 16 * (j // 2 + 2))
                        make_u(j + 2)
                finish(NT - 1)

            @block.tensor
            def _(pe):
                def turn(j, src_t, ready, free, done):
                    pe.wait_ge(ready, j + 1)
                    for g in range(2):
                        for what, least in free(g):
                            pe.wait_ge(what, least)
                        for k in range(4):
                            c = 4 * g + k
                            ins = pe.transpose(psum[g][:, k * P:(k + 1) * P], src_t[:, j % 2, c * P:(c + 1) * P], ident[:])
                        ins.then_inc(done, 1)

                def turn_u(j):
                    turn(j, u, u_done, lambda g: ([(ulo_done, 2 * (j - 1) + g + 1)] if j >= 1 else [])
                         + ([(tx_evac, 2 * (j - 4) + g + 1)] if j >= 4 else []), tu_done)

                def turn_x(j, free):
                    turn(j, xn2, xn2_done, free, tx_done)

                def gate(j, c):
                    i = j % 2
                    pe.wait_ge(w_lo, 4 * (c + 1))
                    pe.wait_ge(ulo_done, 2 * (j + 1))
                    if j >= 2:
                        pe.wait_ge(zg_done, j - 1)
                    for k in range(KC):
                        at, cols = slice(k * P, (k + 1) * P), slice(c * BANK, (c + 1) * BANK)
                        bank = psum[2 + 2 * i + c]
                        pe.matmul(bank[:], uhi[:, i, at], wghi[:, k, cols], start=(k == 0), stop=False)
                        pe.matmul(bank[:], uhi[:, i, at], wglo[:, k, cols], start=False, stop=False)
                        ins = pe.matmul(bank[:], ulo[:, i, at], wghi[:, k, cols], start=False, stop=(k == KC - 1))
                    ins.then_inc(z_done, 1)

                def logits(j):
                    pe.wait_ge(tx_evac, 2 * (j + 1))
                    pe.wait_ge(gwt_evac, 1)
                    for k in range(KC):
                        ins = pe.matmul(LOGITS[:, j * X:(j + 1) * X], xn2t[:, k], gw_t[:, k],
                                        start=(k == 0), stop=(k == KC - 1))
                    ins.then_inc(lg_done, 1)

                turn_u(0)
                pe.wait_ge(small_in, 16)
                for k in range(KC):
                    ins = pe.transpose(psum[7][:, k * X:(k + 1) * X], gw_rows[0:X, k * P:(k + 1) * P], ident[0:X, 0:X])
                ins.then_inc(gwt_done, 1)
                for j in range(NT):
                    if j + 1 < NT:
                        turn_u(j + 1)
                    gate(j, 0)
                    if j >= 2:
                        turn_x(j - 2, lambda g: [(ulo_done, 2 * min(j + 1, NT - 1) + g + 1)])
                    gate(j, 1)
                    if j >= 2:
                        logits(j - 2)
                for j in (NT - 2, NT - 1):
                    turn_x(j, lambda g: [(tx_evac, 2 * (j - 1) + g + 1)])
                    logits(j)

        z5 = Zone(OFF_T, LIMIT - OFF_T)
        C2 = 2 * NT
        lg = z5.put("lg", [P, NT, X], F32)
        pr = z5.put("pr", [P, NT, X], F32)
        top = z5.put("top", [P, NT, 8], F32)
        top_i = z5.put("top_i", [P, NT, 8], U32)
        red = z5.put("red", [P, 3, NT], F32)
        sel_f = z5.put("sel_f", [P, NT, 2], F32)
        past = z5.put("past", [P, 2], F32)
        oh_e = z5.put("oh_e", [P, X, C2], BF16)
        bef = z5.put("bef", [P, X, C2], F32)
        wit = z5.put("wit", [P, X, C2], F32)
        ce = z5.put("ce", [P, 4, X], F32)
        ce_i = z5.put("ce_i", [P, 2, X], I32)
        ones_e = z5.put("ones_e", [P, C2], F32)
        pos = z5.put("pos", [P, C2], F32)
        pos_i = z5.put("pos_i", [P, 3, C2], I32)
        place_i = z5.put("place_i", [P, C2], I32)
        p_lo = z5.put("p_lo", [P, C2], F32)
        p_hi = z5.put("p_hi", [P, C2], F32)
        tok_f = z5.put("tok_f", [P, NT], F32)
        poh_lo = z5.put("poh_lo", [P, C2, P], F32R)
        poh_hi = z5.put("poh_hi", [P, C2, MTE], F32R)
        tok_s = z5.put("tok_s", [P, MTE], F32)
        tok_i = z5.put("tok_i", [P, MTE], I32)
        te = z5.put("te", [P, 2, MTE], F32)
        tile_expert = z5.put("tile_expert", [P, MTE], I32)
        tile_slot = z5.put("tile_slot", [P, MTE], I32)
        first_tile = z5.put("first_tile", [P, X], I32)
        rt_lg, rt_exp, rt_oh, rt_tot, rt_rank, rt_poh, rt_tok, rt_idx, rt_ready = (
            sem("shifted_logits_ready"), sem("exp_done"), sem("expert_onehot_ready"), sem("expert_totals_done"),
            sem("expert_ranks_done"), sem("token_onehots_ready"), sem("tokens_placed"), sem("token_index_ready"),
            sem("tile_expert_ready"))
        rt_iota = sem("token_numbers_ready")

        w13hi = [z5.put(f"w13hi{i}", [P, KC, 2 * H], F32R) for i in range(2)]
        w13lo = [z5.put(f"w13lo{i}", [P, KC, 2 * H], F32R) for i in range(2)]
        w2hi = [z5.put(f"w2hi{i}", [P, HC, D], F32R) for i in range(2)]
        w2lo = [z5.put(f"w2lo{i}", [P, HC, D], F32R) for i in range(2)]
        raw13 = z5.put("raw13", [P, 2, KC, 2 * H], F32)
        raw2 = z5.put("raw2", [P, 2, HC, D], F32)
        xg = z5.put("xg", [P, 2, D], F32)
        xthi = z5.put("xthi", [P, 2, D], F32R)
        xtlo = z5.put("xtlo", [P, 2, D], F32R)
        tanh_h = z5.put("tanh_h", [P, H], F32)
        act_a = z5.put("act_a", [P, H], F32)
        act_g = z5.put("act_g", [P, 2, H], F32)
        gthi = z5.put("gthi", [P, 2, H], F32R)
        gtlo = z5.put("gtlo", [P, 2, H], F32R)
        ye = z5.put("ye", [P, 2, D], F32)
        raw_in = [sem(f"expert_loaded{i}") for i in range(2)]
        experts_here, tiles_split = sem("experts_here"), sem("tiles_split")
        ab_hi = [sem(f"w13_hi_written{c}") for c in range(2)]
        ab_lo = [sem(f"w13_lo_written{c}") for c in range(2)]
        c_hi, c_lo = sem("w2_hi_written"), sem("w2_lo_written")
        xg_in = [sem(f"tokens_gathered{i}") for i in range(2)]
        xt_done, xt_hi, xt_lo = sem("xt_done"), sem("xt_hi"), sem("xt_lo")
        h_done, ht_done, a_done, g_done = sem("h_done"), sem("h_tanh_done"), sem("h_silu_done"), sem("g_done")
        gt_done, gt_hi, gt_lo = sem("gt_done"), sem("gt_hi"), sem("gt_lo")
        ye_done, ye_evac, ye_out = sem("ye_done"), sem("ye_evacuated"), [sem(f"ye_stored{i}") for i in range(2)]
        assert (MT - 3) % 2 == 0 and HC == 2 and 2 * H == BANK

        with nc.Block() as block:
            @block.sync
            def _(sp):
                sp.sem_inc(tiles_split, 1)
                for e in range(X):
                    i = e % 2
                    if e == 2:
                        sp.wait_ge(raw_in[0], 48)
                        sp.sem_inc(experts_here, 1)
                        sp.wait_ge(rt_ready, 1)
                    if e >= 2:
                        sp.wait_ge(raw_in[1 - i], 48 * ((e - 1) // 2 + 1))
                        sp.sem_inc(experts_here, 1)
                        used = sp.value_load(first_tile[0:1, e - 1:e], min_val=0, max_val=MT)
                        sp.wait_ge(tiles_split, used + 1)
                    for n, w in enumerate((w1, w3)):
                        sp.dma_start(raw13[:, i, :, n * H:(n + 1) * H],
                                     w[e].rearrange("(k p) n -> p k n", p=P)).then_inc(raw_in[i], 16)
                    sp.dma_start(raw2[:, i], w2[e].rearrange("(k p) n -> p k n", p=P)).then_inc(raw_in[i], 16)
                sp.wait_ge(raw_in[(X - 1) % 2], 48 * ((X - 1) // 2 + 1))
                sp.sem_inc(experts_here, 1)

            @block.gpsimd
            def _(pool):
                nc.gpsimd.iota(tok_f[:], pattern=[[P, NT]], base=1, channel_multiplier=1,
                               allow_small_or_imprecise_dtypes=True).then_inc(rt_iota, 1)
                pool.wait_ge(rt_idx, 1)

                def gather(i):
                    if i >= 2:
                        pool.wait_ge(xt_done, 2 * (i - 1))
                    nc.gpsimd.indirect_dma_start(
                        out=xg[:, i % 2], out_offset=None, in_=XN2,
                        in_offset=bass.IndirectOffsetOnAxis(ap=tok_i[:, i:i + 1], axis=0)).then_inc(xg_in[i % 2], 16)

                gather(0)
                gather(1)
                for i in range(MT):
                    slot = pool.value_load(tile_slot[0:1, i:i + 1], min_val=0, max_val=1)
                    pool.wait_ge(c_hi, i + 1)
                    nc.gpsimd.tensor_tensor(w2lo[i % 2][:], raw2[:, bass.ds(slot, 1)].rearrange("p a k n -> p (a k) n"),
                                            w2hi[i % 2][:].bitcast(F32), ALU.subtract).then_inc(c_lo, 1)
                    if i + 2 < MT:
                        gather(i + 2)
                    pool.wait_ge(c_lo, i + 1)
                    for c in range(2):
                        pool.wait_ge(ab_lo[c], i + 1)
                    pool.sem_inc(tiles_split, 1)

            @block.scalar
            def _(act):
                a = nc.scalar
                act.wait_ge(rt_lg, 1)
                a.activation(pr[:], lg[:], ACT.Exp).then_inc(rt_exp, 1)

                def slot_of(i):
                    return act.value_load(tile_slot[0:1, bass.ds(i, 1)], min_val=0, max_val=1)

                def expert_of(i):
                    return act.value_load(tile_expert[0:1, bass.ds(i, 1)], min_val=0, max_val=X - 1)

                def hi_ab(i, s, c, slot, expert, first=False):
                    if c == 0:
                        act.wait_ge(experts_here, expert + 1)
                        if not first:
                            act.wait_ge(h_done, i - 1)
                    a.activation(w13hi[s][:, 4 * c:4 * c + 4, :],
                                 raw13[:, bass.ds(slot, 1), 4 * c:4 * c + 4, :].rearrange("p a k n -> p (a k) n"),
                                 ACT.Copy).then_inc(ab_hi[c], 1)

                def hi_c(i, s, slot, first=False):
                    if not first:
                        act.wait_ge(ye_done, 2 * (i - 1))
                    a.activation(w2hi[s][:], raw2[:, bass.ds(slot, 1)].rearrange("p a k n -> p (a k) n"),
                                 ACT.Copy).then_inc(c_hi, 1)

                def hi_x(i, s, first=False):
                    for g in range(2):
                        act.wait_ge(xt_done, 2 * i + g + 1)
                        if not first:
                            act.wait_ge(h_done, i - 1)
                        a.activation(xthi[:, s, g * BANK:(g + 1) * BANK], psum[2 + g][:], ACT.Copy).then_inc(xt_hi, 1)

                def tanh(i, s, first=False):
                    act.wait_ge(h_done, i + 1)
                    if not first:
                        act.wait_ge(a_done, i)
                    a.activation(tanh_h[:], psum[s][:, 0:H], ACT.Tanh, scale=0.5).then_inc(ht_done, 1)

                def hi_g(i, s, first=False):
                    act.wait_ge(gt_done, i + 1)
                    if not first:
                        act.wait_ge(ye_done, 2 * (i - 1))
                    a.activation(gthi[:, s], psum[4][:, 0:H], ACT.Copy).then_inc(gt_hi, 1)

                def evacuate(i, s, first=False):
                    for c in range(2):
                        act.wait_ge(ye_done, 2 * i + c + 1)
                        if not first:
                            act.wait_ge(ye_out[s], 16 * ((i - s) // 2 if isinstance(i, int) else i_half[s]))
                        a.activation(ye[:, s, c * BANK:(c + 1) * BANK], psum[5 + c][:], ACT.Copy).then_inc(ye_evac, 1)

                def store(i, s):
                    act.wait_ge(ye_evac, 2 * (i + 1))
                    act.dma_start(YS[bass.ds(i * P, P), :], ye[:, s]).then_inc(ye_out[s], 16)

                i_half = [0, 0]
                act.wait_ge(rt_ready, 1)
                slot, expert = slot_of(0), expert_of(0)
                for c in range(2):
                    hi_ab(0, 0, c, slot, expert, True)
                hi_x(0, 0, True)
                tanh(0, 0, True)
                hi_c(0, 0, slot, True)
                slot, expert = slot_of(1), expert_of(1)
                for c in range(2):
                    hi_ab(1, 1, c, slot, expert, True)
                hi_x(1, 1, True)

                def step5(i, s, two=True, one=True, n=None):
                    if one:
                        slot_c = slot_of(i + 1)
                    if two:
                        slot, expert = slot_of(i + 2), expert_of(i + 2)
                    if n != 0:
                        evacuate(i - 1, 1 - s, n in (1, 2))
                        store(i - 1, 1 - s)
                    if one:
                        hi_c(i + 1, 1 - s, slot_c, n == 0)
                    if two:
                        hi_ab(i + 2, s, 0, slot, expert)
                    hi_g(i, s, n in (0, 1))
                    if two:
                        hi_ab(i + 2, s, 1, slot, expert)
                        hi_x(i + 2, s)
                    if one:
                        tanh(i + 1, 1 - s)
                for n in range(3):
                    step5(n, n % 2, n=n)
                with act.Fori(1, (MT - 3) // 2) as n:
                    i_half[1], i_half[0] = n, n
                    step5(2 * n + 1, 1)
                    step5(2 * n + 2, 0)
                step5(MT - 2, 1, two=False)
                step5(MT - 1, 0, two=False, one=False)
                evacuate(MT - 1, 0)
                store(MT - 1, 0)
                act.wait_ge(ye_out[0], 16 * ((MT + 1) // 2))
                act.wait_ge(ye_out[1], 16 * (MT // 2))

            @block.vector
            def _(dve):
                v = nc.vector
                step = chain(dve, "stage5_step")

                def flat(t):
                    return t.rearrange("p a b -> p (a b)")
                step(v.tensor_reduce(red[:, 0, :], LOGITS[:, 0:NT * X].rearrange("p (j e) -> p j e", e=X), AX.X, ALU.max))
                v.tensor_tensor(lg[:], LOGITS[:, 0:NT * X].rearrange("p (j e) -> p j e", e=X),
                                red[:, 0, :].unsqueeze(2).to_broadcast([P, NT, X]), ALU.subtract).then_inc(rt_lg, 1)
                dve.wait_ge(rt_exp, 1)
                step(v.tensor_reduce(red[:, 1, :], pr[:], AX.X, ALU.add))
                step(v.reciprocal(red[:, 2, :], red[:, 1, :]))
                step(v.tensor_tensor(pr[:], pr[:], red[:, 2, :].unsqueeze(2).to_broadcast([P, NT, X]), ALU.mult))
                for j in range(NT):
                    ins = v.max(top[:, j, :], pr[:, j, :])
                step(ins)
                for j in range(NT):
                    ins = v.max_index(top_i[:, j, :], top[:, j, :], pr[:, j, :])
                step(ins)
                step(v.tensor_copy(sel_f[:], top_i[:, :, 0:2]))
                step(v.tensor_scalar(past[:, 0:1], lanes[:], float(LASTP), float(X), ALU.is_ge, ALU.mult))
                step(v.tensor_scalar(sel_f[:, NT - 1, :], sel_f[:, NT - 1, :], past[:, 0:1], None, ALU.add))
                for e in range(X):
                    ins = v.tensor_scalar(oh_e[:, e, :], flat(sel_f[:]), float(e), None, ALU.is_equal)
                ins.then_inc(rt_oh, 1)
                step(v.memset(ones_e[:], 1.0))
                dve.wait_ge(rt_tot, 1)
                TOT = psum[4][:, 0:X * C2].rearrange("p (e c) -> p e c", e=X)
                for e in range(X):
                    ins = v.tensor_tensor_scan(bef[:, e, :], ones_e[:], TOT[:, e, :], 0.0, ALU.mult, ALU.add)
                step(ins)
                step(v.tensor_copy(ce[:, 0, :], bef[:, :, C2 - 1]))
                step(v.tensor_tensor(bef[:], bef[:], TOT, ALU.subtract))
                step(v.tensor_scalar(ce_i[:, 0, :], ce[:, 0, :], float(P - 1), None, ALU.add))
                step(v.tensor_scalar(ce_i[:, 1, :], ce_i[:, 0, :], 7, 7, ALU.arith_shift_right, ALU.logical_shift_left))
                step(v.tensor_copy(ce[:, 1, :], ce_i[:, 1, :]))
                step(v.tensor_tensor_scan(ce[:, 2, :], ones_e[:, 0:X], ce[:, 1, :], 0.0, ALU.mult, ALU.add))
                step(v.tensor_tensor(ce[:, 3, :], ce[:, 2, :], ce[:, 1, :], ALU.subtract))
                step(v.tensor_scalar(te[:, 0, :], iota[:, 0:MTE], float(P), None, ALU.mult))
                step(v.memset(te[:, 1, :], 0.0))
                for e in range(1, X):
                    step(v.scalar_tensor_tensor(te[:, 1, :], te[:, 0, :], ce[:, 3, e:e + 1], te[:, 1, :],
                                                ALU.is_ge, ALU.add))
                step(v.tensor_copy(tile_expert[:], te[:, 1, :]))
                step(v.tensor_scalar(tile_slot[:], tile_expert[:], 1, None, ALU.bitwise_and))
                v.tensor_scalar(first_tile[:], ce[:, 3, :], 1.0 / P, None, ALU.mult).then_inc(rt_ready, 1)
                dve.wait_ge(rt_rank, 1)
                step(v.tensor_tensor(wit[:], bef[:], psum[5][:, 0:X * C2].rearrange("p (e c) -> p e c", e=X), ALU.add))
                step(v.tensor_tensor(wit[:], wit[:], ce[:, 3, :].unsqueeze(2).to_broadcast([P, X, C2]), ALU.add))
                step(v.tensor_tensor(wit[:], wit[:], oh_e[:], ALU.mult))
                step(v.tensor_reduce(pos[:], wit[:].rearrange("p e c -> p c e"), AX.X, ALU.add))
                step(v.tensor_copy(place_i[:], pos[:]))
                step(v.tensor_scalar(past[:, 1:2], past[:, 0:1], float(P * 256 // X), None, ALU.mult))
                step(v.tensor_scalar(pos[:, C2 - 2:C2], pos[:, C2 - 2:C2], past[:, 1:2], None, ALU.add))
                step(v.tensor_copy(pos_i[:, 0, :], pos[:]))
                step(v.tensor_scalar(pos_i[:, 1, :], pos_i[:, 0, :], P - 1, None, ALU.bitwise_and))
                step(v.tensor_scalar(pos_i[:, 2, :], pos_i[:, 0, :], 7, None, ALU.arith_shift_right))
                step(v.tensor_copy(p_lo[:], pos_i[:, 1, :]))
                step(v.tensor_copy(p_hi[:], pos_i[:, 2, :]))
                dve.wait_ge(rt_iota, 1)
                for c in range(C2):
                    v.tensor_scalar(poh_lo[:, c], iota[:, 0:P], p_lo[:, c:c + 1], None, ALU.is_equal)
                    ins = v.tensor_scalar(poh_hi[:, c], iota[:, 0:MTE], p_hi[:, c:c + 1], tok_f[:, c // 2:c // 2 + 1],
                                          ALU.is_equal, ALU.mult)
                ins.then_inc(rt_poh, 1)
                dve.wait_ge(rt_tok, 1)
                step(v.tensor_scalar(tok_s[:], psum[7][:, 0:MTE], -1.0, 0.0, ALU.add, ALU.max))
                v.tensor_copy(tok_i[:], tok_s[:]).then_inc(rt_idx, 1)

                def slot_of(i):
                    return dve.value_load(tile_slot[0:1, bass.ds(i, 1)], min_val=0, max_val=1)

                def lo_ab(i, s, c, slot):
                    dve.wait_ge(ab_hi[c], i + 1)
                    v.tensor_tensor(w13lo[s][:, 4 * c:4 * c + 4, :],
                                    raw13[:, bass.ds(slot, 1), 4 * c:4 * c + 4, :].rearrange("p a k n -> p (a k) n"),
                                    w13hi[s][:, 4 * c:4 * c + 4, :].bitcast(F32), ALU.subtract).then_inc(ab_lo[c], 1)

                def lo_x(i, s):
                    for g in range(2):
                        dve.wait_ge(xt_hi, 2 * i + g + 1)
                        at = (slice(None), s, slice(g * BANK, (g + 1) * BANK))
                        v.tensor_tensor(xtlo[at], psum[2 + g][:], xthi[at].bitcast(F32), ALU.subtract).then_inc(xt_lo, 1)

                def silu(i, s, first=False):
                    dve.wait_ge(ht_done, i + 1)
                    v.scalar_tensor_tensor(act_a[:], tanh_h[:], 1.0, psum[s][:, 0:H], ALU.add, ALU.mult).then_inc(a_done, 1)
                    dve.wait_ge(a_done, i + 1)
                    if not first:
                        dve.wait_ge(gt_done, i - 1)
                    v.scalar_tensor_tensor(act_g[:, s], act_a[:], 0.5, psum[s][:, H:2 * H],
                                           ALU.mult, ALU.mult).then_inc(g_done, 1)

                def lo_g(i, s):
                    dve.wait_ge(gt_hi, i + 1)
                    v.tensor_tensor(gtlo[:, s], psum[4][:, 0:H], gthi[:, s].bitcast(F32), ALU.subtract).then_inc(gt_lo, 1)

                dve.wait_ge(rt_ready, 1)
                slot = slot_of(0)
                for c in range(2):
                    lo_ab(0, 0, c, slot)
                lo_x(0, 0)
                silu(0, 0, True)
                slot = slot_of(1)
                for c in range(2):
                    lo_ab(1, 1, c, slot)
                lo_x(1, 1)

                def step5(i, s, two=True, one=True, first=False):
                    if two:
                        slot = slot_of(i + 2)
                        lo_ab(i + 2, s, 0, slot)
                    lo_g(i, s)
                    if two:
                        lo_ab(i + 2, s, 1, slot)
                        lo_x(i + 2, s)
                    if one:
                        silu(i + 1, 1 - s, first)
                step5(0, 0, first=True)
                with dve.Fori(0, (MT - 3) // 2) as n:
                    step5(2 * n + 1, 1)
                    step5(2 * n + 2, 0)
                step5(MT - 2, 1, two=False)
                step5(MT - 1, 0, two=False, one=False)

            @block.tensor
            def _(pe):
                pe.wait_ge(rt_oh, 1)
                pe.matmul(psum[4][:, 0:X * C2], ones[:], oh_e[:].rearrange("p e c -> p (e c)"),
                          start=True, stop=True).then_inc(rt_tot, 1)
                pe.matmul(psum[5][:, 0:X * C2], tri[:], oh_e[:].rearrange("p e c -> p (e c)"),
                          start=True, stop=True).then_inc(rt_rank, 1)
                pe.wait_ge(rt_poh, 1)
                for c in range(C2):
                    ins = pe.matmul(psum[7][:, 0:MTE], poh_lo[:, c], poh_hi[:, c], start=(c == 0), stop=(c == C2 - 1))
                ins.then_inc(rt_tok, 1)

                def turn_x(i, s, first=False):
                    pe.wait_ge(xg_in[s], 16 * (i // 2 + 1 if isinstance(i, int) else half_of[s] + 1))
                    for g in range(2):
                        if not first:
                            pe.wait_ge(xt_lo, 2 * (i - 1) + g + 1)
                        for k in range(4):
                            c = 4 * g + k
                            ins = pe.transpose(psum[2 + g][:, k * P:(k + 1) * P], xg[:, s, c * P:(c + 1) * P], ident[:])
                        ins.then_inc(xt_done, 1)

                def hidden(i, s, c, first=False):
                    pe.wait_ge(ab_lo[c], i + 1)
                    pe.wait_ge(xt_lo, 2 * (i + 1))
                    if not first:
                        pe.wait_ge(g_done, i - 1)
                    for k in range(4 * c, 4 * c + 4):
                        at = slice(k * P, (k + 1) * P)
                        pe.matmul(psum[s][:], xthi[:, s, at], w13hi[s][:, k], start=(k == 0), stop=False)
                        pe.matmul(psum[s][:], xthi[:, s, at], w13lo[s][:, k], start=False, stop=False)
                        ins = pe.matmul(psum[s][:], xtlo[:, s, at], w13hi[s][:, k], start=False, stop=(k == KC - 1))
                    if c == 1:
                        ins.then_inc(h_done, 1)

                def turn_g(i, s, first=False):
                    pe.wait_ge(g_done, i + 1)
                    if not first:
                        pe.wait_ge(gt_lo, i)
                    for k in range(HC):
                        ins = pe.transpose(psum[4][:, k * P:(k + 1) * P], act_g[:, s, k * P:(k + 1) * P], ident[:])
                    ins.then_inc(gt_done, 1)

                def outputs(i, s, first=False):
                    pe.wait_ge(c_lo, i + 1)
                    pe.wait_ge(gt_lo, i + 1)
                    for c in range(2):
                        if not first:
                            pe.wait_ge(ye_evac, 2 * (i - 1) + c + 1)
                        for k in range(HC):
                            at, cols = slice(k * P, (k + 1) * P), slice(c * BANK, (c + 1) * BANK)
                            pe.matmul(psum[5 + c][:], gthi[:, s, at], w2hi[s][:, k, cols], start=(k == 0), stop=False)
                            pe.matmul(psum[5 + c][:], gthi[:, s, at], w2lo[s][:, k, cols], start=False, stop=False)
                            ins = pe.matmul(psum[5 + c][:], gtlo[:, s, at], w2hi[s][:, k, cols], start=False,
                                            stop=(k == HC - 1))
                        ins.then_inc(ye_done, 1)

                half_of = [0, 0]
                turn_x(0, 0, True)
                hidden(0, 0, 0, True)
                hidden(0, 0, 1, True)
                turn_x(1, 1)

                def step5(i, s, two=True, one=True, first=False):
                    if one:
                        hidden(i + 1, 1 - s, 0, first)
                    turn_g(i, s, first)
                    if one:
                        hidden(i + 1, 1 - s, 1, first)
                    if two:
                        turn_x(i + 2, s)
                    outputs(i, s, first)
                step5(0, 0, first=True)
                with pe.Fori(0, (MT - 3) // 2) as n:
                    half_of[1], half_of[0] = n + 1, n + 2
                    step5(2 * n + 1, 1)
                    step5(2 * n + 2, 0)
                step5(MT - 2, 1, two=False)
                step5(MT - 1, 0, two=False, one=False)

        z6 = Zone(z5.start + 64 * KB, 64 * KB)
        first_y = z6.put("first_y", [P, 3, D], F32)
        second_y = z6.put("second_y", [P, 3, D], F32)
        x1b = z6.put("x1b", [P, 3, D], F32)
        y1_in, y2_in, x1_in, res_out = ([sem(f"{n}{i}") for i in range(3)] for n in
                                        ("first_gathered", "second_gathered", "x1_loaded", "result_stored"))
        half_done, res_done = sem("first_added"), sem("result_done")
        with nc.Block() as block:
            @block.sync
            def _(sp):
                def load(j):
                    if j >= 3:
                        sp.wait_ge(res_out[j % 3], 16 * (j // 3))
                    sp.dma_start(x1b[:, j % 3], X1[j * P:(j + 1) * P, :]).then_inc(x1_in[j % 3], 16)
                for j in range(3):
                    load(j)
                for j in range(NT):
                    sp.wait_ge(res_done, j + 1)
                    sp.dma_start(out[j * P:j * P + rows(j), :], x1b[:rows(j), j % 3]).then_inc(res_out[j % 3], 16)
                    if j >= 1 and j + 2 < NT:
                        load(j + 2)
                for i in range(3):
                    sp.wait_ge(res_out[i], 16 * len(range(i, NT, 3)))

            @block.gpsimd
            def _(pool):
                for j in range(NT):
                    for k, (buf, got) in enumerate(((first_y, y1_in), (second_y, y2_in))):
                        if j >= 3:
                            pool.wait_ge(res_done, j - 2)
                        nc.gpsimd.indirect_dma_start(
                            out=buf[:, j % 3], out_offset=None, in_=YS,
                            in_offset=bass.IndirectOffsetOnAxis(ap=place_i[:, 2 * j + k:2 * j + k + 1], axis=0)
                        ).then_inc(got[j % 3], 16)

            @block.vector
            def _(dve):
                v = nc.vector
                for j in range(NT):
                    i = j % 3
                    dve.wait_ge(y1_in[i], 16 * (j // 3 + 1))
                    dve.wait_ge(x1_in[i], 16 * (j // 3 + 1))
                    v.scalar_tensor_tensor(x1b[:, i], first_y[:, i], top[:, j, 0:1], x1b[:, i],
                                           ALU.mult, ALU.add).then_inc(half_done, 1)
                    dve.wait_ge(half_done, j + 1)
                    dve.wait_ge(y2_in[i], 16 * (j // 3 + 1))
                    v.scalar_tensor_tensor(x1b[:, i], second_y[:, i], top[:, j, 1:2], x1b[:, i],
                                           ALU.mult, ALU.add).then_inc(res_done, 1)


_INS = ["x", "src", "dst", "edge_type_8", "L0_gnn_weight", "L0_gnn_root", "L0_gnn_bias", "L0_gnn_w_gate",
        "L0_gnn_b_gate", "L0_ffn_gate_w", "L0_ffn_w1", "L0_ffn_w2", "L0_ffn_w3"]


def kernel(**inputs):
    import numpy as _np
    import concourse.bacc as _bacc
    from concourse import mybir as _mybir
    from concourse.bass_utils import run_bass_kernel_spmd as _run

    nc = _bacc.Bacc("TRN2", target_bir_lowering=False, num_devices=1)
    arrays, args = {}, []
    for name in _INS:
        a = _np.ascontiguousarray(inputs[name])
        arrays[f"in_{name}"] = a
        args.append(nc.dram_tensor(f"in_{name}", a.shape, _mybir.dt.from_np(a.dtype), kind="ExternalInput").ap())
    result = nc.dram_tensor("result", inputs["x"].shape, _mybir.dt.float32, kind="ExternalOutput").ap()
    build_program(nc, *args, result)
    r = _run(nc, [arrays], core_ids=[0])
    return r.results[0]["result"]
```

```python
import numpy as np
import concourse.bass as bass
from concourse import mybir
from contextlib import ExitStack

F32 = mybir.dt.float32
F32R = mybir.dt.float32r
BF16 = mybir.dt.bfloat16
I32 = mybir.dt.int32
U32 = mybir.dt.uint32
ALU = mybir.AluOpType
ACT = mybir.ActivationFunctionType
AX = mybir.AxisListType

P = 128
BANK = 512
EPS = 1e-5
GROUP = 2


def shapes(x, src, weight, w1, gate_w):
    s = {}
    s["N"], s["D"] = x.shape
    s["E"] = src.shape[0]
    s["R"] = weight.shape[0]
    s["X"], _, s["H"] = w1.shape
    s["NT"] = -(-s["N"] // P)
    s["NP"] = s["NT"] * P
    s["KC"] = s["D"] // P
    s["HC"] = s["H"] // P
    s["EFULL"] = s["E"] // P
    s["EREST"] = s["E"] - s["EFULL"] * P
    s["ECOLS"] = 168
    pad = GROUP * P
    pairs = (s["E"] + s["NT"] * (pad - 1)) // pad
    s["PAIRS"] = 4 * (-(-pairs // 8) * 2)
    s["ET"] = s["PAIRS"] * GROUP
    s["MT"] = (2 * s["N"] + s["X"] * (P - 1)) // P
    s["MTE"] = s["MT"] + s["MT"] % 2
    return s


def build_program(nc, x, src, dst, edge_type, weight, root, bias, w_gate, b_gate,
                  gate_w, w1, w2, w3, out):
    s = shapes(x, src, weight, w1, gate_w)
    N, D, R, X, H, NT, NP, KC, HC = (s[k] for k in ("N", "D", "R", "X", "H", "NT", "NP", "KC", "HC"))
    E, EFULL, EREST, ECOLS, PAIRS, ET, MT, MTE = (
        s[k] for k in ("E", "EFULL", "EREST", "ECOLS", "PAIRS", "ET", "MT", "MTE"))
    LASTP = N - (NT - 1) * P
    HALF = D // 2
    assert ECOLS >= EFULL + (EREST > 0) and HALF == BANK and D == 1024 and R == 8 and X == 8
    KEYS = NP * R
    KHI = KEYS // 256

    with ExitStack() as ctx:
        psum = [ctx.enter_context(nc.psum_tensor(f"bank{i}", [P, BANK], F32)) for i in range(8)]

        def sem(name):
            return ctx.enter_context(nc.semaphore(name))

        size = {F32: 4, F32R: 4, BF16: 2, I32: 4, U32: 4}

        class Zone:
            def __init__(self, start, length):
                self.at, self.end, self.start = start, start + length, start

            def put(self, name, shape, dt):
                n = size[dt] * int(np.prod(shape[1:]))
                n = -(-n // 32) * 32
                assert self.at + n <= self.end, (name, self.at + n - self.end)
                t = nc.alloc_sbuf_tensor_at(name, shape, dt, offset=self.at)
                self.at += n
                return t

        KB = 1024
        base = -(-nc.sbuf_base // 32) * 32
        LIMIT = nc.sbuf_base + nc.sbuf_bytes_remaining
        keep = Zone(base, 13 * KB // 2)
        OFF_T = base + 13 * KB // 2
        OFF_STAGE = OFF_T + 80 * KB
        OFF_YOUT = OFF_STAGE + 8 * KB
        OFF_W0 = OFF_YOUT + 8 * KB
        OFF_W1 = OFF_W0 + 32 * KB
        OFF_END = OFF_W1 + 32 * KB

        ident = keep.put("ident", [P, P], F32)
        iota = keep.put("iota", [P, 257], F32)
        lanes = keep.put("lanes", [P, 1], F32)
        mean = keep.put("mean", [P, NT], F32)
        rstd = keep.put("rstd", [P, NT], F32)
        edge_row = keep.put("edge_row", [P, ET], I32)
        edge_dst = keep.put("edge_dst", [P, ET], F32)
        edge_key = keep.put("edge_key", [P, ET], I32)
        edge_w = keep.put("edge_w", [P, ET], F32)
        tile_block = keep.put("tile_block", [P, ET], I32)
        tri = keep.put("tri", [P, P], BF16)
        ones = keep.put("ones", [P, P], BF16)

        acc = nc.alloc_sbuf_tensor_at("acc", [P, NT * D], F32, offset=OFF_END)

        def dram(name, shape, dt=F32):
            return nc.dram_tensor(name, shape, dt, kind="Internal").ap()

        Y = dram("Y", (R * NP, D))
        YX = dram("YX", (2, NP, D))
        INV = dram("INV", (KEYS, 1))
        XN2 = dram("XN2", (NP, D))
        X1 = dram("X1", (NP, D))
        YS = dram("YS", (MT * P, D))

        def rows(j):
            return LASTP if j == NT - 1 else P

        def chain(eng, name):
            done, count = sem(name), [0]

            def step(ins):
                count[0] += 1
                ins.then_inc(done, 1)
                eng.wait_ge(done, count[0])
            return step

        xhi = nc.alloc_sbuf_tensor_at("xhi", [P, KC, NP], F32R, offset=OFF_T)
        xlo = nc.alloc_sbuf_tensor_at("xlo", [P, KC, NP], F32R, offset=OFF_T + 4 * KC * NP)
        z2 = Zone(OFF_END, LIMIT - OFF_END)
        place_lo = z2.put("place_lo", [P, ECOLS], F32)
        place_hi = z2.put("place_hi", [P, ECOLS], F32)
        val_src = z2.put("val_src", [P, ECOLS], F32)
        val_dst = z2.put("val_dst", [P, ECOLS], F32)
        key_hi = z2.put("key_hi", [P, ECOLS], F32)
        key_lo = z2.put("key_lo", [P, ECOLS], F32)
        blk_base = z2.put("blk_base", [P, NT], F32)
        z2t = Zone(z2.at, LIMIT - z2.at)
        onehot = z2t.put("onehot", [P, NT, ECOLS], BF16)
        before = z2t.put("before", [P, NT, ECOLS], F32)
        within = z2t.put("within", [P, 3 * ECOLS], F32)
        ones_f = z2t.put("ones_f", [P, ECOLS], F32)
        edge_tmp = z2t.put("edge_tmp", [P, ECOLS], I32)
        dlo = z2t.put("dlo", [P, ECOLS], F32)
        blk = z2t.put("blk", [P, ECOLS], F32)
        typ = z2t.put("typ", [P, ECOLS], F32)
        posf = z2t.put("posf", [P, ECOLS], F32)
        src_i = z2t.put("src_i", [P, ECOLS], I32)
        dst_i = z2t.put("dst_i", [P, ECOLS], I32)
        typ_i = z2t.put("typ_i", [P, ECOLS], I32)
        cnt_f = z2t.put("cnt_f", [P, 3, NT], F32)
        cnt_i = z2t.put("cnt_i", [P, 2, NT], I32)

        XA = 6
        x_first = nc.alloc_sbuf_tensor_at("x_first", [P, XA, D], F32, offset=OFF_W1)
        x_last = z2t.put("x_last", [P, NT - XA, D], F32)
        stat = z2t.put("stat", [P, NT, 2, 6], F32)
        aggr = z2t.put("aggr", [P, NT, 2], F32)
        tmp10 = z2t.put("tmp10", [P, 4, NT], F32)

        def x_tile(j):
            return x_first[:, j] if j < XA else x_last[:, j - XA]

        LN_GROUPS = ((0, 1), (1, 2), (2, 3), (3, 4), (4, 6), (6, 8), (8, NT))
        xin = [sem(f"x_loaded{j}") for j in range(NT)]
        edges_set, edges_in = sem("edges_set"), sem("edges_in")
        consts = sem("consts_ready")
        onehot_ready, totals_done, totals_read, tri_done, tri_read = (
            sem("block_onehot_ready"), sem("column_totals_done"), sem("column_totals_read"),
            sem("ranks_done"), sem("ranks_read"))
        pad_set = sem("pad_rows_set")
        norm_ready, tr_done, hi_done, lo_done = (
            sem("norm_ready"), sem("transposed"), sem("xhi_written"), sem("xlo_written"))
        var_ready, sqrt_ready = sem("var_ready"), sem("sqrt_ready")

        groups = [list(range(a, min(a + 3, NT))) for a in range(0, NT, 3)]
        stage = nc.alloc_sbuf_tensor_at("w_stage", [P, 2, 2, HALF], F32, offset=OFF_STAGE)
        w_early = nc.alloc_sbuf_tensor_at("w_early", [P, 2, 2, HALF], F32, offset=OFF_YOUT)
        yout = nc.alloc_sbuf_tensor_at("y_out", [P, 4, HALF], F32, offset=OFF_YOUT)
        whi = [nc.alloc_sbuf_tensor_at(f"whi{h}", [P, KC, HALF], F32R, offset=o)
               for h, o in enumerate((OFF_W0, OFF_W1))]
        wlo = [nc.alloc_sbuf_tensor_at(f"wlo{h}", [P, KC, HALF], F32R, offset=o + 16 * KB)
               for h, o in enumerate((OFF_W0, OFF_W1))]
        z2b = Zone(z2.at, LIMIT - z2.at)
        CPQ = 7
        SORT_R = ECOLS // (8 * CPQ)
        assert SORT_R * 8 * CPQ == ECOLS
        oh_lo = z2b.put("oh_lo", [P, CPQ, P], F32R)
        oh_val = z2b.put("oh_val", [P, CPQ, 2, ET], F32R)
        oh_khi = z2b.put("oh_khi", [P, CPQ, KHI], BF16)
        oh_klo = z2b.put("oh_klo", [P, CPQ, 256], BF16)
        placed = z2b.put("placed", [P, 2, ET], F32)
        placed_i = z2b.put("placed_i", [P, 3, ET], I32)
        tfl = z2b.put("tfl", [P, 4, ET], F32)
        inv = z2b.put("inv", [KHI, 256], F32)
        YB, PLACE_BANK, COUNT_BANK = 4, psum[6], psum[7]

        w_in = [sem(f"w_stage_loaded{i}") for i in range(2)]
        early_in = [sem(f"w_early_loaded{i}") for i in range(2)]

        def staged(r, h, q):
            if isinstance(r, int) and (r, h) == (0, 0):
                return (stage[:, q], w_in[q], 16) if q < 2 else (w_early[:, q - 2], early_in[q - 2], 16)
            return stage[:, q % 2], w_in[q % 2], 16 * (r * 4 + h * 2 + q // 2)
        w_hi, w_lo = sem("w_hi_written"), sem("w_lo_written")
        y_ready, y_evac = sem("y_ready"), sem("y_evacuated")
        y_out = [sem(f"y_stored{i}") for i in range(YB)]
        cols_ready, cols_used = sem("onehots_ready"), sem("onehots_used")
        inv_ready, inv_out, key_ready, w_gathered = (
            sem("inv_ready"), sem("inv_stored"), sem("keys_ready"), sem("edge_w_gathered"))

        RANK_AFTER = ((0, NT - 1), (1, 3))
        FIRST_SPLITS, FIRST_LOADS = (3, 5, 7, 8), (4, 6, 8, 9)

        def w_rows(w, q, h):
            return w[2 * q * P:(2 * q + 2) * P, h * HALF:(h + 1) * HALF].rearrange("(k p) n -> p k n", p=P)

        with nc.Block() as block:
            @block.sync
            def _(sp):
                def load(r, h, q, first=False):
                    n = r * 8 + h * 4 + q
                    if not first:
                        sp.wait_ge(w_lo, n - 1)
                    w = (weight[bass.ds(r, 1)].rearrange("a k n -> (a k) n") if not isinstance(r, int)
                         else root if r == R else weight[r])
                    place, arrived, _ = staged(r, h, q)
                    sp.dma_start(place, w_rows(w, q, h)).then_inc(arrived, 16)

                def store(r, h, j):
                    m = r * 2 * NT + h * NT + j
                    sp.wait_ge(y_evac, m + 1)
                    sp.dma_start(Y[bass.ds(r * NP + j * P, P), h * HALF:(h + 1) * HALF],
                                 yout[:, (h * NT + j) % YB]).then_inc(y_out[(h * NT + j) % YB], 16)

                def load_x(*tiles):
                    for j in tiles:
                        if j == NT - 1:
                            sp.wait_ge(pad_set, 1)
                        sp.dma_start(x_tile(j)[:rows(j)], x[j * P:j * P + rows(j), :]).then_inc(xin[j], 16)

                load_x(0)
                load(0, 0, 0, True)
                load_x(1)
                load(0, 0, 1, True)
                load(0, 0, 2, True)
                load(0, 0, 3, True)
                load_x(*range(2, NT))
                for q in (0, 1):
                    load(0, 1, q)

                def relation(r, first=False, last=False):
                    for h in range(2):
                        after = FIRST_LOADS if first and h == 0 else (0, 2, 4, 6)
                        for j in range(NT):
                            store(r, h, j)
                            if j in after:
                                q = after.index(j) + 2
                                r2, h2 = (r, h + 1) if q < 4 else (r, h + 2)
                                if h2 >= 2:
                                    r2, h2 = r2 + 1, h2 - 2
                                if last and h2 == 1 and h == 1:
                                    continue
                                load(r2, h2, q % 4)
                relation(0, first=True)
                with sp.Fori(1, R - 1) as r:
                    relation(r)
                relation(R - 1, last=True)
                for i in range(YB):
                    sp.wait_ge(y_out[i], 16 * (R * 2 * NT // YB))

            @block.scalar
            def _(act):
                def split_hi(r, h, q, first=False):
                    n = r * 8 + h * 4 + q
                    place, arrived, count = staged(r, h, q)
                    act.wait_ge(arrived, count)
                    if not first and q == 0:
                        act.wait_ge(y_ready, (r * 2 + h - 1) * NT)
                    nc.scalar.activation(whi[h][:, 2 * q:2 * q + 2, :], place, ACT.Copy).then_inc(w_hi, 1)

                def evacuate(r, h, j, first=False):
                    m = r * 2 * NT + h * NT + j
                    slot = (h * NT + j) % YB
                    act.wait_ge(y_ready, m + 1)
                    if not (first and h * NT + j < YB):
                        act.wait_ge(y_out[slot], 16 * (r * (2 * NT // YB) + (h * NT + j) // YB))
                    nc.scalar.activation(yout[:, slot], psum[slot][:], ACT.Copy).then_inc(y_evac, 1)

                def root_of(g):
                    a, b = LN_GROUPS[g]
                    act.wait_ge(var_ready, g + 1)
                    nc.scalar.activation(tmp10[:, 1, a:b], tmp10[:, 0, a:b], ACT.Sqrt).then_inc(sqrt_ready, 1)

                def x_hi(j):
                    for n in (2 * j, 2 * j + 1):
                        g = n % 2
                        act.wait_ge(tr_done, n + 1)
                        nc.scalar.activation(xhi[:, 4 * g:4 * g + 4, j * P:(j + 1) * P],
                                             psum[4 + n % 4][:].rearrange("p (k n) -> p k n", k=4),
                                             ACT.Copy).then_inc(hi_done, 1)

                root_of(0)
                split_hi(0, 0, 0, True)
                root_of(1)
                split_hi(0, 0, 1, True)
                x_hi(0)
                split_hi(0, 0, 2, True)
                split_hi(0, 0, 3, True)
                x_hi(1)
                root_of(2)
                root_of(3)

                def relation(r, first=False):
                    for h in range(2):
                        beside_x = first and h == 0
                        after = FIRST_SPLITS if beside_x else (0, 2, 4, 6)
                        for j in range(NT):
                            evacuate(r, h, j, first)
                            if beside_x and j + 2 < NT:
                                x_hi(j + 2)
                            if beside_x and j + 4 < len(LN_GROUPS):
                                root_of(j + 4)
                            if j in after:
                                split_hi(*((r, 1) if h == 0 else (r + 1, 0)), after.index(j), first and h == 0)
                relation(0, first=True)
                with act.Fori(1, R - 1) as r:
                    relation(r)
                relation(R - 1)

            @block.vector
            def _(dve):
                v = nc.vector

                def split_lo(r, h, q):
                    dve.wait_ge(w_hi, r * 8 + h * 4 + q + 1)
                    v.tensor_tensor(wlo[h][:, 2 * q:2 * q + 2, :], staged(r, h, q)[0],
                                    whi[h][:, 2 * q:2 * q + 2, :].bitcast(F32), ALU.subtract).then_inc(w_lo, 1)

                def columns(r, part, first=False):
                    if not first:
                        dve.wait_ge(cols_used, (r - 1) * 8 + part)
                    for i in range(CPQ):
                        c = (r - 1) * 8 * CPQ + part * CPQ + i
                        at = bass.ds(c, 1)
                        v.tensor_scalar(oh_lo[:, i], iota[:, 0:P], place_lo[:, at], None, ALU.is_equal)
                        v.tensor_scalar(oh_val[:, i, 0], iota[:, 0:ET], place_hi[:, at], val_src[:, at],
                                        ALU.is_equal, ALU.mult)
                        v.tensor_scalar(oh_val[:, i, 1], iota[:, 0:ET], place_hi[:, at], val_dst[:, at],
                                        ALU.is_equal, ALU.mult)
                        v.tensor_scalar(oh_khi[:, i], iota[:, 0:KHI], key_hi[:, at], None, ALU.is_equal)
                        ins = v.tensor_scalar(oh_klo[:, i], iota[:, 0:256], key_lo[:, at], None, ALU.is_equal)
                    ins.then_inc(cols_ready, 1)

                def edge_places():
                    step = chain(dve, "places_step")
                    dve.wait_ge(edges_in, 16 * 6)
                    dve.wait_ge(consts, 5)
                    v.tensor_copy(val_src[:], src_i[:])
                    step(v.tensor_copy(typ[:], typ_i[:]))
                    step(v.tensor_scalar(edge_tmp[:], dst_i[:], 7, None, ALU.arith_shift_right))
                    step(v.tensor_copy(blk[:], edge_tmp[:]))
                    for j in range(NT):
                        ins = v.tensor_scalar(onehot[:, j, :], blk[:], float(j), None, ALU.is_equal)
                    ins.then_inc(onehot_ready, 1)
                    step(v.tensor_scalar(edge_tmp[:], dst_i[:], P - 1, None, ALU.bitwise_and))
                    step(v.tensor_copy(dlo[:], edge_tmp[:]))
                    step(v.tensor_scalar(dlo[:], dlo[:], 1.0, float(R), ALU.add, ALU.mult))
                    step(v.tensor_tensor(val_dst[:], dlo[:], typ[:], ALU.add))
                    step(v.tensor_scalar(edge_tmp[:], dst_i[:], 5, None, ALU.arith_shift_right))
                    step(v.tensor_copy(key_hi[:], edge_tmp[:]))
                    step(v.tensor_scalar(edge_tmp[:], dst_i[:], 31, None, ALU.bitwise_and))
                    step(v.tensor_copy(dlo[:], edge_tmp[:]))
                    step(v.scalar_tensor_tensor(key_lo[:], dlo[:], float(R), typ[:], ALU.mult, ALU.add))
                    for g, js in enumerate(groups):
                        dve.wait_ge(totals_done, g + 1)
                        for n, j in enumerate(js):
                            step(v.tensor_tensor_scan(before[:, j, :], ones_f[:], psum[4 + g][:, n * ECOLS:(n + 1) * ECOLS],
                                                      0.0, ALU.mult, ALU.add))
                            step(v.tensor_copy(cnt_f[:, 0, j:j + 1], before[:, j, ECOLS - 1:ECOLS]))
                            ins = v.tensor_tensor(before[:, j, :], before[:, j, :],
                                                  psum[4 + g][:, n * ECOLS:(n + 1) * ECOLS], ALU.subtract)
                            step(ins)
                    shift = (GROUP * P).bit_length() - 1
                    step(v.tensor_scalar(cnt_i[:, 0, :], cnt_f[:, 0, :], float(GROUP * P - 1), None, ALU.add))
                    step(v.tensor_scalar(cnt_i[:, 1, :], cnt_i[:, 0, :], shift, shift,
                                         ALU.arith_shift_right, ALU.logical_shift_left))
                    step(v.tensor_copy(cnt_f[:, 1, :], cnt_i[:, 1, :]))
                    step(v.tensor_tensor_scan(cnt_f[:, 2, :], ones_f[:, 0:NT], cnt_f[:, 1, :], 0.0, ALU.mult, ALU.add))
                    step(v.tensor_tensor(blk_base[:], cnt_f[:, 2, :], cnt_f[:, 1, :], ALU.subtract))
                    v.tensor_copy(cnt_f[:, 0, :], cnt_f[:, 2, :]).then_inc(totals_read, 1)
                    step(v.tensor_scalar(posf[:], blk[:], 0.0, float(1 << 16), ALU.is_lt, ALU.mult))
                    for g, js in enumerate(groups):
                        dve.wait_ge(tri_done, g + 1)
                        w = len(js) * ECOLS
                        step(v.tensor_tensor(within[:, :w], psum[4 + g][:, :w],
                                             before[:, js[0]:js[-1] + 1, :].rearrange("p j c -> p (j c)"), ALU.add))
                        for n, j in enumerate(js):
                            cut = within[:, n * ECOLS:(n + 1) * ECOLS]
                            step(v.scalar_tensor_tensor(cut, cut, blk_base[:, j:j + 1], onehot[:, j, :],
                                                        ALU.add, ALU.mult))
                            step(v.tensor_tensor(posf[:], posf[:], cut, ALU.add))
                    v.tensor_copy(edge_tmp[:], posf[:]).then_inc(tri_read, 1)
                    dve.wait_ge(tri_read, 1)
                    step(v.tensor_scalar(dst_i[:], edge_tmp[:], P - 1, None, ALU.bitwise_and))
                    step(v.tensor_copy(place_lo[:], dst_i[:]))
                    step(v.tensor_scalar(dst_i[:], edge_tmp[:], 7, None, ALU.arith_shift_right))
                    step(v.tensor_copy(place_hi[:], dst_i[:]))

                step1 = chain(dve, "stage1_step")
                v.memset(x_last[96:P, NT - 1 - XA, :], 0.0).then_inc(pad_set, 1)
                step1(v.memset(src_i[:], 0))
                step1(v.memset(typ_i[:], 0))
                v.memset(dst_i[:], -1).then_inc(edges_set, 1)
                step1(v.memset(ones_f[:], 1.0))

                def normalize(g):
                    a, b = LN_GROUPS[g]
                    for j in range(a, b):
                        dve.wait_ge(xin[j], 16)
                        v.bn_stats(stat[:, j, 0, :], x_tile(j)[:, 0:HALF])
                        step1(v.bn_stats(stat[:, j, 1, :], x_tile(j)[:, HALF:D]))
                        step1(v.bn_aggr(aggr[:, j, :], stat[:, j, :, :].rearrange("p a b -> p (a b)")))
                    v.tensor_scalar(tmp10[:, 0, a:b], aggr[:, a:b, 1], EPS, None, ALU.add).then_inc(var_ready, 1)
                    step1(v.tensor_copy(mean[:, a:b], aggr[:, a:b, 0]))
                    dve.wait_ge(sqrt_ready, g + 1)
                    dve.wait_ge(var_ready, g + 1)
                    step1(v.reciprocal(tmp10[:, 2, a:b], tmp10[:, 1, a:b]))
                    step1(v.tensor_tensor(tmp10[:, 3, a:b], tmp10[:, 2, a:b], tmp10[:, 2, a:b], ALU.mult))
                    step1(v.tensor_tensor(tmp10[:, 3, a:b], tmp10[:, 3, a:b], tmp10[:, 0, a:b], ALU.mult))
                    step1(v.tensor_scalar(tmp10[:, 3, a:b], tmp10[:, 3, a:b], -0.5, 1.5, ALU.mult, ALU.add))
                    step1(v.tensor_tensor(rstd[:, a:b], tmp10[:, 3, a:b], tmp10[:, 2, a:b], ALU.mult))
                    for j in range(a, b):
                        v.tensor_scalar(x_tile(j), x_tile(j), mean[:, j:j + 1], rstd[:, j:j + 1],
                                        ALU.subtract, ALU.mult).then_inc(norm_ready, 1)

                def x_lo(*tiles):
                    for n in (n for j in tiles for n in (2 * j, 2 * j + 1)):
                        j, g = n // 2, n % 2
                        dve.wait_ge(hi_done, n + 1)
                        at = (slice(None), slice(4 * g, 4 * g + 4), slice(j * P, (j + 1) * P))
                        v.tensor_tensor(xlo[at], psum[4 + n % 4][:].rearrange("p (k n) -> p k n", k=4),
                                        xhi[at].bitcast(F32), ALU.subtract).then_inc(lo_done, 1)

                normalize(0)
                split_lo(0, 0, 0)
                normalize(1)
                split_lo(0, 0, 1)
                x_lo(0)
                split_lo(0, 0, 2)
                split_lo(0, 0, 3)
                x_lo(1)
                normalize(2)
                normalize(3)
                for j in range(NT):
                    if j + 2 < NT:
                        x_lo(j + 2)
                    if j + 4 < len(LN_GROUPS):
                        normalize(j + 4)
                    if j in FIRST_SPLITS:
                        split_lo(0, 1, FIRST_SPLITS.index(j))
                edge_places()

                def relation(r, sorts, start=False, first=False):
                    for h in range(2):
                        for q in range(4):
                            if sorts:
                                columns(r, 4 * h + q, first and h * 4 + q == 0)
                            if not (start and h == 0):
                                split_lo(*((r, 1) if h == 0 else (r + 1, 0)), q)
                relation(0, False, start=True)
                relation(1, True, first=True)
                with dve.Fori(2, 1 + SORT_R) as r:
                    relation(r, True)
                step = chain(dve, "stage2_step")
                dve.wait_ge(cols_used, 8 * SORT_R)
                step(v.tensor_copy(placed[:], PLACE_BANK[:, 0:2 * ET].rearrange("p (a t) -> p a t", a=2)))
                step(v.tensor_scalar(inv[:], COUNT_BANK[0:KHI, 0:256], 1.0, None, ALU.max))
                v.reciprocal(inv[:], inv[:]).then_inc(inv_ready, 1)
                step(v.tensor_copy(placed_i[:, 0], placed[:, 1]))
                step(v.tensor_scalar(placed_i[:, 1], placed_i[:, 0], 3, None, ALU.arith_shift_right))
                step(v.tensor_copy(edge_dst[:], placed_i[:, 1]))
                step(v.tensor_scalar(placed_i[:, 2], placed_i[:, 0], R - 1, None, ALU.bitwise_and))
                step(v.tensor_copy(tfl[:, 0], placed_i[:, 2]))
                step(v.scalar_tensor_tensor(edge_row[:], tfl[:, 0], float(NP), placed[:, 0], ALU.mult, ALU.add))
                step(v.tensor_scalar(tfl[:, 1], iota[:, 0:ET], float(P), None, ALU.mult))
                step(v.memset(tfl[:, 2], 0.0))
                for j in range(1, NT):
                    step(v.scalar_tensor_tensor(tfl[:, 2], tfl[:, 1], blk_base[:, j:j + 1], tfl[:, 2],
                                                ALU.is_ge, ALU.add))
                step(v.tensor_copy(tile_block[:], tfl[:, 2]))
                step(v.scalar_tensor_tensor(tfl[:, 3], tfl[:, 2], float(P * R), placed[:, 1], ALU.mult, ALU.add))
                v.tensor_scalar(edge_key[:], tfl[:, 3], -float(R), 0.0, ALU.add, ALU.max).then_inc(key_ready, 1)
                with dve.Fori(1 + SORT_R, R - 1) as r:
                    relation(r, False)
                dve.wait_ge(inv_out, 16)
                v.memset(acc[:], 0.0)
                relation(R - 1, False)

            @block.gpsimd
            def _(pool):
                built = sem("built")
                nc.gpsimd.memset(ident[:], 0.0).then_inc(built, 1)
                nc.gpsimd.memset(tri[:], 1.0).then_inc(built, 1)
                pool.wait_ge(built, 2)
                nc.gpsimd.affine_select(out=ident[:], in_=ident[:], compare_op=ALU.not_equal, fill=1.0,
                                        base=0, pattern=[[-1, P]], channel_multiplier=1).then_inc(consts, 1)
                nc.gpsimd.affine_select(out=tri[:], in_=tri[:], compare_op=ALU.is_gt, fill=0.0,
                                        base=0, pattern=[[1, P]], channel_multiplier=-1).then_inc(consts, 1)
                nc.gpsimd.memset(ones[:], 1.0).then_inc(consts, 1)
                nc.gpsimd.iota(iota[:], pattern=[[1, 257]], base=0, channel_multiplier=0,
                               allow_small_or_imprecise_dtypes=True).then_inc(consts, 1)
                nc.gpsimd.iota(lanes[:], pattern=[[1, 1]], base=0, channel_multiplier=1,
                               allow_small_or_imprecise_dtypes=True).then_inc(consts, 1)
                pool.wait_ge(edges_set, 1)
                for tile, vec in ((src_i, src), (dst_i, dst), (typ_i, edge_type)):
                    pool.dma_start(tile[:, 0:EFULL], vec[0:EFULL * P].rearrange("(p c) -> p c", p=P)
                                   ).then_inc(edges_in, 16)
                    pool.dma_start(tile[0:EREST, EFULL:EFULL + 1],
                                   vec[EFULL * P:E].rearrange("(p c) -> p c", c=1)).then_inc(edges_in, 16)
                pool.wait_ge(inv_ready, 1)
                pool.dma_start(INV.rearrange("(a b) c -> a (b c)", b=256), inv[:]).then_inc(inv_out, 16)
                pool.wait_ge(inv_out, 16)
                pool.wait_ge(key_ready, 1)
                for t in range(ET):
                    nc.gpsimd.indirect_dma_start(
                        out=edge_w[:, t:t + 1], out_offset=None, in_=INV,
                        in_offset=bass.IndirectOffsetOnAxis(ap=edge_key[:, t:t + 1], axis=0)).then_inc(w_gathered, 16)
                pool.wait_ge(w_gathered, 16 * ET)

            @block.tensor
            def _(pe):
                def product(r, h, j, first=False):
                    m = r * 2 * NT + h * NT + j
                    slot = (h * NT + j) % YB
                    if first and h == 0:
                        pe.wait_ge(lo_done, 2 * (j + 1))
                    if not (first and h * NT + j < YB):
                        pe.wait_ge(y_evac, m + 1 - YB)
                    at = slice(j * P, (j + 1) * P)
                    for k in range(KC):
                        if j == 0 and k % 2 == 0:
                            pe.wait_ge(w_lo, r * 8 + h * 4 + k // 2 + 1)
                        pe.matmul(psum[slot][:], xhi[:, k, at], whi[h][:, k], start=(k == 0), stop=False)
                        pe.matmul(psum[slot][:], xhi[:, k, at], wlo[h][:, k], start=False, stop=False)
                        ins = pe.matmul(psum[slot][:], xlo[:, k, at], whi[h][:, k], start=False, stop=(k == KC - 1))
                    ins.then_inc(y_ready, 1)

                def columns(r, part, first=False, last=False):
                    pe.wait_ge(cols_ready, (r - 1) * 8 + part + 1)
                    for i in range(CPQ):
                        a, z = first and i == 0, last and i == CPQ - 1
                        pe.matmul(PLACE_BANK[:, 0:2 * ET], oh_lo[:, i],
                                  oh_val[:, i].rearrange("p a t -> p (a t)"), start=a, stop=z, skip_group_check=True)
                        ins = pe.matmul(COUNT_BANK[0:KHI, 0:256], oh_khi[:, i], oh_klo[:, i],
                                        start=a, stop=z, skip_group_check=True)
                    ins.then_inc(cols_used, 1)

                def ranks(left, done):
                    pe.wait_ge(onehot_ready, 1)
                    for g, js in enumerate(groups):
                        pe.matmul(psum[4 + g][:, :len(js) * ECOLS], left[:],
                                  onehot[:, js[0]:js[-1] + 1, :].rearrange("p j c -> p (j c)"),
                                  start=True, stop=True).then_inc(done, 1)

                def turn(j):
                    pe.wait_ge(norm_ready, j + 1)
                    for n in (2 * j, 2 * j + 1):
                        if n >= 4:
                            pe.wait_ge(lo_done, n - 3)
                        for k in range(4):
                            kc = 4 * (n % 2) + k
                            ins = pe.transpose(psum[4 + n % 4][:, k * P:(k + 1) * P],
                                               x_tile(j)[:, kc * P:(kc + 1) * P], ident[:])
                        ins.then_inc(tr_done, 1)

                pe.wait_ge(consts, 5)
                turn(0)
                turn(1)

                def relation(r, sorts, start=False, first=False, last=False):
                    for h in range(2):
                        for j in range(NT):
                            product(r, h, j, start)
                            if start and h == 0 and j + 2 < NT:
                                turn(j + 2)
                            if start and (h, j) == RANK_AFTER[0]:
                                ranks(ones, totals_done)
                            if start and (h, j) == RANK_AFTER[1]:
                                pe.wait_ge(totals_read, 1)
                                ranks(tri, tri_done)
                            if sorts and j % 2 == 1 and j < 8:
                                part = 4 * h + j // 2
                                columns(r, part, first and part == 0, last and part == 7)
                relation(0, False, start=True)
                relation(1, True, first=True)
                with pe.Fori(2, SORT_R) as r:
                    relation(r, True)
                relation(SORT_R, True, last=True)
                with pe.Fori(1 + SORT_R, R) as r:
                    relation(r, False)


        z3 = Zone(OFF_W1, OFF_END - OFF_W1)
        after_acc = OFF_END + 4 * NT * D
        gath = z3.put("gathered", [P, 4, D], F32)
        ghi = z3.put("ghi", [P, 2, D], F32R)
        glo = z3.put("glo", [P, 2, D], F32R)
        sel = Zone(OFF_YOUT + 4 * KB, 4 * KB).put("sel", [P, 4, P], F32R)
        PH = PAIRS // 4
        TH = PH * GROUP
        EXTRA = PH - 2 * NT
        assert GROUP == 2 and EXTRA >= 1 and TH % 4 == 0
        w_in = [sem(f"w3_stage_loaded{i}") for i in range(2)]
        w_hi, w_lo = sem("w3_hi_written"), sem("w3_lo_written")
        y_ready, y_evac = sem("y3_ready"), sem("y3_evacuated")
        y_out = [sem(f"y3_stored{i}") for i in range(2)]
        g_in = [sem(f"rows_gathered{i}") for i in range(4)]
        sel_ready, g_hi, g_lo, g_used, acc_done = (
            sem("sel_ready"), sem("rows_hi"), sem("rows_lo"), sem("edge_tiles_used"), sem("pairs_accumulated"))

        def changes(g):
            for q in range(4):
                yield "split", q
                if q < EXTRA:
                    yield "pair", 2 * NT + q
            for e in range(4, EXTRA):
                yield "pair", 2 * NT + e

        with nc.Block() as block:
            @block.sync
            def _(sp):
                def load(g, q):
                    n = 4 * (g - 1) + q
                    if n >= 2:
                        sp.wait_ge(w_lo, n - 1)
                    w = root if g < 2 else w_gate[D:2 * D, :]
                    sp.dma_start(stage[:, q % 2], w_rows(w, q, g % 2)).then_inc(w_in[q % 2], 16)

                load(1, 0)
                load(1, 1)
                for g in range(4):
                    if g >= 1:
                        load(g, 2)
                        load(g, 3)
                    if 1 <= g < 3:
                        load(g + 1, 0)
                        load(g + 1, 1)
                    for j in range(NT):
                        sp.wait_ge(y_evac, g * NT + j + 1)
                        sp.dma_start(YX[g // 2, j * P:(j + 1) * P, (g % 2) * HALF:(g % 2 + 1) * HALF],
                                     yout[:, j % 2]).then_inc(y_out[j % 2], 16)
                for i in range(2):
                    sp.wait_ge(y_out[i], 16 * 2 * NT)

            @block.gpsimd
            def _(pool):
                for t in range(ET):
                    if t >= 4:
                        pool.wait_ge(g_lo, t - 3)
                    nc.gpsimd.indirect_dma_start(
                        out=gath[:, t % 4], out_offset=None, in_=Y,
                        in_offset=bass.IndirectOffsetOnAxis(ap=edge_row[:, t:t + 1], axis=0)).then_inc(g_in[t % 4], 16)
                    if t >= 4:
                        pool.wait_ge(g_used, t - 3)
                    nc.gpsimd.tensor_scalar(sel[:, t % 4], iota[:, 1:P + 1], edge_dst[:, t:t + 1], None,
                                            ALU.is_equal).then_inc(sel_ready, 1)

            @block.scalar
            def _(act):
                def split_hi(g, q):
                    act.wait_ge(w_in[q % 2], 16 * (2 * (g - 1) + q // 2 + 1))
                    nc.scalar.activation(whi[0][:, 2 * q:2 * q + 2, :], stage[:, q % 2], ACT.Copy).then_inc(w_hi, 1)

                def pair_hi(g, p, first=False):
                    for i in range(2):
                        tl = 2 * p + i
                        t = g * TH + tl
                        act.wait_ge(g_in[tl % 4], 16 * (g * (TH // 4) + tl // 4 + 1))
                        if not (first and tl < 2):
                            act.wait_ge(g_used, t - 1)
                        nc.scalar.activation(ghi[:, i], gath[:, tl % 4], ACT.Copy,
                                             scale=edge_w[:, bass.ds(t, 1)]).then_inc(g_hi, 1)

                def half(g, first=False, last=False):
                    for j in range(NT):
                        for b in range(2):
                            pair_hi(g, 2 * j + b, first)
                        act.wait_ge(y_ready, g * NT + j + 1)
                        if not (first and j < 2):
                            act.wait_ge(y_out[j % 2], 16 * (g * (NT // 2) + j // 2))
                        nc.scalar.activation(yout[:, j % 2], psum[j % 2][:], ACT.Copy).then_inc(y_evac, 1)
                    for what, n in changes(g):
                        if what == "pair":
                            pair_hi(g, n)
                        elif not last:
                            split_hi(g + 1, n)
                half(0, first=True)
                with act.Fori(1, 3) as g:
                    half(g)
                half(3, last=True)

            @block.vector
            def _(dve):
                v = nc.vector

                def split_lo(g, q):
                    dve.wait_ge(w_hi, 4 * (g - 1) + q + 1)
                    v.tensor_tensor(wlo[0][:, 2 * q:2 * q + 2, :], stage[:, q % 2],
                                    whi[0][:, 2 * q:2 * q + 2, :].bitcast(F32), ALU.subtract).then_inc(w_lo, 1)

                def pair_lo(g, p, first=False):
                    for i in range(2):
                        tl = 2 * p + i
                        t = g * TH + tl
                        if not (first and tl < 2):
                            dve.wait_ge(g_used, t - 1)
                        dve.wait_ge(g_hi, t + 1)
                        v.scalar_tensor_tensor(glo[:, i], gath[:, tl % 4], edge_w[:, bass.ds(t, 1)],
                                               ghi[:, i].bitcast(F32), ALU.mult, ALU.subtract).then_inc(g_lo, 1)

                def accumulate(g, p, first=False):
                    n = g * PH + p
                    block_of = dve.value_load(tile_block[0:1, bass.ds(n * GROUP, 1)], min_val=0, max_val=NT - 1)
                    at = bass.ds(block_of * D, D)
                    dve.wait_ge(g_used, 2 * (n + 1))
                    if not first:
                        dve.wait_ge(acc_done, n)
                    for c in range(2):
                        at = bass.ds(block_of * D + c * BANK, BANK)
                        ins = v.tensor_tensor(acc[:, at], acc[:, at], psum[4 + 2 * (p % 2) + c][:], ALU.add)
                    ins.then_inc(acc_done, 1)

                def half(g, first=False, last=False):
                    for p in range(2 * NT):
                        pair_lo(g, p, first)
                        if p:
                            accumulate(g, p - 1, first and p == 1)
                    for what, n in changes(g):
                        if what == "pair":
                            pair_lo(g, n)
                            accumulate(g, n - 1)
                        elif not last:
                            split_lo(g + 1, n)
                    accumulate(g, PH - 1)
                half(0, first=True)
                with dve.Fori(1, 3) as g:
                    half(g)
                half(3, last=True)

            @block.tensor
            def _(pe):
                def product(g, j, b, first=False):
                    if b == 0:
                        if j == 0 and not first:
                            pe.wait_ge(w_lo, 4 * g)
                        if not (first and j < 2):
                            pe.wait_ge(y_evac, g * NT + j - 1)
                    at = slice(j * P, (j + 1) * P)
                    for k in range(4 * b, 4 * b + 4):
                        pe.matmul(psum[j % 2][:], xhi[:, k, at], whi[0][:, k], start=(k == 0), stop=False)
                        pe.matmul(psum[j % 2][:], xhi[:, k, at], wlo[0][:, k], start=False, stop=False)
                        ins = pe.matmul(psum[j % 2][:], xlo[:, k, at], whi[0][:, k], start=False, stop=(k == KC - 1))
                    if b == 1:
                        ins.then_inc(y_ready, 1)

                def pair(g, p, first=False):
                    if not (first and p < 2):
                        pe.wait_ge(acc_done, g * PH + p - 1)
                    for i in range(2):
                        pe.wait_ge(g_lo, g * TH + 2 * p + i + 1)
                        pe.wait_ge(sel_ready, g * TH + 2 * p + i + 1)
                        one_hot = sel[:, (2 * p + i) % 4]
                        for c in range(2):
                            bank = psum[4 + 2 * (p % 2) + c]
                            cols = slice(c * BANK, (c + 1) * BANK)
                            pe.matmul(bank[:], one_hot, ghi[:, i, cols], start=(i == 0), stop=False)
                            ins = pe.matmul(bank[:], one_hot, glo[:, i, cols], start=False, stop=(i == 1))
                        ins.then_inc(g_used, 1)

                def half(g, first=False):
                    for j in range(NT):
                        for b in range(2):
                            product(g, j, b, first)
                            pair(g, 2 * j + b, first)
                    for e in range(EXTRA):
                        pair(g, 2 * NT + e)
                half(0, True)
                with pe.Fori(1, 4) as g:
                    half(g)


        wghi = nc.alloc_sbuf_tensor_at("wghi", [P, KC, D], F32R, offset=OFF_T)
        wglo = nc.alloc_sbuf_tensor_at("wglo", [P, KC, D], F32R, offset=OFF_T + 32 * KB)
        za, zb, zc = (Zone(OFF_T + 64 * KB, 16 * KB), Zone(OFF_YOUT, OFF_W1 - OFF_YOUT),
                      Zone(OFF_W1, OFF_END - OFF_W1))
        zd = Zone(after_acc, LIMIT - after_acc)
        uhi = za.put("uhi", [P, 2, D], F32R)
        ulo = za.put("ulo", [P, 2, D], F32R)
        u = zb.put("u", [P, 2, D], F32)
        xr = zb.put("xr", [P, 2, D], F32)
        zg = zb.put("zg", [P, 2, D], F32)
        th = zb.put("th", [P, 2, D], F32)
        xn = zb.put("xn", [P, 2, D], F32)
        x1 = zc.put("x1", [P, 2, D], F32)
        xn2 = zc.put("xn2", [P, 2, D], F32)
        xn2t = zc.put("xn2t", [P, KC, P], F32)
        bias_b = zc.put("bias_b", [P, D], F32)
        bgate_b = zc.put("bgate_b", [P, D], F32)
        gw_rows = zc.put("gw_rows", [P, D], F32)
        gw_t = zd.put("gw_t", [P, KC, X], F32)
        st2 = zd.put("st2", [P, 2, 6], F32)
        ag2 = zd.put("ag2", [P, 2], F32)
        rs = zd.put("rs", [P, 4], F32)
        rs_i = zd.put("rs_i", [P, 2], I32)
        LOGITS = psum[6]

        w_in = [sem(f"wg_stage_loaded{i}") for i in range(2)]
        w_hi, w_lo = sem("wg_hi_written"), sem("wg_lo_written")
        rows_in, small_in = sem("small_rows_loaded"), sem("gate_w_loaded")
        x_in, r_in, g_in4 = ([sem(f"{n}_loaded{i}") for i in range(2)] for n in ("xr", "u", "zg"))
        bias_done, bg_done, sum_done = sem("bias_added"), sem("bgate_added"), sem("x_plus_norm")
        u_done, xn_done, tu_done, uhi_done, ulo_done, th_done = (
            sem("u_done"), sem("xn_done"), sem("u_transposed"), sem("uhi_done"), sem("ulo_done"), sem("tanh_done"))
        z_done, zg_done, x1_done, xn2_done = sem("z_done"), sem("z_read"), sem("x1_done"), sem("xn2_done")
        tx_done, tx_evac, lg_done = sem("xn2_transposed"), sem("xn2t_written"), sem("logits_done")
        x1_out, xn2_out = ([sem(f"{n}_stored{i}") for i in range(2)] for n in ("x1", "xn2"))
        gwt_done, gwt_evac = sem("gate_w_transposed"), sem("gate_w_t_written")

        with nc.Block() as block:
            @block.sync
            def _(sp):
                def fetch_u(j):
                    if j >= 2:
                        sp.wait_ge(th_done, j - 1)
                        sp.wait_ge(tu_done, 2 * (j - 1))
                    sp.dma_start(u[:, j % 2], YX[0, j * P:(j + 1) * P, :]).then_inc(r_in[j % 2], 16)

                def fetch_x(j):
                    if j >= 2:
                        sp.wait_ge(x1_done, j - 1)
                    sp.dma_start(xr[:rows(j), j % 2], x[j * P:j * P + rows(j), :]).then_inc(x_in[j % 2], 16)
                    sp.dma_start(zg[:, j % 2], YX[1, j * P:(j + 1) * P, :]).then_inc(g_in4[j % 2], 16)

                for n in range(8):
                    h, q = n // 4, n % 4
                    if n >= 2:
                        sp.wait_ge(w_lo, n - 1)
                    sp.dma_start(stage[:, q % 2], w_rows(w_gate, q, h)).then_inc(w_in[q % 2], 16)
                    if n == 1:
                        fetch_u(0)
                        fetch_u(1)
                        sp.dma_start(bias_b[:], bias.partition_broadcast(P)).then_inc(rows_in, 16)
                        sp.dma_start(bgate_b[:], b_gate.partition_broadcast(P)).then_inc(rows_in, 16)
                        sp.dma_start(gw_rows[0:X, :], gate_w).then_inc(small_in, 16)
                        fetch_x(0)
                        fetch_x(1)
                for j in range(NT + 1):
                    if j + 2 < NT:
                        fetch_u(j + 2)
                    if j == 0:
                        continue
                    d = j - 1
                    sp.wait_ge(x1_done, d + 1)
                    sp.dma_start(X1[d * P:(d + 1) * P, :], x1[:, d % 2]).then_inc(x1_out[d % 2], 16)
                    if d + 2 < NT:
                        fetch_x(d + 2)
                    sp.wait_ge(xn2_done, d + 1)
                    sp.dma_start(XN2[d * P:(d + 1) * P, :], xn2[:, d % 2]).then_inc(xn2_out[d % 2], 16)
                for i in range(2):
                    sp.wait_ge(x1_out[i], 16 * NT // 2)
                    sp.wait_ge(xn2_out[i], 16 * NT // 2)

            @block.gpsimd
            def _(pool):
                pool.wait_ge(rows_in, 32)

                def add_biases(j):
                    pool.wait_ge(r_in[j % 2], 16 * (j // 2 + 1))
                    nc.gpsimd.tensor_tensor(u[:, j % 2], u[:, j % 2], bias_b[:], ALU.add).then_inc(bias_done, 1)
                add_biases(0)
                add_biases(1)
                for j in range(NT):
                    if j + 2 < NT:
                        add_biases(j + 2)
                    pool.wait_ge(g_in4[j % 2], 16 * (j // 2 + 1))
                    nc.gpsimd.tensor_tensor(zg[:, j % 2], zg[:, j % 2], bgate_b[:], ALU.add).then_inc(bg_done, 1)
                    pool.wait_ge(xn_done, j + 1)
                    nc.gpsimd.tensor_tensor(xr[:, j % 2], xr[:, j % 2], xn[:, j % 2], ALU.add).then_inc(sum_done, 1)

            @block.scalar
            def _(act):
                def split_hi(n):
                    h, q = n // 4, n % 4
                    act.wait_ge(w_in[q % 2], 16 * (n // 2 + 1))
                    nc.scalar.activation(wghi[:, 2 * q:2 * q + 2, h * HALF:(h + 1) * HALF], stage[:, q % 2],
                                         ACT.Copy).then_inc(w_hi, 1)

                def u_part(j):
                    for g in range(2):
                        act.wait_ge(tu_done, 2 * j + g + 1)
                        if j >= 2:
                            act.wait_ge(z_done, 2 * (j - 1))
                        nc.scalar.activation(uhi[:, j % 2, g * BANK:(g + 1) * BANK], psum[g][:],
                                             ACT.Copy).then_inc(uhi_done, 1)
                    if j >= 2:
                        act.wait_ge(x1_done, j - 1)
                    act.wait_ge(u_done, j + 1)
                    nc.scalar.activation(th[:, j % 2], u[:, j % 2], ACT.Tanh).then_inc(th_done, 1)

                def xt_part(j):
                    for g in range(2):
                        act.wait_ge(tx_done, 2 * j + g + 1)
                        if j >= 1:
                            act.wait_ge(lg_done, j)
                        nc.scalar.activation(xn2t[:, 4 * g:4 * g + 4, :],
                                             psum[g][:].rearrange("p (k n) -> p k n", k=4),
                                             ACT.Copy).then_inc(tx_evac, 1)
                split_hi(0)
                split_hi(1)
                u_part(0)
                for n in range(2, 8):
                    split_hi(n)
                act.wait_ge(gwt_done, 1)
                nc.scalar.activation(gw_t[:], psum[7][:, 0:KC * X].rearrange("p (k e) -> p k e", e=X),
                                     ACT.Copy).then_inc(gwt_evac, 1)
                for j in range(NT):
                    if j + 1 < NT:
                        u_part(j + 1)
                    if j >= 2:
                        xt_part(j - 2)
                xt_part(NT - 2)
                xt_part(NT - 1)

            @block.vector
            def _(dve):
                v = nc.vector
                step = chain(dve, "stage4_step")

                def split_lo(n):
                    h, q = n // 4, n % 4
                    dve.wait_ge(w_hi, n + 1)
                    at = (slice(None), slice(2 * q, 2 * q + 2), slice(h * HALF, (h + 1) * HALF))
                    v.tensor_tensor(wglo[at], stage[:, q % 2], wghi[at].bitcast(F32), ALU.subtract).then_inc(w_lo, 1)

                def make_u(j):
                    dve.wait_ge(bias_done, j + 1)
                    v.tensor_tensor(u[:, j % 2], u[:, j % 2], acc[:, j * D:(j + 1) * D], ALU.add).then_inc(u_done, 1)

                def u_low(j):
                    for g in range(2):
                        dve.wait_ge(uhi_done, 2 * j + g + 1)
                        at = (slice(None), j % 2, slice(g * BANK, (g + 1) * BANK))
                        v.tensor_tensor(ulo[at], psum[g][:], uhi[at].bitcast(F32), ALU.subtract).then_inc(ulo_done, 1)

                def finish(j):
                    i = j % 2
                    dve.wait_ge(x_in[i], 16 * (j // 2 + 1))
                    v.tensor_scalar(xn[:, i], xr[:, i], mean[:, j:j + 1], rstd[:, j:j + 1],
                                    ALU.subtract, ALU.mult).then_inc(xn_done, 1)
                    dve.wait_ge(th_done, j + 1)
                    dve.wait_ge(xn_done, j + 1)
                    step(v.tensor_tensor(th[:, i], th[:, i], xn[:, i], ALU.subtract))
                    dve.wait_ge(bg_done, j + 1)
                    for c in range(2):
                        dve.wait_ge(z_done, 2 * j + c + 1)
                        ins = v.tensor_tensor(zg[:, i, c * BANK:(c + 1) * BANK], psum[2 + 2 * i + c][:],
                                              zg[:, i, c * BANK:(c + 1) * BANK], ALU.add)
                    ins.then_inc(zg_done, 1)
                    dve.wait_ge(zg_done, j + 1)
                    step(v.tensor_tensor(th[:, i], th[:, i], zg[:, i], ALU.mult))
                    dve.wait_ge(sum_done, j + 1)
                    if j >= 2:
                        dve.wait_ge(x1_out[i], 16 * (j // 2))
                        dve.wait_ge(xn2_out[i], 16 * (j // 2))
                        dve.wait_ge(tx_done, 2 * (j - 1))
                    v.tensor_tensor(x1[:, i], xr[:, i], th[:, i], ALU.add).then_inc(x1_done, 1)
                    dve.wait_ge(x1_done, j + 1)
                    v.bn_stats(st2[:, 0, :], x1[:, i, 0:HALF])
                    step(v.bn_stats(st2[:, 1, :], x1[:, i, HALF:D]))
                    step(v.bn_aggr(ag2[:], st2[:].rearrange("p a b -> p (a b)")))
                    step(v.tensor_scalar(rs[:, 0:1], ag2[:, 1:2], EPS, None, ALU.add))
                    step(v.tensor_scalar(rs_i[:, 0:1], rs[:, 0:1].bitcast(I32), 1, None, ALU.arith_shift_right))
                    step(v.tensor_scalar(rs_i[:, 1:2], rs_i[:, 0:1], -1.0, float(0x5F3759DF), ALU.mult, ALU.add))
                    y = rs_i[:, 1:2].bitcast(F32)
                    for n in range(4):
                        step(v.scalar_tensor_tensor(rs[:, 1:2], y, rs[:, 0:1], y, ALU.mult, ALU.mult))
                        step(v.tensor_scalar(rs[:, 2:3], rs[:, 1:2], -0.5, 1.5, ALU.mult, ALU.add))
                        step(v.tensor_tensor(rs[:, 3:4], y, rs[:, 2:3], ALU.mult))
                        y = rs[:, 3:4]
                    v.tensor_scalar(xn2[:, i], x1[:, i], ag2[:, 0:1], rs[:, 3:4],
                                    ALU.subtract, ALU.mult).then_inc(xn2_done, 1)
                    dve.wait_ge(xn2_done, j + 1)

                split_lo(0)
                split_lo(1)
                make_u(0)
                make_u(1)
                u_low(0)
                for n in range(2, 8):
                    split_lo(n)
                for j in range(NT):
                    if j + 1 < NT:
                        u_low(j + 1)
                    if j >= 1:
                        finish(j - 1)
                    if j + 2 < NT:
                        dve.wait_ge(r_in[j % 2], 16 * (j // 2 + 2))
                        make_u(j + 2)
                finish(NT - 1)

            @block.tensor
            def _(pe):
                def turn(j, src_t, ready, free, done):
                    pe.wait_ge(ready, j + 1)
                    for g in range(2):
                        for what, least in free(g):
                            pe.wait_ge(what, least)
                        for k in range(4):
                            c = 4 * g + k
                            ins = pe.transpose(psum[g][:, k * P:(k + 1) * P], src_t[:, j % 2, c * P:(c + 1) * P], ident[:])
                        ins.then_inc(done, 1)

                def turn_u(j):
                    turn(j, u, u_done, lambda g: ([(ulo_done, 2 * (j - 1) + g + 1)] if j >= 1 else [])
                         + ([(tx_evac, 2 * (j - 4) + g + 1)] if j >= 4 else []), tu_done)

                def turn_x(j, free):
                    turn(j, xn2, xn2_done, free, tx_done)

                def gate(j, c):
                    i = j % 2
                    pe.wait_ge(w_lo, 4 * (c + 1))
                    pe.wait_ge(ulo_done, 2 * (j + 1))
                    if j >= 2:
                        pe.wait_ge(zg_done, j - 1)
                    for k in range(KC):
                        at, cols = slice(k * P, (k + 1) * P), slice(c * BANK, (c + 1) * BANK)
                        bank = psum[2 + 2 * i + c]
                        pe.matmul(bank[:], uhi[:, i, at], wghi[:, k, cols], start=(k == 0), stop=False)
                        pe.matmul(bank[:], uhi[:, i, at], wglo[:, k, cols], start=False, stop=False)
                        ins = pe.matmul(bank[:], ulo[:, i, at], wghi[:, k, cols], start=False, stop=(k == KC - 1))
                    ins.then_inc(z_done, 1)

                def logits(j):
                    pe.wait_ge(tx_evac, 2 * (j + 1))
                    pe.wait_ge(gwt_evac, 1)
                    for k in range(KC):
                        ins = pe.matmul(LOGITS[:, j * X:(j + 1) * X], xn2t[:, k], gw_t[:, k],
                                        start=(k == 0), stop=(k == KC - 1))
                    ins.then_inc(lg_done, 1)

                turn_u(0)
                pe.wait_ge(small_in, 16)
                for k in range(KC):
                    ins = pe.transpose(psum[7][:, k * X:(k + 1) * X], gw_rows[0:X, k * P:(k + 1) * P], ident[0:X, 0:X])
                ins.then_inc(gwt_done, 1)
                for j in range(NT):
                    if j + 1 < NT:
                        turn_u(j + 1)
                    gate(j, 0)
                    if j >= 2:
                        turn_x(j - 2, lambda g: [(ulo_done, 2 * min(j + 1, NT - 1) + g + 1)])
                    gate(j, 1)
                    if j >= 2:
                        logits(j - 2)
                for j in (NT - 2, NT - 1):
                    turn_x(j, lambda g: [(tx_evac, 2 * (j - 1) + g + 1)])
                    logits(j)

        z5 = Zone(OFF_T, LIMIT - OFF_T)
        C2 = 2 * NT
        lg = z5.put("lg", [P, NT, X], F32)
        pr = z5.put("pr", [P, NT, X], F32)
        top = z5.put("top", [P, NT, 8], F32)
        top_i = z5.put("top_i", [P, NT, 8], U32)
        red = z5.put("red", [P, 3, NT], F32)
        sel_f = z5.put("sel_f", [P, NT, 2], F32)
        past = z5.put("past", [P, 2], F32)
        oh_e = z5.put("oh_e", [P, X, C2], BF16)
        bef = z5.put("bef", [P, X, C2], F32)
        wit = z5.put("wit", [P, X, C2], F32)
        ce = z5.put("ce", [P, 4, X], F32)
        ce_i = z5.put("ce_i", [P, 2, X], I32)
        ones_e = z5.put("ones_e", [P, C2], F32)
        pos = z5.put("pos", [P, C2], F32)
        pos_i = z5.put("pos_i", [P, 3, C2], I32)
        place_i = z5.put("place_i", [P, C2], I32)
        p_lo = z5.put("p_lo", [P, C2], F32)
        p_hi = z5.put("p_hi", [P, C2], F32)
        tok_f = z5.put("tok_f", [P, NT], F32)
        poh_lo = z5.put("poh_lo", [P, C2, P], F32R)
        poh_hi = z5.put("poh_hi", [P, C2, MTE], F32R)
        tok_s = z5.put("tok_s", [P, MTE], F32)
        tok_i = z5.put("tok_i", [P, MTE], I32)
        te = z5.put("te", [P, 2, MTE], F32)
        tile_expert = z5.put("tile_expert", [P, MTE], I32)
        tile_slot = z5.put("tile_slot", [P, MTE], I32)
        first_tile = z5.put("first_tile", [P, X], I32)
        rt_lg, rt_exp, rt_oh, rt_tot, rt_rank, rt_poh, rt_tok, rt_idx, rt_ready = (
            sem("shifted_logits_ready"), sem("exp_done"), sem("expert_onehot_ready"), sem("expert_totals_done"),
            sem("expert_ranks_done"), sem("token_onehots_ready"), sem("tokens_placed"), sem("token_index_ready"),
            sem("tile_expert_ready"))
        rt_iota = sem("token_numbers_ready")

        w13_at = z5.at
        w13hi = [z5.put(f"w13hi{i}", [P, KC, 2 * H], F32R) for i in range(2)]
        w13lo = [z5.put(f"w13lo{i}", [P, KC, 2 * H], F32R) for i in range(2)]
        w2hi = [z5.put(f"w2hi{i}", [P, HC, D], F32R) for i in range(2)]
        w2lo = [z5.put(f"w2lo{i}", [P, HC, D], F32R) for i in range(2)]
        raw_at = z5.at
        raw13 = z5.put("raw13", [P, 2, KC, 2 * H], F32)
        raw2 = z5.put("raw2", [P, 2, HC, D], F32)
        xg = z5.put("xg", [P, 2, D], F32)
        xthi = z5.put("xthi", [P, 2, D], F32R)
        xtlo = z5.put("xtlo", [P, 2, D], F32R)
        tanh_h = z5.put("tanh_h", [P, H], F32)
        act_a = z5.put("act_a", [P, H], F32)
        act_g = z5.put("act_g", [P, 2, H], F32)
        gthi = z5.put("gthi", [P, 2, H], F32R)
        gtlo = z5.put("gtlo", [P, 2, H], F32R)
        ye = z5.put("ye", [P, 2, D], F32)
        raw_in = [sem(f"expert_loaded{i}") for i in range(2)]
        experts_here, tiles_split = sem("experts_here"), sem("tiles_split")
        ab_hi = [sem(f"w13_hi_written{c}") for c in range(2)]
        ab_lo = [sem(f"w13_lo_written{c}") for c in range(2)]
        c_hi, c_lo = sem("w2_hi_written"), sem("w2_lo_written")
        xg_in = [sem(f"tokens_gathered{i}") for i in range(2)]
        xt_done, xt_hi, xt_lo = sem("xt_done"), sem("xt_hi"), sem("xt_lo")
        h_done, ht_done, a_done, g_done = sem("h_done"), sem("h_tanh_done"), sem("h_silu_done"), sem("g_done")
        gt_done, gt_hi, gt_lo = sem("gt_done"), sem("gt_hi"), sem("gt_lo")
        ye_done, ye_evac, ye_out = sem("ye_done"), sem("ye_evacuated"), [sem(f"ye_stored{i}") for i in range(2)]
        assert (MT - 3) % 2 == 0 and HC == 2 and 2 * H == BANK
        YT = 8
        assert KC * 2 * H * 2 // D == YT and NT - YT <= 2 * HC
        x1b = nc.alloc_sbuf_tensor_at("x1b", [P, NT, D], F32, offset=raw_at)
        chosen_y = nc.alloc_sbuf_tensor_at("chosen_y", [P, YT, 2, D], F32, offset=w13_at)
        x1_in, out_stored = [sem(f"x1_loaded{i}") for i in range(2)], sem("out_stored")
        y1_in, y2_in = ([sem(f"{n}{i}") for i in range(YT)] for n in ("first_gathered", "second_gathered"))
        half_done, res_done = sem("first_added"), sem("result_done")

        with nc.Block() as block:
            @block.sync
            def _(sp):
                sp.sem_inc(tiles_split, 1)
                for e in range(X):
                    i = e % 2
                    if e == 2:
                        sp.wait_ge(raw_in[0], 48)
                        sp.sem_inc(experts_here, 1)
                        sp.wait_ge(rt_ready, 1)
                    if e >= 2:
                        sp.wait_ge(raw_in[1 - i], 48 * ((e - 1) // 2 + 1))
                        sp.sem_inc(experts_here, 1)
                        used = sp.value_load(first_tile[0:1, e - 1:e], min_val=0, max_val=MT)
                        sp.wait_ge(tiles_split, used + 1)
                    for n, w in enumerate((w1, w3)):
                        sp.dma_start(raw13[:, i, :, n * H:(n + 1) * H],
                                     w[e].rearrange("(k p) n -> p k n", p=P)).then_inc(raw_in[i], 16)
                    sp.dma_start(raw2[:, i], w2[e].rearrange("(k p) n -> p k n", p=P)).then_inc(raw_in[i], 16)
                sp.wait_ge(raw_in[(X - 1) % 2], 48 * ((X - 1) // 2 + 1))
                sp.sem_inc(experts_here, 1)
                sp.wait_ge(ab_lo[0], MT)
                sp.wait_ge(ab_lo[1], MT)
                for g, js in enumerate((slice(0, YT), slice(YT, NT))):
                    if g == 1:
                        sp.wait_ge(tiles_split, MT + 1)
                    sp.dma_start(x1b[:, js], X1.rearrange("(j p) d -> p j d", p=P)[:, js]).then_inc(x1_in[g], 16)
                for j in range(NT):
                    sp.wait_ge(res_done, j + 1)
                    sp.dma_start(out[j * P:j * P + rows(j), :], x1b[:rows(j), j]).then_inc(out_stored, 16)
                sp.wait_ge(out_stored, 16 * NT)

            @block.gpsimd
            def _(pool):
                nc.gpsimd.iota(tok_f[:], pattern=[[P, NT]], base=1, channel_multiplier=1,
                               allow_small_or_imprecise_dtypes=True).then_inc(rt_iota, 1)
                pool.wait_ge(rt_idx, 1)

                def gather(i):
                    if i >= 2:
                        pool.wait_ge(xt_done, 2 * (i - 1))
                    nc.gpsimd.indirect_dma_start(
                        out=xg[:, i % 2], out_offset=None, in_=XN2,
                        in_offset=bass.IndirectOffsetOnAxis(ap=tok_i[:, i:i + 1], axis=0)).then_inc(xg_in[i % 2], 16)

                gather(0)
                gather(1)
                for i in range(MT):
                    slot = pool.value_load(tile_slot[0:1, i:i + 1], min_val=0, max_val=1)
                    pool.wait_ge(c_hi, i + 1)
                    nc.gpsimd.tensor_tensor(w2lo[i % 2][:], raw2[:, bass.ds(slot, 1)].rearrange("p a k n -> p (a k) n"),
                                            w2hi[i % 2][:].bitcast(F32), ALU.subtract).then_inc(c_lo, 1)
                    if i + 2 < MT:
                        gather(i + 2)
                    pool.wait_ge(c_lo, i + 1)
                    for c in range(2):
                        pool.wait_ge(ab_lo[c], i + 1)
                    pool.sem_inc(tiles_split, 1)
                pool.wait_ge(ye_out[0], 16 * ((MT + 1) // 2))
                pool.wait_ge(ye_out[1], 16 * (MT // 2))
                for j in range(NT):
                    if j >= YT:
                        pool.wait_ge(res_done, j - YT + 1)
                    for k, got in enumerate((y1_in, y2_in)):
                        nc.gpsimd.indirect_dma_start(
                            out=chosen_y[:, j % YT, k], out_offset=None, in_=YS,
                            in_offset=bass.IndirectOffsetOnAxis(ap=place_i[:, 2 * j + k:2 * j + k + 1], axis=0)
                        ).then_inc(got[j % YT], 16)

            @block.scalar
            def _(act):
                a = nc.scalar
                act.wait_ge(rt_lg, 1)
                a.activation(pr[:], lg[:], ACT.Exp).then_inc(rt_exp, 1)

                def slot_of(i):
                    return act.value_load(tile_slot[0:1, bass.ds(i, 1)], min_val=0, max_val=1)

                def expert_of(i):
                    return act.value_load(tile_expert[0:1, bass.ds(i, 1)], min_val=0, max_val=X - 1)

                def hi_ab(i, s, c, slot, expert, first=False):
                    if c == 0:
                        act.wait_ge(experts_here, expert + 1)
                        if not first:
                            act.wait_ge(h_done, i - 1)
                    a.activation(w13hi[s][:, 4 * c:4 * c + 4, :],
                                 raw13[:, bass.ds(slot, 1), 4 * c:4 * c + 4, :].rearrange("p a k n -> p (a k) n"),
                                 ACT.Copy).then_inc(ab_hi[c], 1)

                def hi_c(i, s, slot, first=False):
                    if not first:
                        act.wait_ge(ye_done, 2 * (i - 1))
                    a.activation(w2hi[s][:], raw2[:, bass.ds(slot, 1)].rearrange("p a k n -> p (a k) n"),
                                 ACT.Copy).then_inc(c_hi, 1)

                def hi_x(i, s, first=False):
                    for g in range(2):
                        act.wait_ge(xt_done, 2 * i + g + 1)
                        if not first:
                            act.wait_ge(h_done, i - 1)
                        a.activation(xthi[:, s, g * BANK:(g + 1) * BANK], psum[2 + g][:], ACT.Copy).then_inc(xt_hi, 1)

                def tanh(i, s, first=False):
                    act.wait_ge(h_done, i + 1)
                    if not first:
                        act.wait_ge(a_done, i)
                    a.activation(tanh_h[:], psum[s][:, 0:H], ACT.Tanh, scale=0.5).then_inc(ht_done, 1)

                def hi_g(i, s, first=False):
                    act.wait_ge(gt_done, i + 1)
                    if not first:
                        act.wait_ge(ye_done, 2 * (i - 1))
                    a.activation(gthi[:, s], psum[4][:, 0:H], ACT.Copy).then_inc(gt_hi, 1)

                def evacuate(i, s, first=False):
                    for c in range(2):
                        act.wait_ge(ye_done, 2 * i + c + 1)
                        if not first:
                            act.wait_ge(ye_out[s], 16 * ((i - s) // 2 if isinstance(i, int) else i_half[s]))
                        a.activation(ye[:, s, c * BANK:(c + 1) * BANK], psum[5 + c][:], ACT.Copy).then_inc(ye_evac, 1)

                def store(i, s):
                    act.wait_ge(ye_evac, 2 * (i + 1))
                    act.dma_start(YS[bass.ds(i * P, P), :], ye[:, s]).then_inc(ye_out[s], 16)

                i_half = [0, 0]
                act.wait_ge(rt_ready, 1)
                slot, expert = slot_of(0), expert_of(0)
                for c in range(2):
                    hi_ab(0, 0, c, slot, expert, True)
                hi_x(0, 0, True)
                tanh(0, 0, True)
                hi_c(0, 0, slot, True)
                slot, expert = slot_of(1), expert_of(1)
                for c in range(2):
                    hi_ab(1, 1, c, slot, expert, True)
                hi_x(1, 1, True)

                def step5(i, s, two=True, one=True, n=None):
                    if one:
                        slot_c = slot_of(i + 1)
                    if two:
                        slot, expert = slot_of(i + 2), expert_of(i + 2)
                    if n != 0:
                        evacuate(i - 1, 1 - s, n in (1, 2))
                        store(i - 1, 1 - s)
                    if one:
                        hi_c(i + 1, 1 - s, slot_c, n == 0)
                    if two:
                        hi_ab(i + 2, s, 0, slot, expert)
                    hi_g(i, s, n in (0, 1))
                    if two:
                        hi_ab(i + 2, s, 1, slot, expert)
                        hi_x(i + 2, s)
                    if one:
                        tanh(i + 1, 1 - s)
                for n in range(3):
                    step5(n, n % 2, n=n)
                with act.Fori(1, (MT - 3) // 2) as n:
                    i_half[1], i_half[0] = n, n
                    step5(2 * n + 1, 1)
                    step5(2 * n + 2, 0)
                step5(MT - 2, 1, two=False)
                step5(MT - 1, 0, two=False, one=False)
                evacuate(MT - 1, 0)
                store(MT - 1, 0)

            @block.vector
            def _(dve):
                v = nc.vector
                step = chain(dve, "stage5_step")

                def flat(t):
                    return t.rearrange("p a b -> p (a b)")
                step(v.tensor_reduce(red[:, 0, :], LOGITS[:, 0:NT * X].rearrange("p (j e) -> p j e", e=X), AX.X, ALU.max))
                v.tensor_tensor(lg[:], LOGITS[:, 0:NT * X].rearrange("p (j e) -> p j e", e=X),
                                red[:, 0, :].unsqueeze(2).to_broadcast([P, NT, X]), ALU.subtract).then_inc(rt_lg, 1)
                dve.wait_ge(rt_exp, 1)
                step(v.tensor_reduce(red[:, 1, :], pr[:], AX.X, ALU.add))
                step(v.reciprocal(red[:, 2, :], red[:, 1, :]))
                step(v.tensor_tensor(pr[:], pr[:], red[:, 2, :].unsqueeze(2).to_broadcast([P, NT, X]), ALU.mult))
                for j in range(NT):
                    ins = v.max(top[:, j, :], pr[:, j, :])
                step(ins)
                for j in range(NT):
                    ins = v.max_index(top_i[:, j, :], top[:, j, :], pr[:, j, :])
                step(ins)
                step(v.tensor_copy(sel_f[:], top_i[:, :, 0:2]))
                step(v.tensor_scalar(past[:, 0:1], lanes[:], float(LASTP), float(X), ALU.is_ge, ALU.mult))
                step(v.tensor_scalar(sel_f[:, NT - 1, :], sel_f[:, NT - 1, :], past[:, 0:1], None, ALU.add))
                for e in range(X):
                    ins = v.tensor_scalar(oh_e[:, e, :], flat(sel_f[:]), float(e), None, ALU.is_equal)
                ins.then_inc(rt_oh, 1)
                step(v.memset(ones_e[:], 1.0))
                dve.wait_ge(rt_tot, 1)
                TOT = psum[4][:, 0:X * C2].rearrange("p (e c) -> p e c", e=X)
                for e in range(X):
                    ins = v.tensor_tensor_scan(bef[:, e, :], ones_e[:], TOT[:, e, :], 0.0, ALU.mult, ALU.add)
                step(ins)
                step(v.tensor_copy(ce[:, 0, :], bef[:, :, C2 - 1]))
                step(v.tensor_tensor(bef[:], bef[:], TOT, ALU.subtract))
                step(v.tensor_scalar(ce_i[:, 0, :], ce[:, 0, :], float(P - 1), None, ALU.add))
                step(v.tensor_scalar(ce_i[:, 1, :], ce_i[:, 0, :], 7, 7, ALU.arith_shift_right, ALU.logical_shift_left))
                step(v.tensor_copy(ce[:, 1, :], ce_i[:, 1, :]))
                step(v.tensor_tensor_scan(ce[:, 2, :], ones_e[:, 0:X], ce[:, 1, :], 0.0, ALU.mult, ALU.add))
                step(v.tensor_tensor(ce[:, 3, :], ce[:, 2, :], ce[:, 1, :], ALU.subtract))
                step(v.tensor_scalar(te[:, 0, :], iota[:, 0:MTE], float(P), None, ALU.mult))
                step(v.memset(te[:, 1, :], 0.0))
                for e in range(1, X):
                    step(v.scalar_tensor_tensor(te[:, 1, :], te[:, 0, :], ce[:, 3, e:e + 1], te[:, 1, :],
                                                ALU.is_ge, ALU.add))
                step(v.tensor_copy(tile_expert[:], te[:, 1, :]))
                step(v.tensor_scalar(tile_slot[:], tile_expert[:], 1, None, ALU.bitwise_and))
                v.tensor_scalar(first_tile[:], ce[:, 3, :], 1.0 / P, None, ALU.mult).then_inc(rt_ready, 1)
                dve.wait_ge(rt_rank, 1)
                step(v.tensor_tensor(wit[:], bef[:], psum[5][:, 0:X * C2].rearrange("p (e c) -> p e c", e=X), ALU.add))
                step(v.tensor_tensor(wit[:], wit[:], ce[:, 3, :].unsqueeze(2).to_broadcast([P, X, C2]), ALU.add))
                step(v.tensor_tensor(wit[:], wit[:], oh_e[:], ALU.mult))
                step(v.tensor_reduce(pos[:], wit[:].rearrange("p e c -> p c e"), AX.X, ALU.add))
                step(v.tensor_copy(place_i[:], pos[:]))
                step(v.tensor_scalar(past[:, 1:2], past[:, 0:1], float(P * 256 // X), None, ALU.mult))
                step(v.tensor_scalar(pos[:, C2 - 2:C2], pos[:, C2 - 2:C2], past[:, 1:2], None, ALU.add))
                step(v.tensor_copy(pos_i[:, 0, :], pos[:]))
                step(v.tensor_scalar(pos_i[:, 1, :], pos_i[:, 0, :], P - 1, None, ALU.bitwise_and))
                step(v.tensor_scalar(pos_i[:, 2, :], pos_i[:, 0, :], 7, None, ALU.arith_shift_right))
                step(v.tensor_copy(p_lo[:], pos_i[:, 1, :]))
                step(v.tensor_copy(p_hi[:], pos_i[:, 2, :]))
                dve.wait_ge(rt_iota, 1)
                for c in range(C2):
                    v.tensor_scalar(poh_lo[:, c], iota[:, 0:P], p_lo[:, c:c + 1], None, ALU.is_equal)
                    ins = v.tensor_scalar(poh_hi[:, c], iota[:, 0:MTE], p_hi[:, c:c + 1], tok_f[:, c // 2:c // 2 + 1],
                                          ALU.is_equal, ALU.mult)
                ins.then_inc(rt_poh, 1)
                dve.wait_ge(rt_tok, 1)
                step(v.tensor_scalar(tok_s[:], psum[7][:, 0:MTE], -1.0, 0.0, ALU.add, ALU.max))
                v.tensor_copy(tok_i[:], tok_s[:]).then_inc(rt_idx, 1)

                def slot_of(i):
                    return dve.value_load(tile_slot[0:1, bass.ds(i, 1)], min_val=0, max_val=1)

                def lo_ab(i, s, c, slot):
                    dve.wait_ge(ab_hi[c], i + 1)
                    v.tensor_tensor(w13lo[s][:, 4 * c:4 * c + 4, :],
                                    raw13[:, bass.ds(slot, 1), 4 * c:4 * c + 4, :].rearrange("p a k n -> p (a k) n"),
                                    w13hi[s][:, 4 * c:4 * c + 4, :].bitcast(F32), ALU.subtract).then_inc(ab_lo[c], 1)

                def lo_x(i, s):
                    for g in range(2):
                        dve.wait_ge(xt_hi, 2 * i + g + 1)
                        at = (slice(None), s, slice(g * BANK, (g + 1) * BANK))
                        v.tensor_tensor(xtlo[at], psum[2 + g][:], xthi[at].bitcast(F32), ALU.subtract).then_inc(xt_lo, 1)

                def silu(i, s, first=False):
                    dve.wait_ge(ht_done, i + 1)
                    v.scalar_tensor_tensor(act_a[:], tanh_h[:], 1.0, psum[s][:, 0:H], ALU.add, ALU.mult).then_inc(a_done, 1)
                    dve.wait_ge(a_done, i + 1)
                    if not first:
                        dve.wait_ge(gt_done, i - 1)
                    v.scalar_tensor_tensor(act_g[:, s], act_a[:], 0.5, psum[s][:, H:2 * H],
                                           ALU.mult, ALU.mult).then_inc(g_done, 1)

                def lo_g(i, s):
                    dve.wait_ge(gt_hi, i + 1)
                    v.tensor_tensor(gtlo[:, s], psum[4][:, 0:H], gthi[:, s].bitcast(F32), ALU.subtract).then_inc(gt_lo, 1)

                dve.wait_ge(rt_ready, 1)
                slot = slot_of(0)
                for c in range(2):
                    lo_ab(0, 0, c, slot)
                lo_x(0, 0)
                silu(0, 0, True)
                slot = slot_of(1)
                for c in range(2):
                    lo_ab(1, 1, c, slot)
                lo_x(1, 1)

                def step5(i, s, two=True, one=True, first=False):
                    if two:
                        slot = slot_of(i + 2)
                        lo_ab(i + 2, s, 0, slot)
                    lo_g(i, s)
                    if two:
                        lo_ab(i + 2, s, 1, slot)
                        lo_x(i + 2, s)
                    if one:
                        silu(i + 1, 1 - s, first)
                step5(0, 0, first=True)
                with dve.Fori(0, (MT - 3) // 2) as n:
                    step5(2 * n + 1, 1)
                    step5(2 * n + 2, 0)
                step5(MT - 2, 1, two=False)
                step5(MT - 1, 0, two=False, one=False)
                for j in range(NT):
                    dve.wait_ge(y1_in[j % YT], 16 * (j // YT + 1))
                    dve.wait_ge(x1_in[j // YT], 16)
                    v.scalar_tensor_tensor(x1b[:, j], chosen_y[:, j % YT, 0], top[:, j, 0:1], x1b[:, j],
                                           ALU.mult, ALU.add).then_inc(half_done, 1)
                    dve.wait_ge(half_done, j + 1)
                    dve.wait_ge(y2_in[j % YT], 16 * (j // YT + 1))
                    v.scalar_tensor_tensor(x1b[:, j], chosen_y[:, j % YT, 1], top[:, j, 1:2], x1b[:, j],
                                           ALU.mult, ALU.add).then_inc(res_done, 1)

            @block.tensor
            def _(pe):
                pe.wait_ge(rt_oh, 1)
                pe.matmul(psum[4][:, 0:X * C2], ones[:], oh_e[:].rearrange("p e c -> p (e c)"),
                          start=True, stop=True).then_inc(rt_tot, 1)
                pe.matmul(psum[5][:, 0:X * C2], tri[:], oh_e[:].rearrange("p e c -> p (e c)"),
                          start=True, stop=True).then_inc(rt_rank, 1)
                pe.wait_ge(rt_poh, 1)
                for c in range(C2):
                    ins = pe.matmul(psum[7][:, 0:MTE], poh_lo[:, c], poh_hi[:, c], start=(c == 0), stop=(c == C2 - 1))
                ins.then_inc(rt_tok, 1)

                def turn_x(i, s, first=False):
                    pe.wait_ge(xg_in[s], 16 * (i // 2 + 1 if isinstance(i, int) else half_of[s] + 1))
                    for g in range(2):
                        if not first:
                            pe.wait_ge(xt_lo, 2 * (i - 1) + g + 1)
                        for k in range(4):
                            c = 4 * g + k
                            ins = pe.transpose(psum[2 + g][:, k * P:(k + 1) * P], xg[:, s, c * P:(c + 1) * P], ident[:])
                        ins.then_inc(xt_done, 1)

                def hidden(i, s, c, first=False):
                    pe.wait_ge(ab_lo[c], i + 1)
                    pe.wait_ge(xt_lo, 2 * (i + 1))
                    if not first:
                        pe.wait_ge(g_done, i - 1)
                    for k in range(4 * c, 4 * c + 4):
                        at = slice(k * P, (k + 1) * P)
                        pe.matmul(psum[s][:], xthi[:, s, at], w13hi[s][:, k], start=(k == 0), stop=False)
                        pe.matmul(psum[s][:], xthi[:, s, at], w13lo[s][:, k], start=False, stop=False)
                        ins = pe.matmul(psum[s][:], xtlo[:, s, at], w13hi[s][:, k], start=False, stop=(k == KC - 1))
                    if c == 1:
                        ins.then_inc(h_done, 1)

                def turn_g(i, s, first=False):
                    pe.wait_ge(g_done, i + 1)
                    if not first:
                        pe.wait_ge(gt_lo, i)
                    for k in range(HC):
                        ins = pe.transpose(psum[4][:, k * P:(k + 1) * P], act_g[:, s, k * P:(k + 1) * P], ident[:])
                    ins.then_inc(gt_done, 1)

                def outputs(i, s, first=False):
                    pe.wait_ge(c_lo, i + 1)
                    pe.wait_ge(gt_lo, i + 1)
                    for c in range(2):
                        if not first:
                            pe.wait_ge(ye_evac, 2 * (i - 1) + c + 1)
                        for k in range(HC):
                            at, cols = slice(k * P, (k + 1) * P), slice(c * BANK, (c + 1) * BANK)
                            pe.matmul(psum[5 + c][:], gthi[:, s, at], w2hi[s][:, k, cols], start=(k == 0), stop=False)
                            pe.matmul(psum[5 + c][:], gthi[:, s, at], w2lo[s][:, k, cols], start=False, stop=False)
                            ins = pe.matmul(psum[5 + c][:], gtlo[:, s, at], w2hi[s][:, k, cols], start=False,
                                            stop=(k == HC - 1))
                        ins.then_inc(ye_done, 1)

                half_of = [0, 0]
                turn_x(0, 0, True)
                hidden(0, 0, 0, True)
                hidden(0, 0, 1, True)
                turn_x(1, 1)

                def step5(i, s, two=True, one=True, first=False):
                    if one:
                        hidden(i + 1, 1 - s, 0, first)
                    turn_g(i, s, first)
                    if one:
                        hidden(i + 1, 1 - s, 1, first)
                    if two:
                        turn_x(i + 2, s)
                    outputs(i, s, first)
                step5(0, 0, first=True)
                with pe.Fori(0, (MT - 3) // 2) as n:
                    half_of[1], half_of[0] = n + 1, n + 2
                    step5(2 * n + 1, 1)
                    step5(2 * n + 2, 0)
                step5(MT - 2, 1, two=False)
                step5(MT - 1, 0, two=False, one=False)


_INS = ["x", "src", "dst", "edge_type_8", "L0_gnn_weight", "L0_gnn_root", "L0_gnn_bias", "L0_gnn_w_gate",
        "L0_gnn_b_gate", "L0_ffn_gate_w", "L0_ffn_w1", "L0_ffn_w2", "L0_ffn_w3"]


def kernel(**inputs):
    import numpy as _np
    import concourse.bacc as _bacc
    from concourse import mybir as _mybir
    from concourse.bass_utils import run_bass_kernel_spmd as _run

    nc = _bacc.Bacc("TRN2", target_bir_lowering=False, num_devices=1)
    arrays, args = {}, []
    for name in _INS:
        a = _np.ascontiguousarray(inputs[name])
        arrays[f"in_{name}"] = a
        args.append(nc.dram_tensor(f"in_{name}", a.shape, _mybir.dt.from_np(a.dtype), kind="ExternalInput").ap())
    result = nc.dram_tensor("result", inputs["x"].shape, _mybir.dt.float32, kind="ExternalOutput").ap()
    build_program(nc, *args, result)
    r = _run(nc, [arrays], core_ids=[0])
    return r.results[0]["result"]
```

```python
import numpy as np
import concourse.bass as bass
from concourse import mybir
from contextlib import ExitStack

F32 = mybir.dt.float32
F32R = mybir.dt.float32r
BF16 = mybir.dt.bfloat16
I32 = mybir.dt.int32
U32 = mybir.dt.uint32
ALU = mybir.AluOpType
ACT = mybir.ActivationFunctionType
AX = mybir.AxisListType

P = 128
BANK = 512
EPS = 1e-5
GROUP = 2


def shapes(x, src, weight, w1, gate_w):
    s = {}
    s["N"], s["D"] = x.shape
    s["E"] = src.shape[0]
    s["R"] = weight.shape[0]
    s["X"], _, s["H"] = w1.shape
    s["NT"] = -(-s["N"] // P)
    s["NP"] = s["NT"] * P
    s["KC"] = s["D"] // P
    s["HC"] = s["H"] // P
    s["EFULL"] = s["E"] // P
    s["EREST"] = s["E"] - s["EFULL"] * P
    s["ECOLS"] = 168
    pad = GROUP * P
    groups = (s["E"] + s["NT"] * (pad - 1)) // pad
    s["ET"] = -(-groups // 2) * 2 * GROUP
    s["MT"] = (2 * s["N"] + s["X"] * (P - 1)) // P
    s["MTE"] = s["MT"] + s["MT"] % 2
    return s


def build_program(nc, x, src, dst, edge_type, weight, root, bias, w_gate, b_gate,
                  gate_w, w1, w2, w3, out):
    s = shapes(x, src, weight, w1, gate_w)
    N, D, R, X, H, NT, NP, KC, HC = (s[k] for k in ("N", "D", "R", "X", "H", "NT", "NP", "KC", "HC"))
    E, EFULL, EREST, ECOLS, ET, MT, MTE = (
        s[k] for k in ("E", "EFULL", "EREST", "ECOLS", "ET", "MT", "MTE"))
    LASTP = N - (NT - 1) * P
    HALF = D // 2
    assert ECOLS >= EFULL + (EREST > 0) and HALF == BANK and D == 1024 and R == 8 and X == 8
    KEYS = NP * R
    KHI = KEYS // 256

    with ExitStack() as ctx:
        psum = [ctx.enter_context(nc.psum_tensor(f"bank{i}", [P, BANK], F32)) for i in range(8)]

        def sem(name):
            return ctx.enter_context(nc.semaphore(name))

        size = {F32: 4, F32R: 4, BF16: 2, I32: 4, U32: 4}

        class Zone:
            def __init__(self, start, length):
                self.at, self.end, self.start = start, start + length, start

            def put(self, name, shape, dt):
                n = size[dt] * int(np.prod(shape[1:]))
                n = -(-n // 32) * 32
                assert self.at + n <= self.end, (name, self.at + n - self.end)
                t = nc.alloc_sbuf_tensor_at(name, shape, dt, offset=self.at)
                self.at += n
                return t

        KB = 1024
        base = -(-nc.sbuf_base // 32) * 32
        LIMIT = nc.sbuf_base + nc.sbuf_bytes_remaining
        keep = Zone(base, 13 * KB // 2)
        OFF_T = base + 13 * KB // 2
        OFF_STAGE = OFF_T + 80 * KB
        OFF_YOUT = OFF_STAGE + 8 * KB
        OFF_W0 = OFF_YOUT + 8 * KB
        OFF_W1 = OFF_W0 + 32 * KB
        OFF_END = OFF_W1 + 32 * KB

        ident = keep.put("ident", [P, P], F32)
        iota = keep.put("iota", [P, 257], F32)
        lanes = keep.put("lanes", [P, 1], F32)
        mean = keep.put("mean", [P, NT], F32)
        rstd = keep.put("rstd", [P, NT], F32)
        edge_row = keep.put("edge_row", [P, ET], I32)
        edge_dst = keep.put("edge_dst", [P, ET], F32)
        edge_key = keep.put("edge_key", [P, ET], I32)
        edge_w = keep.put("edge_w", [P, ET], F32)
        tile_block = keep.put("tile_block", [P, ET], I32)
        tri = keep.put("tri", [P, P], BF16)
        ones = keep.put("ones", [P, P], BF16)

        acc = nc.alloc_sbuf_tensor_at("acc", [P, NT * D], F32, offset=OFF_END)

        def dram(name, shape, dt=F32):
            return nc.dram_tensor(name, shape, dt, kind="Internal").ap()

        Y = dram("Y", (R * NP, D))
        YX = dram("YX", (2, NP, D))
        INV = dram("INV", (KEYS, 1))
        XN2 = dram("XN2", (NP, D))
        X1 = dram("X1", (NP, D))
        YS = dram("YS", (MT * P, D))

        def rows(j):
            return LASTP if j == NT - 1 else P

        vector_step, count = sem("vector_step"), [0]

        def chain(eng):
            done = vector_step

            def step(ins):
                count[0] += 1
                ins.then_inc(done, 1)
                eng.wait_ge(done, count[0])
            return step

        xhi = nc.alloc_sbuf_tensor_at("xhi", [P, KC, NP], F32R, offset=OFF_T)
        xlo = nc.alloc_sbuf_tensor_at("xlo", [P, KC, NP], F32R, offset=OFF_T + 4 * KC * NP)
        z2 = Zone(OFF_END, LIMIT - OFF_END)
        place_lo = z2.put("place_lo", [P, ECOLS], F32)
        place_hi = z2.put("place_hi", [P, ECOLS], F32)
        val_src = z2.put("val_src", [P, ECOLS], F32)
        val_dst = z2.put("val_dst", [P, ECOLS], F32)
        key_hi = z2.put("key_hi", [P, ECOLS], F32)
        key_lo = z2.put("key_lo", [P, ECOLS], F32)
        blk_base = z2.put("blk_base", [P, NT], F32)
        z2t = Zone(z2.at, LIMIT - z2.at)
        onehot = z2t.put("onehot", [P, NT, ECOLS], BF16)
        before = z2t.put("before", [P, NT, ECOLS], F32)
        within = z2t.put("within", [P, 3 * ECOLS], F32)
        ones_f = z2t.put("ones_f", [P, ECOLS], F32)
        edge_tmp = z2t.put("edge_tmp", [P, ECOLS], I32)
        dlo = z2t.put("dlo", [P, ECOLS], F32)
        blk = z2t.put("blk", [P, ECOLS], F32)
        typ = z2t.put("typ", [P, ECOLS], F32)
        posf = z2t.put("posf", [P, ECOLS], F32)
        src_i = z2t.put("src_i", [P, ECOLS], I32)
        dst_i = z2t.put("dst_i", [P, ECOLS], I32)
        typ_i = z2t.put("typ_i", [P, ECOLS], I32)
        cnt_f = z2t.put("cnt_f", [P, 3, NT], F32)
        cnt_i = z2t.put("cnt_i", [P, 2, NT], I32)

        XA = 6
        x_first = nc.alloc_sbuf_tensor_at("x_first", [P, XA, D], F32, offset=OFF_W1)
        x_last = z2t.put("x_last", [P, NT - XA, D], F32)
        stat = z2t.put("stat", [P, NT, 2, 6], F32)
        aggr = z2t.put("aggr", [P, NT, 2], F32)
        tmp10 = z2t.put("tmp10", [P, 4, NT], F32)

        def x_tile(j):
            return x_first[:, j] if j < XA else x_last[:, j - XA]

        LN_GROUPS = ((0, 1), (1, 2), (2, 3), (3, 4), (4, 6), (6, 8), (8, NT))
        xin = [sem(f"x_loaded{j}") for j in range(NT)]
        edges_set, edges_in = sem("edges_set"), sem("edges_in")
        consts = sem("consts_ready")
        onehot_ready, totals_done, totals_read, tri_done, tri_read = (
            sem("block_onehot_ready"), sem("column_totals_done"), sem("column_totals_read"),
            sem("ranks_done"), sem("ranks_read"))
        pad_set = sem("pad_rows_set")
        norm_ready, tr_done, hi_done, lo_done = (
            sem("norm_ready"), sem("transposed"), sem("xhi_written"), sem("xlo_written"))
        var_ready, sqrt_ready = sem("var_ready"), sem("sqrt_ready")

        groups = [list(range(a, min(a + 3, NT))) for a in range(0, NT, 3)]
        stage = nc.alloc_sbuf_tensor_at("w_stage", [P, 2, 2, HALF], F32, offset=OFF_STAGE)
        w_early = nc.alloc_sbuf_tensor_at("w_early", [P, 2, 2, HALF], F32, offset=OFF_YOUT)
        yout = nc.alloc_sbuf_tensor_at("y_out", [P, 4, HALF], F32, offset=OFF_YOUT)
        whi = [nc.alloc_sbuf_tensor_at(f"whi{h}", [P, KC, HALF], F32R, offset=o)
               for h, o in enumerate((OFF_W0, OFF_W1))]
        wlo = [nc.alloc_sbuf_tensor_at(f"wlo{h}", [P, KC, HALF], F32R, offset=o + 16 * KB)
               for h, o in enumerate((OFF_W0, OFF_W1))]
        z2b = Zone(z2.at, LIMIT - z2.at)
        CPQ = 7
        SORT_R = ECOLS // (8 * CPQ)
        assert SORT_R * 8 * CPQ == ECOLS
        oh_lo = z2b.put("oh_lo", [P, CPQ, P], F32R)
        oh_val = z2b.put("oh_val", [P, CPQ, 2, ET], F32R)
        oh_khi = z2b.put("oh_khi", [P, CPQ, KHI], BF16)
        oh_klo = z2b.put("oh_klo", [P, CPQ, 256], BF16)
        placed = z2b.put("placed", [P, 2, ET], F32)
        placed_i = z2b.put("placed_i", [P, 3, ET], I32)
        tfl = z2b.put("tfl", [P, 4, ET], F32)
        inv = z2b.put("inv", [KHI, 256], F32)
        YB, PLACE_BANK, COUNT_BANK = 4, psum[6], psum[7]

        w_in = [sem(f"w_stage_loaded{i}") for i in range(2)]
        early_in = [sem(f"w_early_loaded{i}") for i in range(2)]

        def staged(r, h, q):
            if isinstance(r, int) and (r, h) == (0, 0):
                return (stage[:, q], w_in[q], 16) if q < 2 else (w_early[:, q - 2], early_in[q - 2], 16)
            return stage[:, q % 2], w_in[q % 2], 16 * (r * 4 + h * 2 + q // 2)
        w_hi, w_lo = sem("w_hi_written"), sem("w_lo_written")
        y_ready, y_evac = sem("y_ready"), sem("y_evacuated")
        y_out = [sem(f"y_stored{i}") for i in range(YB)]
        cols_ready, cols_used = sem("onehots_ready"), sem("onehots_used")
        acc_set, inv_ready, inv_out, key_ready, w_gathered = (
            sem("acc_set"), sem("inv_ready"), sem("inv_stored"), sem("keys_ready"), sem("edge_w_gathered"))

        RANK_AFTER = ((0, NT - 1), (1, 3))
        FIRST_SPLITS, FIRST_LOADS = (3, 5, 7, 8), (4, 6, 8, 9)

        def w_rows(w, q, h):
            return w[2 * q * P:(2 * q + 2) * P, h * HALF:(h + 1) * HALF].rearrange("(k p) n -> p k n", p=P)

        with nc.Block() as block:
            @block.sync
            def _(sp):
                def load(r, h, q, first=False):
                    n = r * 8 + h * 4 + q
                    if not first:
                        sp.wait_ge(w_lo, n - 1)
                    w = (weight[bass.ds(r, 1)].rearrange("a k n -> (a k) n") if not isinstance(r, int)
                         else root if r == R else weight[r])
                    place, arrived, _ = staged(r, h, q)
                    sp.dma_start(place, w_rows(w, q, h)).then_inc(arrived, 16)

                def store(r, h, j):
                    m = r * 2 * NT + h * NT + j
                    sp.wait_ge(y_evac, m + 1)
                    sp.dma_start(Y[bass.ds(r * NP + j * P, P), h * HALF:(h + 1) * HALF],
                                 yout[:, (h * NT + j) % YB]).then_inc(y_out[(h * NT + j) % YB], 16)

                def load_x(*tiles):
                    for j in tiles:
                        if j == NT - 1:
                            sp.wait_ge(pad_set, 1)
                        sp.dma_start(x_tile(j)[:rows(j)], x[j * P:j * P + rows(j), :]).then_inc(xin[j], 16)

                load_x(0)
                load(0, 0, 0, True)
                load_x(1)
                load(0, 0, 1, True)
                load(0, 0, 2, True)
                load(0, 0, 3, True)
                load_x(*range(2, NT))
                for q in (0, 1):
                    load(0, 1, q)

                def relation(r, first=False, last=False):
                    for h in range(2):
                        after = FIRST_LOADS if first and h == 0 else (0, 2, 4, 6)
                        for j in range(NT):
                            store(r, h, j)
                            if j in after:
                                q = after.index(j) + 2
                                r2, h2 = (r, h + 1) if q < 4 else (r, h + 2)
                                if h2 >= 2:
                                    r2, h2 = r2 + 1, h2 - 2
                                if last and h2 == 1 and h == 1:
                                    continue
                                load(r2, h2, q % 4)
                relation(0, first=True)
                with sp.Fori(1, R - 1) as r:
                    relation(r)
                relation(R - 1, last=True)
                for i in range(YB):
                    sp.wait_ge(y_out[i], 16 * (R * 2 * NT // YB))

            @block.scalar
            def _(act):
                def split_hi(r, h, q, first=False):
                    n = r * 8 + h * 4 + q
                    place, arrived, count = staged(r, h, q)
                    act.wait_ge(arrived, count)
                    if not first and q == 0:
                        act.wait_ge(y_ready, (r * 2 + h - 1) * NT)
                    nc.scalar.activation(whi[h][:, 2 * q:2 * q + 2, :], place, ACT.Copy).then_inc(w_hi, 1)

                def evacuate(r, h, j, first=False):
                    m = r * 2 * NT + h * NT + j
                    slot = (h * NT + j) % YB
                    act.wait_ge(y_ready, m + 1)
                    if not (first and h * NT + j < YB):
                        act.wait_ge(y_out[slot], 16 * (r * (2 * NT // YB) + (h * NT + j) // YB))
                    nc.scalar.activation(yout[:, slot], psum[slot][:], ACT.Copy).then_inc(y_evac, 1)

                def root_of(g):
                    a, b = LN_GROUPS[g]
                    act.wait_ge(var_ready, g + 1)
                    nc.scalar.activation(tmp10[:, 1, a:b], tmp10[:, 0, a:b], ACT.Sqrt).then_inc(sqrt_ready, 1)

                def x_hi(j):
                    for n in (2 * j, 2 * j + 1):
                        g = n % 2
                        act.wait_ge(tr_done, n + 1)
                        nc.scalar.activation(xhi[:, 4 * g:4 * g + 4, j * P:(j + 1) * P],
                                             psum[4 + n % 4][:].rearrange("p (k n) -> p k n", k=4),
                                             ACT.Copy).then_inc(hi_done, 1)

                root_of(0)
                split_hi(0, 0, 0, True)
                root_of(1)
                split_hi(0, 0, 1, True)
                x_hi(0)
                split_hi(0, 0, 2, True)
                split_hi(0, 0, 3, True)
                x_hi(1)
                root_of(2)
                root_of(3)

                def relation(r, first=False):
                    for h in range(2):
                        beside_x = first and h == 0
                        after = FIRST_SPLITS if beside_x else (0, 2, 4, 6)
                        for j in range(NT):
                            evacuate(r, h, j, first)
                            if beside_x and j + 2 < NT:
                                x_hi(j + 2)
                            if beside_x and j + 4 < len(LN_GROUPS):
                                root_of(j + 4)
                            if j in after:
                                split_hi(*((r, 1) if h == 0 else (r + 1, 0)), after.index(j), first and h == 0)
                relation(0, first=True)
                with act.Fori(1, R - 1) as r:
                    relation(r)
                relation(R - 1)

            @block.vector
            def _(dve):
                v = nc.vector

                def split_lo(r, h, q):
                    dve.wait_ge(w_hi, r * 8 + h * 4 + q + 1)
                    v.tensor_tensor(wlo[h][:, 2 * q:2 * q + 2, :], staged(r, h, q)[0],
                                    whi[h][:, 2 * q:2 * q + 2, :].bitcast(F32), ALU.subtract).then_inc(w_lo, 1)

                def columns(r, part, first=False):
                    if not first:
                        dve.wait_ge(cols_used, (r - 1) * 8 + part)
                    for i in range(CPQ):
                        c = (r - 1) * 8 * CPQ + part * CPQ + i
                        at = bass.ds(c, 1)
                        v.tensor_scalar(oh_lo[:, i], iota[:, 0:P], place_lo[:, at], None, ALU.is_equal)
                        v.tensor_scalar(oh_val[:, i, 0], iota[:, 0:ET], place_hi[:, at], val_src[:, at],
                                        ALU.is_equal, ALU.mult)
                        v.tensor_scalar(oh_val[:, i, 1], iota[:, 0:ET], place_hi[:, at], val_dst[:, at],
                                        ALU.is_equal, ALU.mult)
                        v.tensor_scalar(oh_khi[:, i], iota[:, 0:KHI], key_hi[:, at], None, ALU.is_equal)
                        ins = v.tensor_scalar(oh_klo[:, i], iota[:, 0:256], key_lo[:, at], None, ALU.is_equal)
                    ins.then_inc(cols_ready, 1)

                def edge_places():
                    step = step1
                    dve.wait_ge(edges_in, 16 * 6)
                    dve.wait_ge(consts, 5)
                    v.tensor_copy(val_src[:], src_i[:])
                    step(v.tensor_copy(typ[:], typ_i[:]))
                    step(v.tensor_scalar(edge_tmp[:], dst_i[:], 7, None, ALU.arith_shift_right))
                    step(v.tensor_copy(blk[:], edge_tmp[:]))
                    for j in range(NT):
                        ins = v.tensor_scalar(onehot[:, j, :], blk[:], float(j), None, ALU.is_equal)
                    ins.then_inc(onehot_ready, 1)
                    step(v.tensor_scalar(edge_tmp[:], dst_i[:], P - 1, None, ALU.bitwise_and))
                    step(v.tensor_copy(dlo[:], edge_tmp[:]))
                    step(v.tensor_scalar(dlo[:], dlo[:], 1.0, float(R), ALU.add, ALU.mult))
                    step(v.tensor_tensor(val_dst[:], dlo[:], typ[:], ALU.add))
                    step(v.tensor_scalar(edge_tmp[:], dst_i[:], 5, None, ALU.arith_shift_right))
                    step(v.tensor_copy(key_hi[:], edge_tmp[:]))
                    step(v.tensor_scalar(edge_tmp[:], dst_i[:], 31, None, ALU.bitwise_and))
                    step(v.tensor_copy(dlo[:], edge_tmp[:]))
                    step(v.scalar_tensor_tensor(key_lo[:], dlo[:], float(R), typ[:], ALU.mult, ALU.add))
                    for g, js in enumerate(groups):
                        dve.wait_ge(totals_done, g + 1)
                        for n, j in enumerate(js):
                            step(v.tensor_tensor_scan(before[:, j, :], ones_f[:], psum[4 + g][:, n * ECOLS:(n + 1) * ECOLS],
                                                      0.0, ALU.mult, ALU.add))
                            step(v.tensor_copy(cnt_f[:, 0, j:j + 1], before[:, j, ECOLS - 1:ECOLS]))
                            ins = v.tensor_tensor(before[:, j, :], before[:, j, :],
                                                  psum[4 + g][:, n * ECOLS:(n + 1) * ECOLS], ALU.subtract)
                            step(ins)
                    shift = (GROUP * P).bit_length() - 1
                    step(v.tensor_scalar(cnt_i[:, 0, :], cnt_f[:, 0, :], float(GROUP * P - 1), None, ALU.add))
                    step(v.tensor_scalar(cnt_i[:, 1, :], cnt_i[:, 0, :], shift, shift,
                                         ALU.arith_shift_right, ALU.logical_shift_left))
                    step(v.tensor_copy(cnt_f[:, 1, :], cnt_i[:, 1, :]))
                    step(v.tensor_tensor_scan(cnt_f[:, 2, :], ones_f[:, 0:NT], cnt_f[:, 1, :], 0.0, ALU.mult, ALU.add))
                    step(v.tensor_tensor(blk_base[:], cnt_f[:, 2, :], cnt_f[:, 1, :], ALU.subtract))
                    v.tensor_copy(cnt_f[:, 0, :], cnt_f[:, 2, :]).then_inc(totals_read, 1)
                    step(v.tensor_scalar(posf[:], blk[:], 0.0, float(1 << 16), ALU.is_lt, ALU.mult))
                    for g, js in enumerate(groups):
                        dve.wait_ge(tri_done, g + 1)
                        w = len(js) * ECOLS
                        step(v.tensor_tensor(within[:, :w], psum[4 + g][:, :w],
                                             before[:, js[0]:js[-1] + 1, :].rearrange("p j c -> p (j c)"), ALU.add))
                        for n, j in enumerate(js):
                            cut = within[:, n * ECOLS:(n + 1) * ECOLS]
                            step(v.scalar_tensor_tensor(cut, cut, blk_base[:, j:j + 1], onehot[:, j, :],
                                                        ALU.add, ALU.mult))
                            step(v.tensor_tensor(posf[:], posf[:], cut, ALU.add))
                    v.tensor_copy(edge_tmp[:], posf[:]).then_inc(tri_read, 1)
                    dve.wait_ge(tri_read, 1)
                    step(v.tensor_scalar(dst_i[:], edge_tmp[:], P - 1, None, ALU.bitwise_and))
                    step(v.tensor_copy(place_lo[:], dst_i[:]))
                    step(v.tensor_scalar(dst_i[:], edge_tmp[:], 7, None, ALU.arith_shift_right))
                    step(v.tensor_copy(place_hi[:], dst_i[:]))

                step1 = chain(dve)
                v.memset(x_last[96:P, NT - 1 - XA, :], 0.0).then_inc(pad_set, 1)
                step1(v.memset(src_i[:], 0))
                step1(v.memset(typ_i[:], 0))
                v.memset(dst_i[:], -1).then_inc(edges_set, 1)
                step1(v.memset(ones_f[:], 1.0))

                def normalize(g):
                    a, b = LN_GROUPS[g]
                    for j in range(a, b):
                        dve.wait_ge(xin[j], 16)
                        v.bn_stats(stat[:, j, 0, :], x_tile(j)[:, 0:HALF])
                        step1(v.bn_stats(stat[:, j, 1, :], x_tile(j)[:, HALF:D]))
                        step1(v.bn_aggr(aggr[:, j, :], stat[:, j, :, :].rearrange("p a b -> p (a b)")))
                    v.tensor_scalar(tmp10[:, 0, a:b], aggr[:, a:b, 1], EPS, None, ALU.add).then_inc(var_ready, 1)
                    step1(v.tensor_copy(mean[:, a:b], aggr[:, a:b, 0]))
                    dve.wait_ge(sqrt_ready, g + 1)
                    dve.wait_ge(var_ready, g + 1)
                    step1(v.reciprocal(tmp10[:, 2, a:b], tmp10[:, 1, a:b]))
                    step1(v.tensor_tensor(tmp10[:, 3, a:b], tmp10[:, 2, a:b], tmp10[:, 2, a:b], ALU.mult))
                    step1(v.tensor_tensor(tmp10[:, 3, a:b], tmp10[:, 3, a:b], tmp10[:, 0, a:b], ALU.mult))
                    step1(v.tensor_scalar(tmp10[:, 3, a:b], tmp10[:, 3, a:b], -0.5, 1.5, ALU.mult, ALU.add))
                    step1(v.tensor_tensor(rstd[:, a:b], tmp10[:, 3, a:b], tmp10[:, 2, a:b], ALU.mult))
                    for j in range(a, b):
                        v.tensor_scalar(x_tile(j), x_tile(j), mean[:, j:j + 1], rstd[:, j:j + 1],
                                        ALU.subtract, ALU.mult).then_inc(norm_ready, 1)

                def x_lo(*tiles):
                    for n in (n for j in tiles for n in (2 * j, 2 * j + 1)):
                        j, g = n // 2, n % 2
                        dve.wait_ge(hi_done, n + 1)
                        at = (slice(None), slice(4 * g, 4 * g + 4), slice(j * P, (j + 1) * P))
                        v.tensor_tensor(xlo[at], psum[4 + n % 4][:].rearrange("p (k n) -> p k n", k=4),
                                        xhi[at].bitcast(F32), ALU.subtract).then_inc(lo_done, 1)

                normalize(0)
                split_lo(0, 0, 0)
                normalize(1)
                split_lo(0, 0, 1)
                x_lo(0)
                split_lo(0, 0, 2)
                split_lo(0, 0, 3)
                x_lo(1)
                normalize(2)
                normalize(3)
                for j in range(NT):
                    if j + 2 < NT:
                        x_lo(j + 2)
                    if j + 4 < len(LN_GROUPS):
                        normalize(j + 4)
                    if j in FIRST_SPLITS:
                        split_lo(0, 1, FIRST_SPLITS.index(j))
                edge_places()

                def relation(r, sorts, start=False, first=False):
                    for h in range(2):
                        for q in range(4):
                            if sorts:
                                columns(r, 4 * h + q, first and h * 4 + q == 0)
                            if not (start and h == 0):
                                split_lo(*((r, 1) if h == 0 else (r + 1, 0)), q)
                relation(0, False, start=True)
                relation(1, True, first=True)
                with dve.Fori(2, 1 + SORT_R) as r:
                    relation(r, True)
                step = step1
                dve.wait_ge(cols_used, 8 * SORT_R)
                step(v.tensor_copy(placed[:], PLACE_BANK[:, 0:2 * ET].rearrange("p (a t) -> p a t", a=2)))
                step(v.tensor_scalar(inv[:], COUNT_BANK[0:KHI, 0:256], 1.0, None, ALU.max))
                v.reciprocal(inv[:], inv[:]).then_inc(inv_ready, 1)
                step(v.tensor_copy(placed_i[:, 0], placed[:, 1]))
                step(v.tensor_scalar(placed_i[:, 1], placed_i[:, 0], 3, None, ALU.arith_shift_right))
                step(v.tensor_copy(edge_dst[:], placed_i[:, 1]))
                step(v.tensor_scalar(placed_i[:, 2], placed_i[:, 0], R - 1, None, ALU.bitwise_and))
                step(v.tensor_copy(tfl[:, 0], placed_i[:, 2]))
                step(v.scalar_tensor_tensor(edge_row[:], tfl[:, 0], float(NP), placed[:, 0], ALU.mult, ALU.add))
                step(v.tensor_scalar(tfl[:, 1], iota[:, 0:ET], float(P), None, ALU.mult))
                step(v.memset(tfl[:, 2], 0.0))
                for j in range(1, NT):
                    step(v.scalar_tensor_tensor(tfl[:, 2], tfl[:, 1], blk_base[:, j:j + 1], tfl[:, 2],
                                                ALU.is_ge, ALU.add))
                step(v.tensor_copy(tile_block[:], tfl[:, 2]))
                step(v.scalar_tensor_tensor(tfl[:, 3], tfl[:, 2], float(P * R), placed[:, 1], ALU.mult, ALU.add))
                v.tensor_scalar(edge_key[:], tfl[:, 3], -float(R), 0.0, ALU.add, ALU.max).then_inc(key_ready, 1)
                with dve.Fori(1 + SORT_R, R - 1) as r:
                    relation(r, False)
                relation(R - 1, False)

            @block.gpsimd
            def _(pool):
                built = sem("built")
                nc.gpsimd.memset(ident[:], 0.0).then_inc(built, 1)
                nc.gpsimd.memset(tri[:], 1.0).then_inc(built, 1)
                pool.wait_ge(built, 2)
                nc.gpsimd.affine_select(out=ident[:], in_=ident[:], compare_op=ALU.not_equal, fill=1.0,
                                        base=0, pattern=[[-1, P]], channel_multiplier=1).then_inc(consts, 1)
                nc.gpsimd.affine_select(out=tri[:], in_=tri[:], compare_op=ALU.is_gt, fill=0.0,
                                        base=0, pattern=[[1, P]], channel_multiplier=-1).then_inc(consts, 1)
                nc.gpsimd.memset(ones[:], 1.0).then_inc(consts, 1)
                nc.gpsimd.iota(iota[:], pattern=[[1, 257]], base=0, channel_multiplier=0,
                               allow_small_or_imprecise_dtypes=True).then_inc(consts, 1)
                nc.gpsimd.iota(lanes[:], pattern=[[1, 1]], base=0, channel_multiplier=1,
                               allow_small_or_imprecise_dtypes=True).then_inc(consts, 1)
                pool.wait_ge(edges_set, 1)
                for tile, vec in ((src_i, src), (dst_i, dst), (typ_i, edge_type)):
                    pool.dma_start(tile[:, 0:EFULL], vec[0:EFULL * P].rearrange("(p c) -> p c", p=P)
                                   ).then_inc(edges_in, 16)
                    pool.dma_start(tile[0:EREST, EFULL:EFULL + 1],
                                   vec[EFULL * P:E].rearrange("(p c) -> p c", c=1)).then_inc(edges_in, 16)
                pool.wait_ge(inv_ready, 1)
                pool.dma_start(INV.rearrange("(a b) c -> a (b c)", b=256), inv[:]).then_inc(inv_out, 16)
                pool.wait_ge(inv_out, 16)
                pool.wait_ge(key_ready, 1)
                for t in range(ET):
                    nc.gpsimd.indirect_dma_start(
                        out=edge_w[:, t:t + 1], out_offset=None, in_=INV,
                        in_offset=bass.IndirectOffsetOnAxis(ap=edge_key[:, t:t + 1], axis=0)).then_inc(w_gathered, 16)
                for j in range(NT):
                    pool.dma_start(acc[:, j * D:(j + 1) * D], bias.partition_broadcast(P)).then_inc(acc_set, 16)
                pool.wait_ge(w_gathered, 16 * ET)
                pool.wait_ge(acc_set, 16 * NT)

            @block.tensor
            def _(pe):
                def product(r, h, j, first=False):
                    m = r * 2 * NT + h * NT + j
                    slot = (h * NT + j) % YB
                    if first and h == 0:
                        pe.wait_ge(lo_done, 2 * (j + 1))
                    if not (first and h * NT + j < YB):
                        pe.wait_ge(y_evac, m + 1 - YB)
                    at = slice(j * P, (j + 1) * P)
                    for k in range(KC):
                        if j == 0 and k % 2 == 0:
                            pe.wait_ge(w_lo, r * 8 + h * 4 + k // 2 + 1)
                        pe.matmul(psum[slot][:], xhi[:, k, at], whi[h][:, k], start=(k == 0), stop=False)
                        pe.matmul(psum[slot][:], xhi[:, k, at], wlo[h][:, k], start=False, stop=False)
                        ins = pe.matmul(psum[slot][:], xlo[:, k, at], whi[h][:, k], start=False, stop=(k == KC - 1))
                    ins.then_inc(y_ready, 1)

                def columns(r, part, first=False, last=False):
                    pe.wait_ge(cols_ready, (r - 1) * 8 + part + 1)
                    for i in range(CPQ):
                        a, z = first and i == 0, last and i == CPQ - 1
                        pe.matmul(PLACE_BANK[:, 0:2 * ET], oh_lo[:, i],
                                  oh_val[:, i].rearrange("p a t -> p (a t)"), start=a, stop=z, skip_group_check=True)
                        ins = pe.matmul(COUNT_BANK[0:KHI, 0:256], oh_khi[:, i], oh_klo[:, i],
                                        start=a, stop=z, skip_group_check=True)
                    ins.then_inc(cols_used, 1)

                def ranks(left, done):
                    pe.wait_ge(onehot_ready, 1)
                    for g, js in enumerate(groups):
                        pe.matmul(psum[4 + g][:, :len(js) * ECOLS], left[:],
                                  onehot[:, js[0]:js[-1] + 1, :].rearrange("p j c -> p (j c)"),
                                  start=True, stop=True).then_inc(done, 1)

                def turn(j):
                    pe.wait_ge(norm_ready, j + 1)
                    for n in (2 * j, 2 * j + 1):
                        if n >= 4:
                            pe.wait_ge(lo_done, n - 3)
                        for k in range(4):
                            kc = 4 * (n % 2) + k
                            ins = pe.transpose(psum[4 + n % 4][:, k * P:(k + 1) * P],
                                               x_tile(j)[:, kc * P:(kc + 1) * P], ident[:])
                        ins.then_inc(tr_done, 1)

                pe.wait_ge(consts, 5)
                turn(0)
                turn(1)

                def relation(r, sorts, start=False, first=False, last=False):
                    for h in range(2):
                        for j in range(NT):
                            product(r, h, j, start)
                            if start and h == 0 and j + 2 < NT:
                                turn(j + 2)
                            if start and (h, j) == RANK_AFTER[0]:
                                ranks(ones, totals_done)
                            if start and (h, j) == RANK_AFTER[1]:
                                pe.wait_ge(totals_read, 1)
                                ranks(tri, tri_done)
                            if sorts and j % 2 == 1 and j < 8:
                                part = 4 * h + j // 2
                                columns(r, part, first and part == 0, last and part == 7)
                relation(0, False, start=True)
                relation(1, True, first=True)
                with pe.Fori(2, SORT_R) as r:
                    relation(r, True)
                relation(SORT_R, True, last=True)
                with pe.Fori(1 + SORT_R, R) as r:
                    relation(r, False)


        z3 = Zone(OFF_W1, OFF_END - OFF_W1)
        after_acc = OFF_END + 4 * NT * D
        GR, HR, SR = 5, 3, 4
        gath = z3.put("gathered", [P, GR, D], F32)
        glo = nc.alloc_sbuf_tensor_at("glo", [P, GR, D], F32R, offset=z3.start)
        ghi = z3.put("ghi", [P, HR, D], F32R)
        sel = Zone(OFF_YOUT + 4 * KB, 4 * KB).put("sel", [P, SR, P], F32R)
        LAG_SPLIT, LAG_OUT = 3, 4
        w_in = [sem(f"w3_stage_loaded{i}") for i in range(2)]
        w_hi, w_lo, w_free = sem("w3_hi_written"), sem("w3_lo_written"), sem("w3_half_used")
        y_ready, y_evac = sem("y3_ready"), sem("y3_evacuated")
        y_out = [sem(f"y3_stored{i}") for i in range(2)]
        g_in = [sem(f"rows_gathered{i}") for i in range(GR)]
        sel_ready, g_hi, g_lo, g_used, acc_done = (
            sem("sel_ready"), sem("rows_hi"), sem("rows_lo"), sem("edge_tiles_used"), sem("pairs_accumulated"))

        def steps():
            half, t, later = NT * KC, 0, {}
            for c in range(4 * half):
                g, j, k = c // half, c % half // KC, c % KC
                yield "product", g, c % half
                if (c + 1) * ET // (4 * half) > t:
                    yield "edges", t
                    t += 1
                if j == NT - 1 and k % 2 == 1 and g < 3:
                    later.setdefault(c + LAG_SPLIT, []).append(("split", g + 1, k // 2))
                if k == KC - 1:
                    later.setdefault(c + LAG_OUT, []).append(("evacuate", g, j))
                yield from later.pop(c, [])
            for c in sorted(later):
                yield from later[c]

        with nc.Block() as block:
            @block.sync
            def _(sp):
                def load(g, q):
                    n = 4 * (g - 1) + q
                    if n >= 2:
                        sp.wait_ge(w_lo, n - 1)
                    w = root if g < 2 else w_gate[D:2 * D, :]
                    sp.dma_start(stage[:, q % 2], w_rows(w, q, g % 2)).then_inc(w_in[q % 2], 16)

                load(1, 0)
                load(1, 1)
                for g in range(4):
                    for j in range(NT):
                        if j == NT - 1 and g < 3:
                            load(g + 1, 2)
                            load(g + 1, 3)
                        sp.wait_ge(y_evac, g * NT + j + 1)
                        sp.dma_start(YX[g // 2, j * P:(j + 1) * P, (g % 2) * HALF:(g % 2 + 1) * HALF],
                                     yout[:, j % 2]).then_inc(y_out[j % 2], 16)
                    if g < 2:
                        load(g + 2, 0)
                        load(g + 2, 1)
                for i in range(2):
                    sp.wait_ge(y_out[i], 16 * 2 * NT)

            @block.gpsimd
            def _(pool):
                for t in range(ET + 1):
                    if t < ET:
                        if t >= GR:
                            pool.wait_ge(g_used, t - GR + 1)
                        nc.gpsimd.indirect_dma_start(
                            out=gath[:, t % GR], out_offset=None, in_=Y,
                            in_offset=bass.IndirectOffsetOnAxis(ap=edge_row[:, t:t + 1], axis=0)).then_inc(g_in[t % GR], 16)
                    if t:
                        if t - 1 >= SR:
                            pool.wait_ge(g_used, t - SR)
                        nc.gpsimd.tensor_scalar(sel[:, (t - 1) % SR], iota[:, 1:P + 1], edge_dst[:, t - 1:t], None,
                                                ALU.is_equal).then_inc(sel_ready, 1)

            @block.scalar
            def _(act):
                def split_hi(g, q):
                    act.wait_ge(w_in[q % 2], 16 * (2 * (g - 1) + q // 2 + 1))
                    if q < 3:
                        act.wait_ge(w_free, 3 * (g - 1) + q + 1)
                    else:
                        act.wait_ge(y_ready, g * NT)
                    nc.scalar.activation(whi[0][:, 2 * q:2 * q + 2, :], stage[:, q % 2], ACT.Copy).then_inc(w_hi, 1)

                def edges_hi(t):
                    act.wait_ge(g_in[t % GR], 16 * (t // GR + 1))
                    if t >= HR:
                        act.wait_ge(g_used, t - HR + 1)
                    nc.scalar.activation(ghi[:, t % HR], gath[:, t % GR], ACT.Copy,
                                         scale=edge_w[:, t:t + 1]).then_inc(g_hi, 1)

                def evacuate(g, j):
                    act.wait_ge(y_ready, g * NT + j + 1)
                    if g * NT + j >= 2:
                        act.wait_ge(y_out[j % 2], 16 * (g * (NT // 2) + j // 2))
                    nc.scalar.activation(yout[:, j % 2], psum[j % 2][:], ACT.Copy).then_inc(y_evac, 1)

                for what, *n in steps():
                    if what == "edges":
                        edges_hi(*n)
                    elif what == "split":
                        split_hi(*n)
                    elif what == "evacuate":
                        evacuate(*n)

            @block.vector
            def _(dve):
                v = nc.vector

                def split_lo(g, q):
                    dve.wait_ge(w_hi, 4 * (g - 1) + q + 1)
                    v.tensor_tensor(wlo[0][:, 2 * q:2 * q + 2, :], stage[:, q % 2],
                                    whi[0][:, 2 * q:2 * q + 2, :].bitcast(F32), ALU.subtract).then_inc(w_lo, 1)

                def edges_lo(t):
                    dve.wait_ge(g_hi, t + 1)
                    v.scalar_tensor_tensor(glo[:, t % GR], gath[:, t % GR], edge_w[:, t:t + 1],
                                           ghi[:, t % HR].bitcast(F32), ALU.mult, ALU.subtract).then_inc(g_lo, 1)

                def accumulate(n):
                    block_of = dve.value_load(tile_block[0:1, n * GROUP:n * GROUP + 1], min_val=0, max_val=NT - 1)
                    dve.wait_ge(g_used, GROUP * (n + 1))
                    if n:
                        dve.wait_ge(acc_done, n)
                    for c in range(2):
                        at = bass.ds(block_of * D + c * BANK, BANK)
                        ins = v.tensor_tensor(acc[:, at], acc[:, at], psum[2 + 2 * (n % 3) + c][:], ALU.add)
                    ins.then_inc(acc_done, 1)

                for what, *n in steps():
                    if what == "edges":
                        t = n[0]
                        edges_lo(t)
                        if t >= HR and (t - HR) % GROUP == GROUP - 1:
                            accumulate((t - HR) // GROUP)
                    elif what == "split":
                        split_lo(*n)
                for n in range((ET - HR) // GROUP, ET // GROUP):
                    accumulate(n)

            @block.tensor
            def _(pe):
                def product(g, j, k):
                    if k == 0 and g * NT + j >= 2:
                        pe.wait_ge(y_evac, g * NT + j - 1)
                    if g and j == 0 and k % 2 == 0:
                        pe.wait_ge(w_lo, 4 * (g - 1) + k // 2 + 1)
                    at = slice(j * P, (j + 1) * P)
                    pe.matmul(psum[j % 2][:], xhi[:, k, at], whi[0][:, k], start=(k == 0), stop=False)
                    pe.matmul(psum[j % 2][:], xhi[:, k, at], wlo[0][:, k], start=False, stop=False)
                    ins = pe.matmul(psum[j % 2][:], xlo[:, k, at], whi[0][:, k], start=False, stop=(k == KC - 1))
                    if k == KC - 1:
                        ins.then_inc(y_ready, 1)
                    elif j == NT - 1 and k % 2 == 1:
                        ins.then_inc(w_free, 1)

                def edges(t):
                    n = t // GROUP
                    if n >= 3 and t % GROUP == 0:
                        pe.wait_ge(acc_done, n - 2)
                    pe.wait_ge(sel_ready, t + 1)
                    pe.wait_ge(g_lo, t + 1)
                    start, stop = t % GROUP == 0, t % GROUP == GROUP - 1
                    for c in range(2):
                        bank = psum[2 + 2 * (n % 3) + c]
                        cols = slice(c * BANK, (c + 1) * BANK)
                        pe.matmul(bank[:], sel[:, t % SR], ghi[:, t % HR, cols], start=start, stop=False)
                        ins = pe.matmul(bank[:], sel[:, t % SR], glo[:, t % GR, cols], start=False, stop=stop)
                    ins.then_inc(g_used, 1)

                for what, *n in steps():
                    if what == "product":
                        product(n[0], n[1] // KC, n[1] % KC)
                    elif what == "edges":
                        edges(*n)

        wghi = nc.alloc_sbuf_tensor_at("wghi", [P, KC, D], F32R, offset=OFF_T)
        wglo = nc.alloc_sbuf_tensor_at("wglo", [P, KC, D], F32R, offset=OFF_T + 32 * KB)
        za, zb, zc = (Zone(OFF_T + 64 * KB, 16 * KB), Zone(OFF_YOUT, OFF_W1 - OFF_YOUT),
                      Zone(OFF_W1, OFF_END - OFF_W1))
        zd = Zone(after_acc, LIMIT - after_acc)
        uhi = za.put("uhi", [P, 2, D], F32R)
        ulo = za.put("ulo", [P, 2, D], F32R)
        u = zb.put("u", [P, 2, D], F32)
        xr = zb.put("xr", [P, 2, D], F32)
        zg = zb.put("zg", [P, 2, D], F32)
        th = zb.put("th", [P, 2, D], F32)
        xn = zb.put("xn", [P, 2, D], F32)
        x1 = zc.put("x1", [P, 2, D], F32)
        xn2 = zc.put("xn2", [P, 2, D], F32)
        xn2t = zc.put("xn2t", [P, KC, P], F32)
        bgate_b = zc.put("bgate_b", [P, D], F32)
        gw_rows = zc.put("gw_rows", [P, D], F32)
        gw_t = zd.put("gw_t", [P, KC, X], F32)
        st2 = zd.put("st2", [P, 2, 6], F32)
        ag2 = zd.put("ag2", [P, 2], F32)
        rs = zd.put("rs", [P, 4], F32)
        rs_i = zd.put("rs_i", [P, 2], I32)
        LOGITS = psum[6]
        wg_early = [nc.alloc_sbuf_tensor_at(f"wg_early{i}", [P, 2, HALF], F32, offset=zc.start + 4 * KB * i)
                    for i in range(4)]

        def wg_staged(n):
            if 2 <= n < 6:
                return wg_early[n - 2][:], xin[n], 32
            return stage[:, n % 2], w_in[n % 2], 16 * (1 + n // 6)

        w_in = [sem(f"wg_stage_loaded{i}") for i in range(2)]
        w_hi, w_lo = sem("wg_hi_written"), sem("wg_lo_written")
        rows_in, small_in = sem("small_rows_loaded"), sem("gate_w_loaded")
        x_in, r_in, g_in4 = ([sem(f"{n}_loaded{i}") for i in range(2)] for n in ("xr", "u", "zg"))
        bg_done, sum_done, diff_done = sem("bgate_added"), sem("x_plus_norm"), sem("tanh_less_norm")
        u_done, xn_done, tu_done, uhi_done, ulo_done, th_done = (
            sem("u_done"), sem("xn_done"), sem("u_transposed"), sem("uhi_done"), sem("ulo_done"), sem("tanh_done"))
        z_done, zg_done, x1_done, xn2_done = sem("z_done"), sem("z_read"), sem("x1_done"), sem("xn2_done")
        tx_done, tx_evac, lg_done = sem("xn2_transposed"), sem("xn2t_written"), sem("logits_done")
        x1_out, xn2_out = ([sem(f"{n}_stored{i}") for i in range(2)] for n in ("x1", "xn2"))
        gwt_done, gwt_evac = sem("gate_w_transposed"), sem("gate_w_t_written")

        with nc.Block() as block:
            @block.sync
            def _(sp):
                def fetch_u(j):
                    if j >= 2:
                        sp.wait_ge(th_done, j - 1)
                        sp.wait_ge(tu_done, 2 * (j - 1))
                    sp.dma_start(u[:, j % 2], YX[0, j * P:(j + 1) * P, :]).then_inc(r_in[j % 2], 16)

                def fetch_x(j):
                    if j >= 2:
                        sp.wait_ge(x1_done, j - 1)
                    sp.dma_start(xr[:rows(j), j % 2], x[j * P:j * P + rows(j), :]).then_inc(x_in[j % 2], 16)
                    sp.dma_start(zg[:, j % 2], YX[1, j * P:(j + 1) * P, :]).then_inc(g_in4[j % 2], 16)

                def load(n):
                    if n >= 6:
                        sp.wait_ge(w_lo, n - 5)
                    place, arrived, _ = wg_staged(n)
                    sp.dma_start(place, w_rows(w_gate, n % 4, n // 4)).then_inc(arrived, 16)

                fetch_u(0)
                for n in range(4):
                    load(n)
                sp.dma_start(gw_rows[0:X, :], gate_w).then_inc(small_in, 16)
                fetch_u(1)
                for n in (4, 5):
                    load(n)
                fetch_x(0)
                sp.dma_start(bgate_b[:], b_gate.partition_broadcast(P)).then_inc(rows_in, 16)
                for n in (6, 7):
                    load(n)
                fetch_x(1)
                for j in range(NT + 1):
                    if j + 2 < NT:
                        fetch_u(j + 2)
                    if j == 0:
                        continue
                    d = j - 1
                    sp.wait_ge(x1_done, d + 1)
                    sp.dma_start(X1[d * P:(d + 1) * P, :], x1[:, d % 2]).then_inc(x1_out[d % 2], 16)
                    if d + 2 < NT:
                        fetch_x(d + 2)
                    sp.wait_ge(xn2_done, d + 1)
                    sp.dma_start(XN2[d * P:(d + 1) * P, :], xn2[:, d % 2]).then_inc(xn2_out[d % 2], 16)
                for i in range(2):
                    sp.wait_ge(x1_out[i], 16 * NT // 2)
                    sp.wait_ge(xn2_out[i], 16 * NT // 2)

            @block.gpsimd
            def _(pool):
                pool.wait_ge(rows_in, 16)
                for j in range(NT):
                    i = j % 2
                    pool.wait_ge(xn_done, j + 1)
                    pool.wait_ge(th_done, j + 1)
                    nc.gpsimd.tensor_tensor(th[:, i], th[:, i], xn[:, i], ALU.subtract).then_inc(diff_done, 1)
                    pool.wait_ge(g_in4[i], 16 * (j // 2 + 1))
                    nc.gpsimd.tensor_tensor(zg[:, i], zg[:, i], bgate_b[:], ALU.add).then_inc(bg_done, 1)
                    nc.gpsimd.tensor_tensor(xr[:, i], xr[:, i], xn[:, i], ALU.add).then_inc(sum_done, 1)

            @block.scalar
            def _(act):
                def split_hi(n):
                    h, q = n // 4, n % 4
                    place, arrived, count = wg_staged(n)
                    act.wait_ge(arrived, count)
                    nc.scalar.activation(wghi[:, 2 * q:2 * q + 2, h * HALF:(h + 1) * HALF], place,
                                         ACT.Copy).then_inc(w_hi, 1)

                def u_part(j):
                    for g in range(2):
                        act.wait_ge(tu_done, 2 * j + g + 1)
                        if j >= 2:
                            act.wait_ge(z_done, 2 * (j - 1))
                        nc.scalar.activation(uhi[:, j % 2, g * BANK:(g + 1) * BANK], psum[g][:],
                                             ACT.Copy).then_inc(uhi_done, 1)
                    if j >= 2:
                        act.wait_ge(x1_done, j - 1)
                    act.wait_ge(u_done, j + 1)
                    nc.scalar.activation(th[:, j % 2], u[:, j % 2], ACT.Tanh).then_inc(th_done, 1)

                def xt_part(j):
                    for g in range(2):
                        act.wait_ge(tx_done, 2 * j + g + 1)
                        if j >= 1:
                            act.wait_ge(lg_done, j)
                        nc.scalar.activation(xn2t[:, 4 * g:4 * g + 4, :],
                                             psum[g][:].rearrange("p (k n) -> p k n", k=4),
                                             ACT.Copy).then_inc(tx_evac, 1)
                split_hi(0)
                split_hi(1)
                u_part(0)
                for n in range(2, 8):
                    split_hi(n)
                act.wait_ge(gwt_done, 1)
                nc.scalar.activation(gw_t[:], psum[7][:, 0:KC * X].rearrange("p (k e) -> p k e", e=X),
                                     ACT.Copy).then_inc(gwt_evac, 1)
                for j in range(NT):
                    if j + 1 < NT:
                        u_part(j + 1)
                    if j >= 2:
                        xt_part(j - 2)
                xt_part(NT - 2)
                xt_part(NT - 1)

            @block.vector
            def _(dve):
                v = nc.vector
                step = chain(dve)

                def split_lo(n):
                    h, q = n // 4, n % 4
                    dve.wait_ge(w_hi, n + 1)
                    at = (slice(None), slice(2 * q, 2 * q + 2), slice(h * HALF, (h + 1) * HALF))
                    v.tensor_tensor(wglo[at], wg_staged(n)[0], wghi[at].bitcast(F32), ALU.subtract).then_inc(w_lo, 1)

                def make_u(j):
                    dve.wait_ge(r_in[j % 2], 16 * (j // 2 + 1))
                    v.tensor_tensor(u[:, j % 2], u[:, j % 2], acc[:, j * D:(j + 1) * D], ALU.add).then_inc(u_done, 1)

                def u_low(j):
                    for g in range(2):
                        dve.wait_ge(uhi_done, 2 * j + g + 1)
                        at = (slice(None), j % 2, slice(g * BANK, (g + 1) * BANK))
                        v.tensor_tensor(ulo[at], psum[g][:], uhi[at].bitcast(F32), ALU.subtract).then_inc(ulo_done, 1)

                def x_norm(j):
                    i = j % 2
                    dve.wait_ge(x_in[i], 16 * (j // 2 + 1))
                    v.tensor_scalar(xn[:, i], xr[:, i], mean[:, j:j + 1], rstd[:, j:j + 1],
                                    ALU.subtract, ALU.mult).then_inc(xn_done, 1)

                def finish(j):
                    i = j % 2
                    dve.wait_ge(bg_done, j + 1)
                    for c in range(2):
                        dve.wait_ge(z_done, 2 * j + c + 1)
                        ins = v.tensor_tensor(zg[:, i, c * BANK:(c + 1) * BANK], psum[2 + 2 * i + c][:],
                                              zg[:, i, c * BANK:(c + 1) * BANK], ALU.add)
                    ins.then_inc(zg_done, 1)
                    dve.wait_ge(zg_done, j + 1)
                    dve.wait_ge(diff_done, j + 1)
                    step(v.tensor_tensor(th[:, i], th[:, i], zg[:, i], ALU.mult))
                    dve.wait_ge(sum_done, j + 1)
                    if j >= 2:
                        dve.wait_ge(x1_out[i], 16 * (j // 2))
                        dve.wait_ge(xn2_out[i], 16 * (j // 2))
                        dve.wait_ge(tx_done, 2 * (j - 1))
                    v.tensor_tensor(x1[:, i], xr[:, i], th[:, i], ALU.add).then_inc(x1_done, 1)
                    dve.wait_ge(x1_done, j + 1)
                    v.bn_stats(st2[:, 0, :], x1[:, i, 0:HALF])
                    step(v.bn_stats(st2[:, 1, :], x1[:, i, HALF:D]))
                    step(v.bn_aggr(ag2[:], st2[:].rearrange("p a b -> p (a b)")))
                    v.tensor_scalar(rs[:, 0:1], ag2[:, 1:2], EPS, -0.5, ALU.add, ALU.mult)
                    step(v.tensor_scalar(rs[:, 1:2], ag2[:, 1:2], EPS, None, ALU.add))
                    step(v.tensor_scalar(rs_i[:, 0:1], rs[:, 1:2].bitcast(I32), 1, None, ALU.arith_shift_right))
                    step(v.tensor_scalar(rs_i[:, 1:2], rs_i[:, 0:1], -1.0, float(0x5F3759DF), ALU.mult, ALU.add))
                    y = rs_i[:, 1:2].bitcast(F32)
                    for n in range(3):
                        step(v.scalar_tensor_tensor(rs[:, 2:3], y, rs[:, 0:1], y, ALU.mult, ALU.mult))
                        step(v.scalar_tensor_tensor(rs[:, 3:4], rs[:, 2:3], 1.5, y, ALU.add, ALU.mult))
                        y = rs[:, 3:4]
                    v.tensor_scalar(xn2[:, i], x1[:, i], ag2[:, 0:1], rs[:, 3:4],
                                    ALU.subtract, ALU.mult).then_inc(xn2_done, 1)
                    dve.wait_ge(xn2_done, j + 1)

                make_u(0)
                split_lo(0)
                split_lo(1)
                u_low(0)
                make_u(1)
                for n in range(2, 8):
                    split_lo(n)
                x_norm(0)
                for j in range(NT):
                    if j + 1 < NT:
                        u_low(j + 1)
                    if j >= 1:
                        finish(j - 1)
                    if j + 2 < NT:
                        make_u(j + 2)
                    if j + 1 < NT:
                        x_norm(j + 1)
                finish(NT - 1)

            @block.tensor
            def _(pe):
                def turn(j, src_t, ready, free, done):
                    pe.wait_ge(ready, j + 1)
                    for g in range(2):
                        for what, least in free(g):
                            pe.wait_ge(what, least)
                        for k in range(4):
                            c = 4 * g + k
                            ins = pe.transpose(psum[g][:, k * P:(k + 1) * P], src_t[:, j % 2, c * P:(c + 1) * P], ident[:])
                        ins.then_inc(done, 1)

                def turn_u(j):
                    turn(j, u, u_done, lambda g: ([(ulo_done, 2 * (j - 1) + g + 1)] if j >= 1 else [])
                         + ([(tx_evac, 2 * (j - 4) + g + 1)] if j >= 4 else []), tu_done)

                def turn_x(j, free):
                    turn(j, xn2, xn2_done, free, tx_done)

                def gate(j, c):
                    i = j % 2
                    pe.wait_ge(ulo_done, 2 * (j + 1))
                    if j >= 2:
                        pe.wait_ge(zg_done, j - 1)
                    for k in range(KC):
                        if j == 0 and k % 2 == 0:
                            pe.wait_ge(w_lo, 4 * c + k // 2 + 1)
                        at, cols = slice(k * P, (k + 1) * P), slice(c * BANK, (c + 1) * BANK)
                        bank = psum[2 + 2 * i + c]
                        pe.matmul(bank[:], uhi[:, i, at], wghi[:, k, cols], start=(k == 0), stop=False)
                        pe.matmul(bank[:], uhi[:, i, at], wglo[:, k, cols], start=False, stop=False)
                        ins = pe.matmul(bank[:], ulo[:, i, at], wghi[:, k, cols], start=False, stop=(k == KC - 1))
                    ins.then_inc(z_done, 1)

                def logits(j):
                    pe.wait_ge(tx_evac, 2 * (j + 1))
                    pe.wait_ge(gwt_evac, 1)
                    for k in range(KC):
                        ins = pe.matmul(LOGITS[:, j * X:(j + 1) * X], xn2t[:, k], gw_t[:, k],
                                        start=(k == 0), stop=(k == KC - 1))
                    ins.then_inc(lg_done, 1)

                turn_u(0)
                pe.wait_ge(small_in, 16)
                for k in range(KC):
                    ins = pe.transpose(psum[7][:, k * X:(k + 1) * X], gw_rows[0:X, k * P:(k + 1) * P], ident[0:X, 0:X])
                ins.then_inc(gwt_done, 1)
                for j in range(NT):
                    if j + 1 < NT:
                        turn_u(j + 1)
                    gate(j, 0)
                    if j >= 2:
                        turn_x(j - 2, lambda g: [(ulo_done, 2 * min(j + 1, NT - 1) + g + 1)])
                    gate(j, 1)
                    if j >= 2:
                        logits(j - 2)
                for j in (NT - 2, NT - 1):
                    turn_x(j, lambda g: [(tx_evac, 2 * (j - 1) + g + 1)])
                    logits(j)

        z5 = Zone(OFF_T, LIMIT - OFF_T)
        C2 = 2 * NT
        lg = z5.put("lg", [P, NT, X], F32)
        pr = z5.put("pr", [P, NT, X], F32)
        top = z5.put("top", [P, NT, 8], F32)
        top_i = z5.put("top_i", [P, NT, 8], U32)
        red = z5.put("red", [P, 3, NT], F32)
        sel_f = z5.put("sel_f", [P, NT, 2], F32)
        past = z5.put("past", [P, 2], F32)
        oh_e = z5.put("oh_e", [P, X, C2], BF16)
        bef = z5.put("bef", [P, X, C2], F32)
        wit = z5.put("wit", [P, X, C2], F32)
        ce = z5.put("ce", [P, 4, X], F32)
        ce_i = z5.put("ce_i", [P, 2, X], I32)
        ones_e = z5.put("ones_e", [P, C2], F32)
        pos = z5.put("pos", [P, C2], F32)
        pos_i = z5.put("pos_i", [P, 3, C2], I32)
        place_i = z5.put("place_i", [P, C2], I32)
        p_lo = z5.put("p_lo", [P, C2], F32)
        p_hi = z5.put("p_hi", [P, C2], F32)
        tok_f = z5.put("tok_f", [P, NT], F32)
        poh_lo = z5.put("poh_lo", [P, C2, P], F32R)
        poh_hi = z5.put("poh_hi", [P, C2, MTE], F32R)
        tok_s = z5.put("tok_s", [P, MTE], F32)
        tok_i = z5.put("tok_i", [P, MTE], I32)
        te = z5.put("te", [P, 2, MTE], F32)
        tile_expert = z5.put("tile_expert", [P, MTE], I32)
        tile_slot = z5.put("tile_slot", [P, MTE], I32)
        first_tile = z5.put("first_tile", [P, X], I32)
        rt_lg, rt_exp, rt_oh, rt_tot, rt_rank, rt_poh, rt_tok, rt_idx, rt_ready = (
            sem("shifted_logits_ready"), sem("exp_done"), sem("expert_onehot_ready"), sem("expert_totals_done"),
            sem("expert_ranks_done"), sem("token_onehots_ready"), sem("tokens_placed"), sem("token_index_ready"),
            sem("tile_expert_ready"))
        rt_iota = sem("token_numbers_ready")

        w13_at = z5.at
        w13hi = [z5.put(f"w13hi{i}", [P, KC, 2 * H], F32R) for i in range(2)]
        w13lo = [z5.put(f"w13lo{i}", [P, KC, 2 * H], F32R) for i in range(2)]
        w2hi = [z5.put(f"w2hi{i}", [P, HC, D], F32R) for i in range(2)]
        w2lo = [z5.put(f"w2lo{i}", [P, HC, D], F32R) for i in range(2)]
        raw_at = z5.at
        raw13 = z5.put("raw13", [P, 2, KC, 2 * H], F32)
        raw2 = z5.put("raw2", [P, 2, HC, D], F32)
        xg = z5.put("xg", [P, 2, D], F32)
        xthi = z5.put("xthi", [P, 2, D], F32R)
        xtlo = z5.put("xtlo", [P, 2, D], F32R)
        tanh_h = z5.put("tanh_h", [P, H], F32)
        act_a = z5.put("act_a", [P, H], F32)
        act_g = z5.put("act_g", [P, 2, H], F32)
        gthi = z5.put("gthi", [P, 2, H], F32R)
        gtlo = z5.put("gtlo", [P, 2, H], F32R)
        ye = z5.put("ye", [P, 2, D], F32)
        raw_in = [sem(f"expert_loaded{i}") for i in range(2)]
        experts_here, tiles_split = sem("experts_here"), sem("tiles_split")
        ab_hi = [sem(f"w13_hi_written{c}") for c in range(2)]
        ab_lo = [sem(f"w13_lo_written{c}") for c in range(2)]
        c_hi, c_lo = sem("w2_hi_written"), sem("w2_lo_written")
        xg_in = [sem(f"tokens_gathered{i}") for i in range(2)]
        xt_done, xt_hi, xt_lo = sem("xt_done"), sem("xt_hi"), sem("xt_lo")
        h_done, ht_done, a_done, g_done = sem("h_done"), sem("h_tanh_done"), sem("h_silu_done"), sem("g_done")
        gt_done, gt_hi, gt_lo = sem("gt_done"), sem("gt_hi"), sem("gt_lo")
        ye_done, ye_evac, ye_out = sem("ye_done"), sem("ye_evacuated"), [sem(f"ye_stored{i}") for i in range(2)]
        assert (MT - 3) % 2 == 0 and HC == 2 and 2 * H == BANK
        YT = 8
        assert KC * 2 * H * 2 // D == YT and NT - YT <= 2 * HC
        x1b = nc.alloc_sbuf_tensor_at("x1b", [P, NT, D], F32, offset=raw_at)
        chosen_y = nc.alloc_sbuf_tensor_at("chosen_y", [P, YT, 2, D], F32, offset=w13_at)
        x1_in, out_stored = [sem(f"x1_loaded{i}") for i in range(2)], sem("out_stored")
        y1_in, y2_in = ([sem(f"{n}{i}") for i in range(YT)] for n in ("first_gathered", "second_gathered"))
        half_done, res_done = sem("first_added"), sem("result_done")

        with nc.Block() as block:
            @block.sync
            def _(sp):
                sp.sem_inc(tiles_split, 1)
                for e in range(X):
                    i = e % 2
                    if e == 2:
                        sp.wait_ge(raw_in[0], 48)
                        sp.sem_inc(experts_here, 1)
                        sp.wait_ge(rt_ready, 1)
                    if e >= 2:
                        sp.wait_ge(raw_in[1 - i], 48 * ((e - 1) // 2 + 1))
                        sp.sem_inc(experts_here, 1)
                        used = sp.value_load(first_tile[0:1, e - 1:e], min_val=0, max_val=MT)
                        sp.wait_ge(tiles_split, used + 1)
                    for n, w in enumerate((w1, w3)):
                        sp.dma_start(raw13[:, i, :, n * H:(n + 1) * H],
                                     w[e].rearrange("(k p) n -> p k n", p=P)).then_inc(raw_in[i], 16)
                    sp.dma_start(raw2[:, i], w2[e].rearrange("(k p) n -> p k n", p=P)).then_inc(raw_in[i], 16)
                sp.wait_ge(raw_in[(X - 1) % 2], 48 * ((X - 1) // 2 + 1))
                sp.sem_inc(experts_here, 1)
                sp.wait_ge(ab_lo[0], MT)
                sp.wait_ge(ab_lo[1], MT)
                for g, js in enumerate((slice(0, YT), slice(YT, NT))):
                    if g == 1:
                        sp.wait_ge(tiles_split, MT + 1)
                    sp.dma_start(x1b[:, js], X1.rearrange("(j p) d -> p j d", p=P)[:, js]).then_inc(x1_in[g], 16)
                for j in range(NT):
                    sp.wait_ge(res_done, j + 1)
                    sp.dma_start(out[j * P:j * P + rows(j), :], x1b[:rows(j), j]).then_inc(out_stored, 16)
                sp.wait_ge(out_stored, 16 * NT)

            @block.gpsimd
            def _(pool):
                nc.gpsimd.iota(tok_f[:], pattern=[[P, NT]], base=1, channel_multiplier=1,
                               allow_small_or_imprecise_dtypes=True).then_inc(rt_iota, 1)
                pool.wait_ge(rt_idx, 1)

                def gather(i):
                    if i >= 2:
                        pool.wait_ge(xt_done, 2 * (i - 1))
                    nc.gpsimd.indirect_dma_start(
                        out=xg[:, i % 2], out_offset=None, in_=XN2,
                        in_offset=bass.IndirectOffsetOnAxis(ap=tok_i[:, i:i + 1], axis=0)).then_inc(xg_in[i % 2], 16)

                gather(0)
                gather(1)
                for i in range(MT):
                    slot = pool.value_load(tile_slot[0:1, i:i + 1], min_val=0, max_val=1)
                    pool.wait_ge(c_hi, i + 1)
                    nc.gpsimd.tensor_tensor(w2lo[i % 2][:], raw2[:, bass.ds(slot, 1)].rearrange("p a k n -> p (a k) n"),
                                            w2hi[i % 2][:].bitcast(F32), ALU.subtract).then_inc(c_lo, 1)
                    if i + 2 < MT:
                        gather(i + 2)
                    pool.wait_ge(c_lo, i + 1)
                    for c in range(2):
                        pool.wait_ge(ab_lo[c], i + 1)
                    pool.sem_inc(tiles_split, 1)
                pool.wait_ge(ye_out[0], 16 * ((MT + 1) // 2))
                pool.wait_ge(ye_out[1], 16 * (MT // 2))
                for j in range(NT):
                    if j >= YT:
                        pool.wait_ge(res_done, j - YT + 1)
                    for k, got in enumerate((y1_in, y2_in)):
                        nc.gpsimd.indirect_dma_start(
                            out=chosen_y[:, j % YT, k], out_offset=None, in_=YS,
                            in_offset=bass.IndirectOffsetOnAxis(ap=place_i[:, 2 * j + k:2 * j + k + 1], axis=0)
                        ).then_inc(got[j % YT], 16)

            @block.scalar
            def _(act):
                a = nc.scalar
                act.wait_ge(rt_lg, 1)
                a.activation(pr[:], lg[:], ACT.Exp).then_inc(rt_exp, 1)

                def slot_of(i):
                    return act.value_load(tile_slot[0:1, bass.ds(i, 1)], min_val=0, max_val=1)

                def expert_of(i):
                    return act.value_load(tile_expert[0:1, bass.ds(i, 1)], min_val=0, max_val=X - 1)

                def hi_ab(i, s, c, slot, expert, first=False):
                    if c == 0:
                        act.wait_ge(experts_here, expert + 1)
                        if not first:
                            act.wait_ge(h_done, i - 1)
                    a.activation(w13hi[s][:, 4 * c:4 * c + 4, :],
                                 raw13[:, bass.ds(slot, 1), 4 * c:4 * c + 4, :].rearrange("p a k n -> p (a k) n"),
                                 ACT.Copy).then_inc(ab_hi[c], 1)

                def hi_c(i, s, slot, first=False):
                    if not first:
                        act.wait_ge(ye_done, 2 * (i - 1))
                    a.activation(w2hi[s][:], raw2[:, bass.ds(slot, 1)].rearrange("p a k n -> p (a k) n"),
                                 ACT.Copy).then_inc(c_hi, 1)

                def hi_x(i, s, first=False):
                    for g in range(2):
                        act.wait_ge(xt_done, 2 * i + g + 1)
                        if not first:
                            act.wait_ge(h_done, i - 1)
                        a.activation(xthi[:, s, g * BANK:(g + 1) * BANK], psum[2 + g][:], ACT.Copy).then_inc(xt_hi, 1)

                def tanh(i, s, first=False):
                    act.wait_ge(h_done, i + 1)
                    if not first:
                        act.wait_ge(a_done, i)
                    a.activation(tanh_h[:], psum[s][:, 0:H], ACT.Tanh, scale=0.5).then_inc(ht_done, 1)

                def hi_g(i, s, first=False):
                    act.wait_ge(gt_done, i + 1)
                    if not first:
                        act.wait_ge(ye_done, 2 * (i - 1))
                    a.activation(gthi[:, s], psum[4][:, 0:H], ACT.Copy).then_inc(gt_hi, 1)

                def evacuate(i, s, first=False):
                    for c in range(2):
                        act.wait_ge(ye_done, 2 * i + c + 1)
                        if not first:
                            act.wait_ge(ye_out[s], 16 * ((i - s) // 2 if isinstance(i, int) else i_half[s]))
                        a.activation(ye[:, s, c * BANK:(c + 1) * BANK], psum[5 + c][:], ACT.Copy).then_inc(ye_evac, 1)

                def store(i, s):
                    act.wait_ge(ye_evac, 2 * (i + 1))
                    act.dma_start(YS[bass.ds(i * P, P), :], ye[:, s]).then_inc(ye_out[s], 16)

                i_half = [0, 0]
                act.wait_ge(rt_ready, 1)
                slot, expert = slot_of(0), expert_of(0)
                for c in range(2):
                    hi_ab(0, 0, c, slot, expert, True)
                hi_c(0, 0, slot, True)
                slot, expert = slot_of(1), expert_of(1)
                for c in range(2):
                    hi_ab(1, 1, c, slot, expert, True)
                hi_x(0, 0, True)
                tanh(0, 0, True)
                hi_x(1, 1, True)

                def step5(i, s, two=True, one=True, n=None):
                    if one:
                        slot_c = slot_of(i + 1)
                    if two:
                        slot, expert = slot_of(i + 2), expert_of(i + 2)
                    if n != 0:
                        evacuate(i - 1, 1 - s, n in (1, 2))
                    if one:
                        hi_c(i + 1, 1 - s, slot_c, n == 0)
                    hi_g(i, s, n in (0, 1))
                    if two:
                        hi_ab(i + 2, s, 0, slot, expert)
                        hi_ab(i + 2, s, 1, slot, expert)
                    if one:
                        tanh(i + 1, 1 - s)
                    if two:
                        hi_x(i + 2, s)
                    if n != 0:
                        store(i - 1, 1 - s)
                for n in range(3):
                    step5(n, n % 2, n=n)
                with act.Fori(1, (MT - 3) // 2) as n:
                    i_half[1], i_half[0] = n, n
                    step5(2 * n + 1, 1)
                    step5(2 * n + 2, 0)
                step5(MT - 2, 1, two=False)
                step5(MT - 1, 0, two=False, one=False)
                evacuate(MT - 1, 0)
                store(MT - 1, 0)

            @block.vector
            def _(dve):
                v = nc.vector
                step = chain(dve)

                def flat(t):
                    return t.rearrange("p a b -> p (a b)")
                step(v.tensor_reduce(red[:, 0, :], LOGITS[:, 0:NT * X].rearrange("p (j e) -> p j e", e=X), AX.X, ALU.max))
                v.tensor_tensor(lg[:], LOGITS[:, 0:NT * X].rearrange("p (j e) -> p j e", e=X),
                                red[:, 0, :].unsqueeze(2).to_broadcast([P, NT, X]), ALU.subtract).then_inc(rt_lg, 1)
                dve.wait_ge(rt_exp, 1)
                step(v.tensor_reduce(red[:, 1, :], pr[:], AX.X, ALU.add))
                step(v.reciprocal(red[:, 2, :], red[:, 1, :]))
                step(v.tensor_tensor(pr[:], pr[:], red[:, 2, :].unsqueeze(2).to_broadcast([P, NT, X]), ALU.mult))
                for j in range(NT):
                    ins = v.max(top[:, j, :], pr[:, j, :])
                step(ins)
                for j in range(NT):
                    ins = v.max_index(top_i[:, j, :], top[:, j, :], pr[:, j, :])
                step(ins)
                step(v.tensor_copy(sel_f[:], top_i[:, :, 0:2]))
                step(v.tensor_scalar(past[:, 0:1], lanes[:], float(LASTP), float(X), ALU.is_ge, ALU.mult))
                step(v.tensor_scalar(sel_f[:, NT - 1, :], sel_f[:, NT - 1, :], past[:, 0:1], None, ALU.add))
                for e in range(X):
                    ins = v.tensor_scalar(oh_e[:, e, :], flat(sel_f[:]), float(e), None, ALU.is_equal)
                ins.then_inc(rt_oh, 1)
                step(v.memset(ones_e[:], 1.0))
                dve.wait_ge(rt_tot, 1)
                TOT = psum[4][:, 0:X * C2].rearrange("p (e c) -> p e c", e=X)
                for e in range(X):
                    ins = v.tensor_tensor_scan(bef[:, e, :], ones_e[:], TOT[:, e, :], 0.0, ALU.mult, ALU.add)
                step(ins)
                step(v.tensor_copy(ce[:, 0, :], bef[:, :, C2 - 1]))
                step(v.tensor_tensor(bef[:], bef[:], TOT, ALU.subtract))
                step(v.tensor_scalar(ce_i[:, 0, :], ce[:, 0, :], float(P - 1), None, ALU.add))
                step(v.tensor_scalar(ce_i[:, 1, :], ce_i[:, 0, :], 7, 7, ALU.arith_shift_right, ALU.logical_shift_left))
                step(v.tensor_copy(ce[:, 1, :], ce_i[:, 1, :]))
                step(v.tensor_tensor_scan(ce[:, 2, :], ones_e[:, 0:X], ce[:, 1, :], 0.0, ALU.mult, ALU.add))
                step(v.tensor_tensor(ce[:, 3, :], ce[:, 2, :], ce[:, 1, :], ALU.subtract))
                step(v.tensor_scalar(te[:, 0, :], iota[:, 0:MTE], float(P), None, ALU.mult))
                step(v.memset(te[:, 1, :], 0.0))
                for e in range(1, X):
                    step(v.scalar_tensor_tensor(te[:, 1, :], te[:, 0, :], ce[:, 3, e:e + 1], te[:, 1, :],
                                                ALU.is_ge, ALU.add))
                step(v.tensor_copy(tile_expert[:], te[:, 1, :]))
                step(v.tensor_scalar(tile_slot[:], tile_expert[:], 1, None, ALU.bitwise_and))
                v.tensor_scalar(first_tile[:], ce[:, 3, :], 1.0 / P, None, ALU.mult).then_inc(rt_ready, 1)
                dve.wait_ge(rt_rank, 1)
                step(v.tensor_tensor(wit[:], bef[:], psum[5][:, 0:X * C2].rearrange("p (e c) -> p e c", e=X), ALU.add))
                step(v.tensor_tensor(wit[:], wit[:], ce[:, 3, :].unsqueeze(2).to_broadcast([P, X, C2]), ALU.add))
                step(v.tensor_tensor(wit[:], wit[:], oh_e[:], ALU.mult))
                step(v.tensor_reduce(pos[:], wit[:].rearrange("p e c -> p c e"), AX.X, ALU.add))
                step(v.tensor_copy(place_i[:], pos[:]))
                step(v.tensor_scalar(past[:, 1:2], past[:, 0:1], float(P * 256 // X), None, ALU.mult))
                step(v.tensor_scalar(pos[:, C2 - 2:C2], pos[:, C2 - 2:C2], past[:, 1:2], None, ALU.add))
                step(v.tensor_copy(pos_i[:, 0, :], pos[:]))
                step(v.tensor_scalar(pos_i[:, 1, :], pos_i[:, 0, :], P - 1, None, ALU.bitwise_and))
                step(v.tensor_scalar(pos_i[:, 2, :], pos_i[:, 0, :], 7, None, ALU.arith_shift_right))
                step(v.tensor_copy(p_lo[:], pos_i[:, 1, :]))
                step(v.tensor_copy(p_hi[:], pos_i[:, 2, :]))
                dve.wait_ge(rt_iota, 1)
                for c in range(C2):
                    v.tensor_scalar(poh_lo[:, c], iota[:, 0:P], p_lo[:, c:c + 1], None, ALU.is_equal)
                    ins = v.tensor_scalar(poh_hi[:, c], iota[:, 0:MTE], p_hi[:, c:c + 1], tok_f[:, c // 2:c // 2 + 1],
                                          ALU.is_equal, ALU.mult)
                    ins.then_inc(rt_poh, 1)
                dve.wait_ge(rt_tok, 1)
                step(v.tensor_scalar(tok_s[:], psum[7][:, 0:MTE], -1.0, 0.0, ALU.add, ALU.max))
                v.tensor_copy(tok_i[:], tok_s[:]).then_inc(rt_idx, 1)

                def slot_of(i):
                    return dve.value_load(tile_slot[0:1, bass.ds(i, 1)], min_val=0, max_val=1)

                def lo_ab(i, s, c, slot):
                    dve.wait_ge(ab_hi[c], i + 1)
                    v.tensor_tensor(w13lo[s][:, 4 * c:4 * c + 4, :],
                                    raw13[:, bass.ds(slot, 1), 4 * c:4 * c + 4, :].rearrange("p a k n -> p (a k) n"),
                                    w13hi[s][:, 4 * c:4 * c + 4, :].bitcast(F32), ALU.subtract).then_inc(ab_lo[c], 1)

                def lo_x(i, s):
                    for g in range(2):
                        dve.wait_ge(xt_hi, 2 * i + g + 1)
                        at = (slice(None), s, slice(g * BANK, (g + 1) * BANK))
                        v.tensor_tensor(xtlo[at], psum[2 + g][:], xthi[at].bitcast(F32), ALU.subtract).then_inc(xt_lo, 1)

                def silu(i, s, first=False):
                    dve.wait_ge(ht_done, i + 1)
                    v.scalar_tensor_tensor(act_a[:], tanh_h[:], 1.0, psum[s][:, 0:H], ALU.add, ALU.mult).then_inc(a_done, 1)
                    dve.wait_ge(a_done, i + 1)
                    if not first:
                        dve.wait_ge(gt_done, i - 1)
                    v.scalar_tensor_tensor(act_g[:, s], act_a[:], 0.5, psum[s][:, H:2 * H],
                                           ALU.mult, ALU.mult).then_inc(g_done, 1)

                def lo_g(i, s):
                    dve.wait_ge(gt_hi, i + 1)
                    v.tensor_tensor(gtlo[:, s], psum[4][:, 0:H], gthi[:, s].bitcast(F32), ALU.subtract).then_inc(gt_lo, 1)

                dve.wait_ge(rt_ready, 1)
                slot = slot_of(0)
                for c in range(2):
                    lo_ab(0, 0, c, slot)
                lo_x(0, 0)
                slot = slot_of(1)
                for c in range(2):
                    lo_ab(1, 1, c, slot)
                silu(0, 0, True)
                lo_x(1, 1)

                def step5(i, s, two=True, one=True, first=False):
                    if two:
                        slot = slot_of(i + 2)
                    lo_g(i, s)
                    if two:
                        lo_ab(i + 2, s, 0, slot)
                    if one:
                        silu(i + 1, 1 - s, first)
                    if two:
                        lo_x(i + 2, s)
                        lo_ab(i + 2, s, 1, slot)
                step5(0, 0, first=True)
                with dve.Fori(0, (MT - 3) // 2) as n:
                    step5(2 * n + 1, 1)
                    step5(2 * n + 2, 0)
                step5(MT - 2, 1, two=False)
                step5(MT - 1, 0, two=False, one=False)
                for j in range(NT):
                    dve.wait_ge(y1_in[j % YT], 16 * (j // YT + 1))
                    dve.wait_ge(x1_in[j // YT], 16)
                    v.scalar_tensor_tensor(x1b[:, j], chosen_y[:, j % YT, 0], top[:, j, 0:1], x1b[:, j],
                                           ALU.mult, ALU.add).then_inc(half_done, 1)
                    dve.wait_ge(half_done, j + 1)
                    dve.wait_ge(y2_in[j % YT], 16 * (j // YT + 1))
                    v.scalar_tensor_tensor(x1b[:, j], chosen_y[:, j % YT, 1], top[:, j, 1:2], x1b[:, j],
                                           ALU.mult, ALU.add).then_inc(res_done, 1)

            @block.tensor
            def _(pe):
                pe.wait_ge(rt_oh, 1)
                pe.matmul(psum[4][:, 0:X * C2], ones[:], oh_e[:].rearrange("p e c -> p (e c)"),
                          start=True, stop=True).then_inc(rt_tot, 1)
                pe.matmul(psum[5][:, 0:X * C2], tri[:], oh_e[:].rearrange("p e c -> p (e c)"),
                          start=True, stop=True).then_inc(rt_rank, 1)
                for c in range(C2):
                    pe.wait_ge(rt_poh, c + 1)
                    ins = pe.matmul(psum[7][:, 0:MTE], poh_lo[:, c], poh_hi[:, c], start=(c == 0), stop=(c == C2 - 1))
                ins.then_inc(rt_tok, 1)

                def turn_x(i, s, first=False):
                    pe.wait_ge(xg_in[s], 16 * (i // 2 + 1 if isinstance(i, int) else half_of[s] + 1))
                    for g in range(2):
                        if not first:
                            pe.wait_ge(xt_lo, 2 * (i - 1) + g + 1)
                        for k in range(4):
                            c = 4 * g + k
                            ins = pe.transpose(psum[2 + g][:, k * P:(k + 1) * P], xg[:, s, c * P:(c + 1) * P], ident[:])
                        ins.then_inc(xt_done, 1)

                def hidden(i, s, c, first=False):
                    pe.wait_ge(ab_lo[c], i + 1)
                    pe.wait_ge(xt_lo, 2 * (i + 1))
                    if not first:
                        pe.wait_ge(g_done, i - 1)
                    for k in range(4 * c, 4 * c + 4):
                        at = slice(k * P, (k + 1) * P)
                        pe.matmul(psum[s][:], xthi[:, s, at], w13hi[s][:, k], start=(k == 0), stop=False)
                        pe.matmul(psum[s][:], xthi[:, s, at], w13lo[s][:, k], start=False, stop=False)
                        ins = pe.matmul(psum[s][:], xtlo[:, s, at], w13hi[s][:, k], start=False, stop=(k == KC - 1))
                    if c == 1:
                        ins.then_inc(h_done, 1)

                def turn_g(i, s, first=False):
                    pe.wait_ge(g_done, i + 1)
                    if not first:
                        pe.wait_ge(gt_lo, i)
                    for k in range(HC):
                        ins = pe.transpose(psum[4][:, k * P:(k + 1) * P], act_g[:, s, k * P:(k + 1) * P], ident[:])
                    ins.then_inc(gt_done, 1)

                def outputs(i, s, first=False):
                    pe.wait_ge(c_lo, i + 1)
                    pe.wait_ge(gt_lo, i + 1)
                    for c in range(2):
                        if not first:
                            pe.wait_ge(ye_evac, 2 * (i - 1) + c + 1)
                        for k in range(HC):
                            at, cols = slice(k * P, (k + 1) * P), slice(c * BANK, (c + 1) * BANK)
                            pe.matmul(psum[5 + c][:], gthi[:, s, at], w2hi[s][:, k, cols], start=(k == 0), stop=False)
                            pe.matmul(psum[5 + c][:], gthi[:, s, at], w2lo[s][:, k, cols], start=False, stop=False)
                            ins = pe.matmul(psum[5 + c][:], gtlo[:, s, at], w2hi[s][:, k, cols], start=False,
                                            stop=(k == HC - 1))
                        ins.then_inc(ye_done, 1)

                half_of = [0, 0]
                turn_x(0, 0, True)
                hidden(0, 0, 0, True)
                hidden(0, 0, 1, True)
                turn_x(1, 1)

                def step5(i, s, two=True, one=True, first=False):
                    if one:
                        hidden(i + 1, 1 - s, 0, first)
                    turn_g(i, s, first)
                    if one:
                        hidden(i + 1, 1 - s, 1, first)
                    if two:
                        turn_x(i + 2, s)
                    outputs(i, s, first)
                step5(0, 0, first=True)
                with pe.Fori(0, (MT - 3) // 2) as n:
                    half_of[1], half_of[0] = n + 1, n + 2
                    step5(2 * n + 1, 1)
                    step5(2 * n + 2, 0)
                step5(MT - 2, 1, two=False)
                step5(MT - 1, 0, two=False, one=False)


_INS = ["x", "src", "dst", "edge_type_8", "L0_gnn_weight", "L0_gnn_root", "L0_gnn_bias", "L0_gnn_w_gate",
        "L0_gnn_b_gate", "L0_ffn_gate_w", "L0_ffn_w1", "L0_ffn_w2", "L0_ffn_w3"]


def kernel(**inputs):
    import numpy as _np
    import concourse.bacc as _bacc
    from concourse import mybir as _mybir
    from concourse.bass_utils import run_bass_kernel_spmd as _run

    nc = _bacc.Bacc("TRN2", target_bir_lowering=False, num_devices=1)
    arrays, args = {}, []
    for name in _INS:
        a = _np.ascontiguousarray(inputs[name])
        arrays[f"in_{name}"] = a
        args.append(nc.dram_tensor(f"in_{name}", a.shape, _mybir.dt.from_np(a.dtype), kind="ExternalInput").ap())
    result = nc.dram_tensor("result", inputs["x"].shape, _mybir.dt.float32, kind="ExternalOutput").ap()
    build_program(nc, *args, result)
    r = _run(nc, [arrays], core_ids=[0])
    return r.results[0]["result"]
```
